# Optimizing a Trainium2 kernel written in Bass

```python
import numpy as np
import jax
import jax.numpy as jnp

def _softmax(x, axis=-1):
    return jax.nn.softmax(x, axis=axis)

def _gelu(x):
    return jax.nn.gelu(x, approximate=True)

def _silu(x):
    return jax.nn.silu(x)

def _sigmoid(x):
    return jax.nn.sigmoid(x)

def _layernorm(x, axis=-1, eps=1e-05):
    m = jnp.mean(x, axis=axis, keepdims=True)
    v = jnp.var(x, axis=axis, keepdims=True)
    return (x - m) / jnp.sqrt(v + eps)

def _scatter_add(tgt, idx, src, axis=0):
    return tgt.at[idx].add(src)

def _segment_sum(src, seg, n):
    return jax.ops.segment_sum(src, seg, n)
kernel_name = 'mk_flamingo_gated_d2_seqx_r8_e21884'

def setup_inputs(seed: int=0):
    np.random.seed(seed)
    _w = jnp.asarray

    def _rec_inputs():
        import jax
        import jax.numpy as jnp
        _rk = jax.random.key(seed)
        x = -0.0002928 + 1 * jax.random.normal(jax.random.fold_in(_rk, 1), (4, 256, 256), jnp.float32)
        _lenS = 256 - jax.random.randint(jax.random.fold_in(_rk, 7), (4,), 0, max(1, 256 // 4) + 1, jnp.int32)
        _lenS2 = 256 - jax.random.randint(jax.random.fold_in(_rk, 8), (4,), 0, max(1, 256 // 4) + 1, jnp.int32)
        _ctx_2048P = jax.random.normal(jax.random.fold_in(_rk, 11), (4, 16, 256), jnp.float32)
        _ctx_2048c = jax.random.dirichlet(jax.random.fold_in(_rk, 511), 0.3 * jnp.ones((16,), jnp.float32), (4, 256))
        _ctx_2048t = jnp.einsum('bsk,bkd->bsd', _ctx_2048c, _ctx_2048P)
        _ctx_2048t = _ctx_2048t * jax.lax.rsqrt(jnp.mean(jnp.square(_ctx_2048t)) + 1e-12) * 0.953939
        ctx_2048 = -1.39393e-06 + 0.999914 * (_ctx_2048t + 0.3 * jax.random.normal(jax.random.fold_in(_rk, 611), (4, 256, 256), jnp.float32))
        pos_BxS2 = jnp.broadcast_to(jnp.arange(256, dtype=jnp.int32), (4, 256))
        itok_BxS_4096_4607 = jax.random.randint(jax.random.fold_in(_rk, 13), (4, 256), 512, 576, jnp.int32)
        _g = jax.random.normal(jax.random.fold_in(_rk, 9001), (2, 2), jnp.float32)
        _g = jnp.sign(_g) * jnp.maximum(jnp.abs(_g), 1.0) + (_g == 0) * 1.0
        g_xattn = _g[0]
        g_ffn = _g[1]
        return (x, ctx_2048, pos_BxS2, itok_BxS_4096_4607, g_xattn, g_ffn)
    x, ctx_2048, pos_BxS2, itok_BxS_4096_4607, g_xattn, g_ffn = _rec_inputs()

    def _L0_xattn_setup():
        import jax, jax.numpy as jnp
        import numpy as np
        B, S, E, NH = (2, 128, 256, 16)
        DH = E // NH
        EPS = 1e-06

        def _mlstm_forward(q, k, v, Wi, bi, Wf, bf, ln_scale):
            b, s, e = q.shape
            nh = Wi.shape[1]
            dh = e // nh
            x = jnp.concatenate([q, k, v], axis=-1)
            ig = (x @ Wi + bi).transpose(0, 2, 1)[..., None]
            fg = (x @ Wf + bf).transpose(0, 2, 1)[..., None]
            split = lambda t: t.reshape(b, s, nh, dh).transpose(0, 2, 1, 3)
            qh, kh, vh = (split(q), split(k), split(v))
            log_f = jax.nn.log_sigmoid(fg)
            log_f_cum = jnp.concatenate([jnp.zeros((b, nh, 1, 1), q.dtype), jnp.cumsum(log_f, axis=2)], axis=2)
            fg_mat = log_f_cum - jnp.transpose(log_f_cum, (0, 1, 3, 2))
            ltr = jnp.tril(jnp.ones((s, s), dtype=bool))
            log_fg = jnp.where(ltr, fg_mat[:, :, 1:, 1:], -jnp.inf)
            log_D = log_fg + jnp.transpose(ig, (0, 1, 3, 2))
            max_log_D = jnp.max(log_D, axis=-1, keepdims=True)
            D = jnp.exp(log_D - max_log_D)
            qk = jnp.einsum('bhsd,bhtd->bhst', qh, kh) / jnp.sqrt(jnp.asarray(dh, q.dtype))
            C = qk * D
            normalizer = jnp.maximum(jnp.abs(C.sum(-1, keepdims=True)), jnp.exp(-max_log_D))
            Cn = C / (normalizer + EPS)
            h = jnp.einsum('bhst,bhtd->bhsd', Cn, vh)
            mu = h.mean(-1, keepdims=True)
            var = ((h - mu) ** 2).mean(-1, keepdims=True)
            hn = (h - mu) * jax.lax.rsqrt(var + EPS)
            hn = hn * ln_scale.reshape(1, nh, 1, dh)
            return hn.transpose(0, 2, 1, 3).reshape(b, s, e)
        key = jax.random.key(seed)
        ks = jax.random.split(key, 6)
        q = jax.random.normal(ks[0], (B, S, E), dtype=jnp.float32)
        k = jax.random.normal(ks[1], (B, S, E), dtype=jnp.float32)
        v = jax.random.normal(ks[2], (B, S, E), dtype=jnp.float32)
        Wi = jax.random.normal(ks[3], (3 * E, NH), dtype=jnp.float32) * 0.02
        bi = jax.random.normal(ks[4], (NH,), dtype=jnp.float32) * 0.1
        Wf = jax.random.normal(ks[5], (3 * E, NH), dtype=jnp.float32) * 0.02
        bf = jnp.linspace(3.0, 6.0, NH, dtype=jnp.float32)
        ln_scale = jnp.ones((E,), dtype=jnp.float32)
        return {'q': q, 'k': k, 'v': v, 'Wi': Wi, 'bi': bi, 'Wf': Wf, 'bf': bf, 'ln_scale': ln_scale}
    _L0_xattn_all = _L0_xattn_setup()
    _L0_xattn_in = {k: v for k, v in _L0_xattn_all.items() if k in ('Wi', 'bi', 'Wf', 'bf', 'ln_scale')}
    del _L0_xattn_all

    def _L0_ffn_setup():
        import jax, jax.numpy as jnp
        import numpy as np
        D_MODEL = 256
        D_FF = 1024
        BATCH = 4
        SEQ = 256
        MAX_EXP = 4
        NUM_BITS = 8
        C_CHUNKS = 2
        SCALE = 0.1

        def _pow2_ternary(key, out_dim, in_dim, max_exp):
            k1, k2 = jax.random.split(key)
            t = jax.random.randint(k1, (out_dim, in_dim), -1, 2).astype(jnp.float32)
            e = jax.random.randint(k2, (out_dim, in_dim), 0, max_exp + 1).astype(jnp.float32)
            return t * jnp.exp2(-e)

        def _lookup_act(h):
            total_bits = NUM_BITS * C_CHUNKS
            qmax = 2 ** (total_bits - 1) - 1
            qmin = -2 ** (total_bits - 1)
            q = jnp.clip(jnp.round(h / SCALE), qmin, qmax)
            return jax.nn.gelu(q * SCALE)
        key = jax.random.key(seed)
        kx, k1, k2 = jax.random.split(key, 3)
        x = jax.random.normal(kx, (BATCH, SEQ, D_MODEL), dtype=jnp.float32)
        W1 = _pow2_ternary(k1, D_FF, D_MODEL, MAX_EXP)
        W2 = _pow2_ternary(k2, D_MODEL, D_FF, MAX_EXP)
        return {'x': x, 'W1': W1, 'W2': W2}
    _L0_ffn_all = _L0_ffn_setup()
    _L0_ffn_in = {k: v for k, v in _L0_ffn_all.items() if k in ('W1', 'W2')}
    del _L0_ffn_all

    def _L1_xattn_setup():
        import jax, jax.numpy as jnp
        import numpy as np
        B, CTX, DRAFT, D = (2, 512, 64, 256)
        H, KVH, HD = (16, 4, 128)
        N_REP = H // KVH
        EPS = 1e-06
        THETA = 10000.0
        SCALE = 1.0 / np.sqrt(HD).astype(np.float32)

        def _rms_norm(x, w):
            v = jnp.mean(jnp.square(x.astype(jnp.float32)), axis=-1, keepdims=True)
            return (w * (x.astype(jnp.float32) * jax.lax.rsqrt(v + EPS))).astype(x.dtype)

        def _rotate_half(x):
            x1, x2 = jnp.split(x, 2, axis=-1)
            return jnp.concatenate((-x2, x1), axis=-1)

        def _rope(x, pos):
            inv_freq = 1.0 / THETA ** (jnp.arange(0, HD, 2, dtype=jnp.float32) / HD)
            freqs = pos.astype(jnp.float32)[:, None, :, None] * inv_freq
            emb = jnp.concatenate((freqs, freqs), axis=-1)
            return x * jnp.cos(emb) + _rotate_half(x) * jnp.sin(emb)
        key = jax.random.key(seed)
        ks = jax.random.split(key, 6)
        return {'draft_hidden': jax.random.normal(ks[0], (B, DRAFT, D), jnp.float32), 'context_hidden': jax.random.normal(ks[1], (B, CTX, D), jnp.float32), 'Wq': jax.random.normal(ks[2], (H * HD, D), jnp.float32) * 0.02, 'Wk': jax.random.normal(ks[3], (KVH * HD, D), jnp.float32) * 0.02, 'Wv': jax.random.normal(ks[4], (KVH * HD, D), jnp.float32) * 0.02, 'Wo': jax.random.normal(ks[5], (D, H * HD), jnp.float32) * 0.02, 'q_norm_w': jnp.ones((HD,), jnp.float32), 'k_norm_w': jnp.ones((HD,), jnp.float32), 'context_position_ids': jnp.broadcast_to(jnp.arange(CTX, dtype=jnp.int32), (B, CTX)), 'draft_position_ids': jnp.broadcast_to(CTX + jnp.arange(DRAFT, dtype=jnp.int32), (B, DRAFT))}
    _L1_xattn_all = _L1_xattn_setup()
    _L1_xattn_in = {k: v for k, v in _L1_xattn_all.items() if k in ('Wq', 'Wk', 'Wv', 'Wo', 'q_norm_w', 'k_norm_w')}
    del _L1_xattn_all

    def _L1_ffn_setup():
        import jax, jax.numpy as jnp
        import numpy as np
        SEQ, BS, H, I, E = (256, 4, 256, 512, 8)
        key = jax.random.key(seed)
        ks = jax.random.split(key, 5)
        s = 0.02
        return {'hidden_states': jax.random.normal(ks[0], (SEQ, BS, H), dtype=jnp.float32), 'router_w': jax.random.normal(ks[1], (H, E), dtype=jnp.float32) * s, 'gate_w': jax.random.normal(ks[2], (E, H, I), dtype=jnp.float32) * s, 'up_w': jax.random.normal(ks[3], (E, H, I), dtype=jnp.float32) * s, 'down_w': jax.random.normal(ks[4], (E, I, H), dtype=jnp.float32) * s}
    _L1_ffn_all = _L1_ffn_setup()
    _L1_ffn_in = {k: v for k, v in _L1_ffn_all.items() if k in ('router_w', 'gate_w', 'up_w', 'down_w')}
    del _L1_ffn_all
    return {'x': x, 'ctx_2048': ctx_2048, 'pos_BxS2': pos_BxS2, 'itok_BxS_4096_4607': itok_BxS_4096_4607, 'g_xattn': g_xattn, 'g_ffn': g_ffn, 'L0_xattn_Wi': _L0_xattn_in['Wi'], 'L0_xattn_bi': _L0_xattn_in['bi'], 'L0_xattn_Wf': _L0_xattn_in['Wf'], 'L0_xattn_bf': _L0_xattn_in['bf'], 'L0_xattn_ln_scale': _L0_xattn_in['ln_scale'], 'L0_ffn_W1': _L0_ffn_in['W1'], 'L0_ffn_W2': _L0_ffn_in['W2'], 'L1_xattn_Wq': _L1_xattn_in['Wq'], 'L1_xattn_Wk': _L1_xattn_in['Wk'], 'L1_xattn_Wv': _L1_xattn_in['Wv'], 'L1_xattn_Wo': _L1_xattn_in['Wo'], 'L1_xattn_q_norm_w': _L1_xattn_in['q_norm_w'], 'L1_xattn_k_norm_w': _L1_xattn_in['k_norm_w'], 'L1_ffn_router_w': _L1_ffn_in['router_w'], 'L1_ffn_gate_w': _L1_ffn_in['gate_w'], 'L1_ffn_up_w': _L1_ffn_in['up_w'], 'L1_ffn_down_w': _L1_ffn_in['down_w']}

def reference(x, ctx_2048, pos_BxS2, itok_BxS_4096_4607, g_xattn, g_ffn, L0_xattn_Wi, L0_xattn_bi, L0_xattn_Wf, L0_xattn_bf, L0_xattn_ln_scale, L0_ffn_W1, L0_ffn_W2, L1_xattn_Wq, L1_xattn_Wk, L1_xattn_Wv, L1_xattn_Wo, L1_xattn_q_norm_w, L1_xattn_k_norm_w, L1_ffn_router_w, L1_ffn_gate_w, L1_ffn_up_w, L1_ffn_down_w):
    import jax
    import jax.numpy as jnp

    def _L0_xattn_ref(q, k, v, Wi, bi, Wf, bf, ln_scale):
        import jax, jax.numpy as jnp
        import numpy as np
        B, S, E, NH = (2, 128, 256, 16)
        DH = E // NH
        EPS = 1e-06

        def _mlstm_forward(q, k, v, Wi, bi, Wf, bf, ln_scale):
            b, s, e = q.shape
            nh = Wi.shape[1]
            dh = e // nh
            x = jnp.concatenate([q, k, v], axis=-1)
            ig = (x @ Wi + bi).transpose(0, 2, 1)[..., None]
            fg = (x @ Wf + bf).transpose(0, 2, 1)[..., None]
            split = lambda t: t.reshape(b, s, nh, dh).transpose(0, 2, 1, 3)
            qh, kh, vh = (split(q), split(k), split(v))
            log_f = jax.nn.log_sigmoid(fg)
            log_f_cum = jnp.concatenate([jnp.zeros((b, nh, 1, 1), q.dtype), jnp.cumsum(log_f, axis=2)], axis=2)
            fg_mat = log_f_cum - jnp.transpose(log_f_cum, (0, 1, 3, 2))
            ltr = jnp.tril(jnp.ones((s, s), dtype=bool))
            log_fg = jnp.where(ltr, fg_mat[:, :, 1:, 1:], -jnp.inf)
            log_D = log_fg + jnp.transpose(ig, (0, 1, 3, 2))
            max_log_D = jnp.max(log_D, axis=-1, keepdims=True)
            D = jnp.exp(log_D - max_log_D)
            qk = jnp.einsum('bhsd,bhtd->bhst', qh, kh) / jnp.sqrt(jnp.asarray(dh, q.dtype))
            C = qk * D
            normalizer = jnp.maximum(jnp.abs(C.sum(-1, keepdims=True)), jnp.exp(-max_log_D))
            Cn = C / (normalizer + EPS)
            h = jnp.einsum('bhst,bhtd->bhsd', Cn, vh)
            mu = h.mean(-1, keepdims=True)
            var = ((h - mu) ** 2).mean(-1, keepdims=True)
            hn = (h - mu) * jax.lax.rsqrt(var + EPS)
            hn = hn * ln_scale.reshape(1, nh, 1, dh)
            return hn.transpose(0, 2, 1, 3).reshape(b, s, e)
        return _mlstm_forward(q, k, v, Wi, bi, Wf, bf, ln_scale)

    def _L0_ffn_ref(x, W1, W2):
        import jax, jax.numpy as jnp
        import numpy as np
        D_MODEL = 256
        D_FF = 1024
        BATCH = 4
        SEQ = 256
        MAX_EXP = 4
        NUM_BITS = 8
        C_CHUNKS = 2
        SCALE = 0.1

        def _pow2_ternary(key, out_dim, in_dim, max_exp):
            k1, k2 = jax.random.split(key)
            t = jax.random.randint(k1, (out_dim, in_dim), -1, 2).astype(jnp.float32)
            e = jax.random.randint(k2, (out_dim, in_dim), 0, max_exp + 1).astype(jnp.float32)
            return t * jnp.exp2(-e)

        def _lookup_act(h):
            total_bits = NUM_BITS * C_CHUNKS
            qmax = 2 ** (total_bits - 1) - 1
            qmin = -2 ** (total_bits - 1)
            q = jnp.clip(jnp.round(h / SCALE), qmin, qmax)
            return jax.nn.gelu(q * SCALE)
        h = jnp.einsum('bsd,fd->bsf', x, W1)
        a = _lookup_act(h)
        return jnp.einsum('bsf,df->bsd', a, W2)

    def _L1_xattn_ref(draft_hidden, context_hidden, Wq, Wk, Wv, Wo, q_norm_w, k_norm_w, context_position_ids, draft_position_ids):
        import jax, jax.numpy as jnp
        import numpy as np
        B, CTX, DRAFT, D = (2, 512, 64, 256)
        H, KVH, HD = (16, 4, 128)
        N_REP = H // KVH
        EPS = 1e-06
        THETA = 10000.0
        SCALE = 1.0 / np.sqrt(HD).astype(np.float32)

        def _rms_norm(x, w):
            v = jnp.mean(jnp.square(x.astype(jnp.float32)), axis=-1, keepdims=True)
            return (w * (x.astype(jnp.float32) * jax.lax.rsqrt(v + EPS))).astype(x.dtype)

        def _rotate_half(x):
            x1, x2 = jnp.split(x, 2, axis=-1)
            return jnp.concatenate((-x2, x1), axis=-1)

        def _rope(x, pos):
            inv_freq = 1.0 / THETA ** (jnp.arange(0, HD, 2, dtype=jnp.float32) / HD)
            freqs = pos.astype(jnp.float32)[:, None, :, None] * inv_freq
            emb = jnp.concatenate((freqs, freqs), axis=-1)
            return x * jnp.cos(emb) + _rotate_half(x) * jnp.sin(emb)
        bsz, draft_len, _ = draft_hidden.shape
        ctx_len = context_hidden.shape[1]
        total_len = ctx_len + draft_len
        q = (draft_hidden @ Wq.T).reshape(bsz, draft_len, H, HD)
        q = _rms_norm(q, q_norm_w).transpose(0, 2, 1, 3)
        kv_in = jnp.concatenate([context_hidden, draft_hidden], axis=1)
        k = (kv_in @ Wk.T).reshape(bsz, total_len, KVH, HD)
        v = (kv_in @ Wv.T).reshape(bsz, total_len, KVH, HD).transpose(0, 2, 1, 3)
        k = _rms_norm(k, k_norm_w).transpose(0, 2, 1, 3)
        full_position_ids = jnp.concatenate([context_position_ids, draft_position_ids], axis=1)
        q = _rope(q, draft_position_ids)
        k = _rope(k, full_position_ids)
        k = jnp.repeat(k, N_REP, axis=1)
        v = jnp.repeat(v, N_REP, axis=1)
        scores = jnp.einsum('bhqd,bhkd->bhqk', q, k) * SCALE
        probs = jax.nn.softmax(scores, axis=-1)
        attn = jnp.einsum('bhqk,bhkd->bhqd', probs, v)
        attn = attn.transpose(0, 2, 1, 3).reshape(bsz, draft_len, H * HD)
        return attn @ Wo.T

    def _L1_ffn_ref(hidden_states, router_w, gate_w, up_w, down_w):
        import jax, jax.numpy as jnp
        import numpy as np
        SEQ, BS, H, I, E = (256, 4, 256, 512, 8)
        router_logits = jnp.einsum('sbh,he->sbe', hidden_states, router_w)
        routing_indices = jnp.argmax(router_logits, axis=-1)
        routing_weights = jax.nn.sigmoid(jnp.max(router_logits, axis=-1))
        out = jnp.zeros_like(hidden_states)
        for e in range(E):
            mask = (routing_indices == e)[..., None]
            g = jnp.einsum('sbh,hi->sbi', hidden_states, gate_w[e])
            u = jnp.einsum('sbh,hi->sbi', hidden_states, up_w[e])
            y = jnp.einsum('sbi,ih->sbh', jax.nn.silu(g) * u, down_w[e])
            out = out + jnp.where(mask, y, jnp.zeros((), out.dtype))
        return out
    x = x + jnp.tanh(g_xattn[0]) * _L0_xattn_ref(_layernorm(x, axis=-1), ctx_2048, ctx_2048, L0_xattn_Wi, L0_xattn_bi, L0_xattn_Wf, L0_xattn_bf, L0_xattn_ln_scale)
    x = x + jnp.tanh(g_ffn[0]) * _L0_ffn_ref(_layernorm(x, axis=-1), L0_ffn_W1, L0_ffn_W2)
    x = x + jnp.tanh(g_xattn[1]) * _L1_xattn_ref(_layernorm(x, axis=-1), ctx_2048, L1_xattn_Wq, L1_xattn_Wk, L1_xattn_Wv, L1_xattn_Wo, L1_xattn_q_norm_w, L1_xattn_k_norm_w, pos_BxS2, itok_BxS_4096_4607)
    x = x + jnp.tanh(g_ffn[1]) * _L1_ffn_ref(_layernorm(x, axis=-1), L1_ffn_router_w, L1_ffn_gate_w, L1_ffn_up_w, L1_ffn_down_w)
    return x

_drawn_inputs = setup_inputs


def setup_inputs(seed=0):
    import zlib

    import numpy as np

    out = dict(_drawn_inputs(seed))
    spreads = {'g_ffn': (-1.0, 0.6),
     'L0_xattn_ln_scale': (1.0, 0.2),
     'L1_xattn_q_norm_w': (1.0, 0.6),
     'L1_xattn_k_norm_w': (1.0, 0.6)}
    factors = {'L0_xattn_bi': 64.0,
     'L0_xattn_Wf': 3.612,
     'L1_xattn_Wq': 8.0,
     'L1_xattn_Wk': 8.0,
     'L1_xattn_Wv': 8.0,
     'L1_xattn_Wo': 8.0,
     'L1_ffn_router_w': 8.0,
     'L1_ffn_gate_w': 8.0,
     'L1_ffn_up_w': 8.0,
     'L1_ffn_down_w': 8.0}
    for name, (base, spread) in spreads.items():
        noise = np.random.default_rng([zlib.crc32(name.encode()), seed]).standard_normal(out[name].shape)
        drawn = base * np.exp(spread * noise) if base else spread * noise
        out[name] = jnp.asarray(drawn.astype(out[name].dtype))
    for name, factor in factors.items():
        out[name] = (out[name] * factor).astype(out[name].dtype)
    return out
```

```python
from contextlib import ExitStack

import concourse.bass as bass
from concourse import mybir
from concourse.alu_op_type import AluOpType as ALU
import numpy as np

F32 = mybir.dt.float32
F32R = mybir.dt.float32r
I32 = mybir.dt.int32
U32 = mybir.dt.uint32
ACT = mybir.ActivationFunctionType
AX = mybir.AxisListType

P = 128
B = 4
S_LEN = 256
D = 256
TOK = B * S_LEN
TILES = TOK // P
DC = D // P
TPB = S_LEN // P

M_HEADS = 16
M_DH = D // M_HEADS
HALF = P // M_DH
AUG = M_DH + 1

FF = 1024
FC = FF // P

HEADS = 16
KV_HEADS = 4
HD = 128
REP = HEADS // KV_HEADS
KEYS = 2 * S_LEN
KT_TILES = KEYS // P
ROT = HD // 2

EXPERTS = 8
INNER = 512
IC = INNER // P
SLOT_TILES = (TOK - EXPERTS) // P + EXPERTS
SLOTS = SLOT_TILES * P

LN_EPS = 1e-5
EPS = 1e-6
ROUND = 12582912.0
PI_CLAMP = 3.1415925

C_IDENT = 0
C_ONES = C_IDENT + P
C_TRI = C_ONES + P
C_PAR = C_TRI + P
C_BDM = C_PAR + 2
C_SPLIT = C_BDM + HALF * AUG
C_FREQ = C_SPLIT + 2
C_NEGHALF = C_FREQ + ROT
C_TILE = C_NEGHALF + 64
C_EXP = C_TILE + SLOT_TILES
C_WIDE = C_EXP + EXPERTS


def host_constants():
    c = np.zeros((P, C_WIDE), np.float32)
    p = np.arange(P)
    c[:, C_IDENT:C_IDENT + P] = np.eye(P)
    c[:, C_ONES:C_ONES + P] = 1.0
    c[:, C_TRI:C_TRI + P] = p[:, None] < p[None, :]
    for par in range(2):
        c[:, C_PAR + par] = np.where((p // M_DH) % 2 == par, float(M_DH) ** -0.5, 0.0)
    c[:, C_BDM:C_BDM + HALF * AUG] = np.repeat(p[:, None] // M_DH == np.arange(HALF)[None, :], AUG, 1)
    c[:, C_SPLIT] = p % 32 >= 16
    c[:, C_SPLIT + 1] = np.where(p % 32 >= 16, -1.0, 1.0)
    freq = np.float32(1.0) / np.float32(10000.0) ** (np.arange(0, HD, 2, dtype=np.float32) / np.float32(HD))
    c[:, C_FREQ:C_FREQ + ROT] = freq
    c[:, C_NEGHALF:C_NEGHALF + 64] = -0.5
    c[:, C_TILE:C_TILE + SLOT_TILES] = np.arange(SLOT_TILES)
    c[:, C_EXP:C_EXP + EXPERTS] = np.arange(EXPERTS)
    sel = np.zeros((32, M_HEADS, P), np.float32)
    for h in range(M_HEADS):
        sel[h, h] = 1.0
        sel[16 + h, h] = 1.0
    return c, sel.reshape(32, M_HEADS * P)


class Memory:

    def __init__(self, nc, stack):
        self.nc, self.stack = nc, stack

    def sb(self, name, shape, dt=F32):
        return self.stack.enter_context(self.nc.sbuf_tensor(name, shape, dt))

    def ps(self, name, banks):
        return self.stack.enter_context(self.nc.psum_tensor(name, [P, banks, 512], F32))

    def sem(self, name):
        return self.stack.enter_context(self.nc.semaphore(name))


def first_then_loop(eng, n, body):
    body(0)
    with eng.Fori(1, n) as j:
        body(j)


def wait_for(eng, sem, count):
    if not (isinstance(count, int) and count == 0):
        eng.wait_ge(sem, count)


def layernorm_transposed(nc, tag, X, lnT, ident, const, const_ready=None, x_ready=None, kept=None):
    with ExitStack() as st:
        m = Memory(nc, st)
        stats = m.sb(f"{tag}_stats", [P, TILES, 6])
        mv = m.sb(f"{tag}_mv", [P, TILES, 2])
        ve = m.sb(f"{tag}_ve", [P, TILES])
        rstd = m.sb(f"{tag}_rstd", [P, TILES])
        ln = m.sb(f"{tag}_ln", [P, 2, TPB, D]) if kept is None else None
        lnps = m.ps(f"{tag}_lnps", 2)
        stats_done = m.sem(f"{tag}_stats_done")
        mv_done = m.sem(f"{tag}_mv_done")
        ve_done = m.sem(f"{tag}_ve_done")
        rstd_done = m.sem(f"{tag}_rstd_done")
        ln_done = m.sem(f"{tag}_ln_done")
        turned = m.sem(f"{tag}_turned")
        stored = m.sem(f"{tag}_stored")
        with nc.Block() as block:
            @block.vector
            def _(dve):
                if x_ready is not None:
                    dve.wait_ge(*x_ready)

                def tile(t):
                    dve.bn_stats(stats[:, t, :], X[:, t, :]).then_inc(stats_done, 1)

                first_then_loop(dve, TILES, tile)
                dve.wait_ge(stats_done, TILES)
                for t in range(TILES):
                    dve.bn_aggr(mv[:, t, :], stats[:, t, :]).then_inc(mv_done, 1)
                dve.wait_ge(rstd_done, 1)

                def normalise(j):
                    for par in range(2):
                        wait_for(dve, turned, 2 * j)
                        for tt in range(TPB):
                            t = 4 * j + 2 * par + tt
                            dve.tensor_scalar(ln[:, par, tt, :] if kept is None else kept[:, t, :],
                                              X[:, t, :], mv[:, t, 0:1], rstd[:, bass.ds(t, 1)],
                                              ALU.subtract, ALU.mult).then_inc(ln_done, 1)

                for j in range(2):
                    normalise(j)

            @block.gpsimd
            def _(pool):
                if const_ready is not None:
                    pool.wait_ge(*const_ready)
                pool.wait_ge(mv_done, TILES)
                pool.tensor_scalar(ve[:, :], mv[:, :, 1], LN_EPS, 1.0, ALU.add, ALU.mult).then_inc(ve_done, 1)
                pool.wait_ge(ve_done, 1)
                pool.tensor_tensor(rstd[:, :], ve[:, :], const[:, C_NEGHALF:C_NEGHALF + TILES],
                                   ALU.pow).then_inc(rstd_done, 1)

            @block.tensor
            def _(pe):
                if const_ready is not None:
                    pe.wait_ge(*const_ready)

                def turn(j):
                    for par in range(2):
                        pe.wait_ge(ln_done, 4 * j + 2 * par + 2)
                        wait_for(pe, stored, 2 * j)
                        for tt in range(TPB):
                            src = ln[:, par, tt, :] if kept is None else kept[:, 4 * j + 2 * par + tt, :]
                            for c in range(DC):
                                last = pe.transpose(lnps[:, par, c * S_LEN + tt * P:c * S_LEN + (tt + 1) * P],
                                                    src[:, c * P:(c + 1) * P], ident)
                        last.then_inc(turned, 1)

                for j in range(2):
                    turn(j)

            @block.scalar
            def _(act):

                def pair(j):
                    for par in range(2):
                        act.wait_ge(turned, 2 * j + par + 1)
                        act.activation(lnT[:, :, bass.ds((2 * j + par) * S_LEN, S_LEN)],
                                       lnps[:, par, :].rearrange("p (c s) -> p c s", c=DC),
                                       ACT.Copy).then_inc(stored, 1)

                first_then_loop(act, 2, pair)


def mlstm_rows(nc, mem, lnT, ctxT, gate_w, gate_b, sel, const, cols, Gr, Mr, selr, ident, loads):
    with ExitStack() as st:
        m = Memory(nc, st)
        z = m.sb("a_z", [32, TOK])
        soft = m.sb("a_soft", [32, TOK])
        logf = m.sb("a_logf", [32, TOK])
        F = m.sb("a_F", [32, TOK])
        Fs = m.sb("a_Fs", [32, TOK])
        g = m.sb("a_g", [32, TOK])
        M = m.sb("a_M", [32, TOK])
        dup = m.sb("a_dup", [32, TOK])
        hi = m.sb("a_hi", [32, TOK], F32R)
        low = m.sb("a_low", [32, TOK])
        ones = m.sb("a_ones", [32, S_LEN])
        ex = m.sb("a_ex", [32, B, 4, P])
        zps = m.ps("a_zps", 2)
        cps = m.ps("a_cps", 1)
        gates_done = m.sem("a_gates_done")
        z_done = m.sem("a_z_done")
        act_step = m.sem("a_act_step")
        row_step = m.sem("a_row_step")
        ones_done = m.sem("a_ones_done")
        arg_done = m.sem("a_arg_done")
        ex_done = m.sem("a_ex_done")
        cols_turned = m.sem("a_cols_turned")
        shift = [16 + i for i in range(16)] + [16 + i for i in range(16)]
        twice = [i % 16 for i in range(32)]
        with nc.Block() as block:
            @block.tensor
            def _(pe):
                for ready in loads:
                    pe.wait_ge(*ready)
                for half in range(2):
                    for c in range(3 * DC):
                        src = lnT if c < DC else ctxT
                        last = pe.matmul(zps[0:32, half, :], gate_w[:, c, :],
                                         src[:, c % DC, half * 512:(half + 1) * 512],
                                         start=(c == 0), stop=(c == 3 * DC - 1))
                last.then_inc(gates_done, 1)
                pe.wait_ge(ex_done, 1)
                for b in range(B):
                    for kind in range(4):
                        last = pe.transpose(cps[:, 0, (b * 4 + kind) * 32:(b * 4 + kind + 1) * 32],
                                            ex[:, b, kind, :], ident[0:32, 0:32])
                last.then_inc(cols_turned, 1)

            @block.scalar
            def _(act):
                act.wait_ge(z_done, 1)
                act.activation(soft[:, :], z[:, :], ACT.Abs).then_inc(act_step, 1)
                act.wait_ge(act_step, 1)
                act.activation(soft[:, :], soft[:, :], ACT.Exp, scale=-1.0).then_inc(act_step, 1)
                act.wait_ge(act_step, 2)
                act.activation(soft[:, :], soft[:, :], ACT.Ln, bias=1.0).then_inc(act_step, 1)
                act.wait_ge(arg_done, 4)
                act.activation(ex[:, :, :, :], ex[:, :, :, :], ACT.Exp).then_inc(ex_done, 1)
                act.wait_ge(cols_turned, 1)
                act.activation(cols[:, :, :, :].rearrange("p b k r -> p (b k r)"), cps[:, 0, :], ACT.Copy)

            @block.vector
            def _(dve):
                dve.memset(ones[:, :], 1.0).then_inc(ones_done, 1)
                for ready in loads:
                    dve.wait_ge(*ready)
                dve.tensor_copy(selr[:, :], sel[:, :])
                dve.wait_ge(gates_done, 1)
                dve.tensor_scalar(z[:, :], zps[0:32, :, :].rearrange("p a n -> p (a n)"), gate_b[:, 0:1], None,
                                  ALU.add).then_inc(z_done, 1)
                dve.wait_ge(z_done, 1)
                dve.wait_ge(act_step, 3)
                dve.scalar_tensor_tensor(out=logf[:, :], in0=z[:, :], scalar=0.0, in1=soft[:, :],
                                         op0=ALU.min, op1=ALU.subtract).then_inc(row_step, 1)
                dve.wait_ge(row_step, 1)
                dve.wait_ge(ones_done, 1)
                for b in range(B):
                    s = slice(b * S_LEN, (b + 1) * S_LEN)
                    dve.tensor_tensor_scan(F[:, s], ones[:, :], logf[:, s], 0.0, ALU.mult,
                                           ALU.add).then_inc(row_step, 1)
                dve.wait_ge(row_step, 5)
                dve.stream_shuffle(Fs[:, :], F[:, :], shift).then_inc(row_step, 1)
                dve.wait_ge(row_step, 6)
                dve.tensor_tensor(g[:, :], z[:, :], Fs[:, :], ALU.subtract).then_inc(row_step, 1)
                dve.wait_ge(row_step, 7)
                for b in range(B):
                    s = slice(b * S_LEN, (b + 1) * S_LEN)
                    dve.tensor_tensor_scan(M[:, s], g[:, s], g[:, s], -3.0e38, ALU.max,
                                           ALU.max).then_inc(row_step, 1)
                dve.wait_ge(row_step, 11)
                M4 = M[:, :].rearrange("p (b k s) -> p b k s", b=B, k=2)
                F4 = Fs[:, :].rearrange("p (b k s) -> p b k s", b=B, k=2)
                g4 = g[:, :].rearrange("p (b k s) -> p b k s", b=B, k=2)
                last0 = M4[:, :, 0, P - 1:P].to_broadcast([32, B, P])
                for k in range(2):
                    dve.scalar_tensor_tensor(out=ex[:, :, k, :], in0=M4[:, :, k, :], scalar=-1.0,
                                             in1=F4[:, :, k, :], op0=ALU.mult,
                                             op1=ALU.subtract).then_inc(arg_done, 1)
                dve.tensor_tensor(ex[:, :, 2, :], g4[:, :, 0, :], last0, ALU.subtract).then_inc(arg_done, 1)
                dve.tensor_tensor(ex[:, :, 3, :], last0, M4[:, :, 1, :], ALU.subtract).then_inc(arg_done, 1)
                step = 11
                for src, sign, dst in ((g, 1.0, Gr), (M, -1.0, Mr)):
                    dve.stream_shuffle(dup[:, :], src[:, :], twice).then_inc(row_step, 1)
                    dve.wait_ge(row_step, step + 1)
                    dve.tensor_scalar(hi[:, :], dup[:, :], sign, None, ALU.mult).then_inc(row_step, 1)
                    dve.tensor_scalar(low[:, :], dup[:, :], const[0:32, C_SPLIT:C_SPLIT + 1], sign, ALU.mult,
                                      ALU.mult).then_inc(row_step, 1)
                    dve.wait_ge(row_step, step + 3)
                    dve.scalar_tensor_tensor(out=dst[:, :], in0=hi[:, :].bitcast(F32),
                                             scalar=const[0:32, C_SPLIT + 1:C_SPLIT + 2], in1=low[:, :],
                                             op0=ALU.mult, op1=ALU.add).then_inc(row_step, 1)
                    step += 4


def mlstm_heads(nc, mem, X, lnT, ctx, ctxT, cols, Gr, Mr, selr, scale_row, const):
    HH = M_HEADS // HALF
    W = HALF * AUG
    with ExitStack() as st:
        m = Memory(nc, st)
        kT = m.sb("b_kT", [P, DC, S_LEN])
        Gb = m.sb("b_Gb", [32, S_LEN], F32R)
        Qm = m.sb("b_Qm", [P, DC, 2, S_LEN])
        V1 = m.sb("b_V1", [P, TPB, M_HEADS, AUG])
        KU = m.sb("b_KU", [P, D])
        BD = m.sb("b_BD", [P, HH, W])
        E = m.sb("b_E", [P, 2, HALF, P])
        C = m.sb("b_C", [P, 2, HALF, P])
        num = m.sb("b_num", [P, TPB, M_HEADS, AUG])
        carried = m.sb("b_carried", [P, M_HEADS, AUG])
        den = m.sb("b_den", [P, TPB, M_HEADS])
        rden = m.sb("b_rden", [P, TPB, M_HEADS])
        h = m.sb("b_h", [P, TPB * M_HEADS, M_DH])
        hc = m.sb("b_hc", [P, TPB * M_HEADS, M_DH])
        sq = m.sb("b_sq", [P, TPB * M_HEADS, M_DH])
        hsum = m.sb("b_hsum", [P, TPB * M_HEADS])
        vsum = m.sb("b_vsum", [P, TPB * M_HEADS])
        ve = m.sb("b_ve", [P, TPB * M_HEADS])
        rs = m.sb("b_rs", [P, TPB * M_HEADS])
        hn = m.sb("b_hn", [P, TPB, D])
        sps = m.ps("b_sps", 4)
        eps_ = m.ps("b_eps", 2)
        pvps = m.ps("b_pvps", 1)
        stps = m.ps("b_stps", 1)
        ones_in = m.sem("b_ones_in")
        k_ready = m.sem("b_k_ready")
        g_ready = m.sem("b_g_ready")
        q_ready = m.sem("b_q_ready")
        v_ready = m.sem("b_v_ready")
        ku_ready = m.sem("b_ku_ready")
        state_done = m.sem("b_state_done")
        bd_ready = m.sem("b_bd_ready")
        decay_done = m.sem("b_decay_done")
        scores_done = m.sem("b_scores_done")
        exp_done = m.sem("b_exp_done")
        masked = m.sem("b_masked")
        prod_done = m.sem("b_prod_done")
        pv_done = m.sem("b_pv_done")
        carry_done = m.sem("b_carry_done")
        num_done = m.sem("b_num_done")
        step = m.sem("b_step")
        centred = m.sem("b_centred")
        squared = m.sem("b_squared")
        var_done = m.sem("b_var_done")
        ve_done = m.sem("b_ve_done")
        rs_done = m.sem("b_rs_done")
        x_done = m.sem("b_x_done")
        STEPS = 10
        UNITS = TPB * HH
        with nc.Block() as block:
            @block.gpsimd
            def _(pool):
                for b in range(B):
                    wait_for(pool, scores_done, UNITS * b)
                    pool.tensor_scalar(kT[:, :, :], ctxT[:, :, bass.ds(b * S_LEN, S_LEN)], 1.0, 1.0,
                                       ALU.mult, ALU.mult).then_inc(k_ready, 1)
                    for u in range(UNITS):
                        pool.wait_ge(exp_done, UNITS * b + u + 1)
                        pool.affine_select(out=E[:, u % 2, :, :], in_=E[:, u % 2, :, :], compare_op=ALU.is_ge,
                                           fill=0.0, base=0, pattern=[[0, HALF], [1, P]],
                                           channel_multiplier=-1).then_inc(masked, 1)
                    pool.wait_ge(var_done, b + 1)
                    pool.tensor_scalar(ve[:, :], vsum[:, :], 1.0 / M_DH, EPS, ALU.mult,
                                       ALU.add).then_inc(ve_done, 1)
                    pool.wait_ge(ve_done, b + 1)
                    pool.tensor_tensor(rs[:, :], ve[:, :], const[:, C_NEGHALF:C_NEGHALF + TPB * M_HEADS],
                                       ALU.pow).then_inc(rs_done, 1)

            @block.scalar
            def _(act):
                act.wait_ge(ones_in, 1)

                def batch(b):
                    wait_for(act, pv_done, UNITS * b)
                    act.activation(V1[:, :, :, 0:M_DH].rearrange("p t h d -> p (t h) d"),
                                   ctx[:, bass.ds(b * TPB, TPB), :].rearrange("p t (h d) -> p (t h) d", d=M_DH),
                                   ACT.Copy).then_inc(v_ready, 1)
                    for u in range(UNITS):
                        act.wait_ge(decay_done, UNITS * b + u + 1)
                        wait_for(act, prod_done, UNITS * b + max(u - 1, 0))
                        act.activation(E[:, u % 2, :, :].rearrange("p (a h) s -> p a (h s)", a=2),
                                       eps_[:, :, :], ACT.Exp).then_inc(exp_done, 1)
                    act.wait_ge(centred, b + 1)
                    act.activation(sq[:, :, :], hc[:, :, :], ACT.Square).then_inc(squared, 1)

                first_then_loop(act, B, batch)

            @block.vector
            def _(dve):
                dve.memset(V1[:, :, :, M_DH:AUG], 1.0).then_inc(ones_in, 1)

                def batch(b):
                    wait_for(dve, decay_done, UNITS * b)
                    dve.tensor_copy(Gb[:, :], Gr[:, bass.ds(b * S_LEN, S_LEN)].bitcast(F32)).then_inc(g_ready, 1)
                    wait_for(dve, scores_done, UNITS * b)
                    wait_for(dve, carry_done, b)
                    for par in range(2):
                        dve.tensor_scalar(Qm[:, :, par, :], lnT[:, :, bass.ds(b * S_LEN, S_LEN)],
                                          const[:, C_PAR + par:C_PAR + par + 1], None,
                                          ALU.mult).then_inc(q_ready, 1)
                    wait_for(dve, state_done, b)
                    dve.tensor_tensor(KU[:, :].rearrange("p (h d) -> p h d", d=M_DH),
                                      ctx[:, b * TPB, :].rearrange("p (h d) -> p h d", d=M_DH),
                                      cols[:, b, 2, 0:M_HEADS].unsqueeze(2).to_broadcast([P, M_HEADS, M_DH]),
                                      ALU.mult).then_inc(ku_ready, 1)
                    dve.wait_ge(state_done, b + 1)
                    dve.tensor_tensor(BD[:, :, :], stps[:, 0, 0:HH * W].rearrange("p (a w) -> p a w", a=HH),
                                      const[:, C_BDM:C_BDM + W].unsqueeze(1).to_broadcast([P, HH, W]),
                                      ALU.mult).then_inc(bd_ready, 1)

                    def product(u):
                        dve.wait_ge(scores_done, UNITS * b + u + 1)
                        dve.wait_ge(masked, UNITS * b + u + 1)
                        if u >= 2:
                            dve.wait_ge(pv_done, UNITS * b + u - 1)
                        dve.tensor_tensor(C[:, u % 2, :, :].rearrange("p (g h) s -> p g (h s)", g=4),
                                          sps[:, :, 0:2 * P],
                                          E[:, u % 2, :, :].rearrange("p (g h) s -> p g (h s)", g=4),
                                          ALU.mult).then_inc(prod_done, 1)

                    product(0)
                    product(1)
                    product(2)
                    dve.wait_ge(pv_done, UNITS * b + 2)
                    dve.tensor_copy(num[:, 0, :, :].rearrange("p h a -> p (h a)"),
                                    pvps[:, 0, 0:HH * W]).then_inc(num_done, 1)
                    product(3)
                    dve.wait_ge(carry_done, b + 1)
                    dve.tensor_tensor(carried[:, :, :], stps[:, 0, 0:HH * W].rearrange("p (h a) -> p h a", a=AUG),
                                      cols[:, b, 3, 0:M_HEADS].unsqueeze(2).to_broadcast([P, M_HEADS, AUG]),
                                      ALU.mult).then_inc(step, 1)
                    dve.wait_ge(step, STEPS * b + 1)
                    dve.wait_ge(pv_done, UNITS * b + 4)
                    dve.tensor_tensor(num[:, 1, :, :].rearrange("p h a -> p (h a)"), pvps[:, 0, 0:HH * W],
                                      carried[:, :, :].rearrange("p h a -> p (h a)"),
                                      ALU.add).then_inc(num_done, 1)
                    dve.wait_ge(num_done, 2 * b + 2)
                    dve.scalar_tensor_tensor(out=den[:, :, :], in0=num[:, :, :, M_DH], scalar=-1.0,
                                             in1=num[:, :, :, M_DH], op0=ALU.mult,
                                             op1=ALU.max).then_inc(step, 1)
                    dve.wait_ge(step, STEPS * b + 2)
                    dve.tensor_tensor(den[:, :, :], den[:, :, :], cols[:, b, 0:TPB, 0:M_HEADS],
                                      ALU.max).then_inc(step, 1)
                    dve.wait_ge(step, STEPS * b + 3)
                    dve.tensor_scalar(den[:, :, :], den[:, :, :], EPS, None, ALU.add).then_inc(step, 1)
                    dve.wait_ge(step, STEPS * b + 4)
                    dve.reciprocal(rden[:, :, :], den[:, :, :]).then_inc(step, 1)
                    dve.wait_ge(step, STEPS * b + 5)
                    dve.tensor_tensor(h[:, :, :], num[:, :, :, 0:M_DH].rearrange("p t h d -> p (t h) d"),
                                      rden[:, :, :].rearrange("p t h -> p (t h)").unsqueeze(2)
                                      .to_broadcast([P, TPB * M_HEADS, M_DH]), ALU.mult).then_inc(step, 1)
                    dve.wait_ge(step, STEPS * b + 6)
                    dve.tensor_reduce(hsum[:, :], h[:, :, :], AX.X, ALU.add).then_inc(step, 1)
                    dve.wait_ge(step, STEPS * b + 7)
                    dve.scalar_tensor_tensor(out=hc[:, :, :],
                                             in0=hsum[:, :].unsqueeze(2).to_broadcast([P, TPB * M_HEADS, M_DH]),
                                             scalar=-1.0 / M_DH, in1=h[:, :, :], op0=ALU.mult,
                                             op1=ALU.add).then_inc(centred, 1)
                    dve.wait_ge(squared, b + 1)
                    dve.tensor_reduce(vsum[:, :], sq[:, :, :], AX.X, ALU.add).then_inc(var_done, 1)
                    dve.wait_ge(rs_done, b + 1)
                    dve.tensor_tensor(hn[:, :, :].rearrange("p t (h d) -> p (t h) d", d=M_DH), hc[:, :, :],
                                      rs[:, :].unsqueeze(2).to_broadcast([P, TPB * M_HEADS, M_DH]),
                                      ALU.mult).then_inc(step, 1)
                    dve.wait_ge(step, STEPS * b + 8)
                    dve.tensor_tensor(hn[:, :, :], hn[:, :, :],
                                      scale_row[:, :].unsqueeze(1).to_broadcast([P, TPB, D]),
                                      ALU.mult).then_inc(step, 1)
                    dve.wait_ge(step, STEPS * b + 9)
                    dve.tensor_tensor(X[:, bass.ds(b * TPB, TPB), :], X[:, bass.ds(b * TPB, TPB), :],
                                      hn[:, :, :], ALU.add).then_inc(step, 1)
                    dve.wait_ge(step, STEPS * b + 10)

                first_then_loop(dve, B, batch)

            @block.tensor
            def _(pe):

                def batch(b):
                    def decay(u):
                        blk, hh = divmod(u, HH)
                        if u == 0:
                            pe.wait_ge(g_ready, b + 1)
                        wait_for(pe, exp_done, UNITS * b + u)
                        for a in range(2):
                            pe.matmul(eps_[:, a, :], Gb[:, blk * P:(blk + 1) * P],
                                      selr[:, (hh * 2 + a) * 512:(hh * 2 + a + 1) * 512], start=True, stop=False)
                            for k in range(4):
                                hd = hh * HALF + a * 4 + k
                                last = pe.matmul(eps_[:, a, k * P:(k + 1) * P], selr[:, hd * P:(hd + 1) * P],
                                                 Mr[:, bass.ds(b * S_LEN + blk * P, P)], start=False,
                                                 stop=(k == 3))
                        last.then_inc(decay_done, 1)

                    def scores(u):
                        blk, hh = divmod(u, HH)
                        if u == 0:
                            pe.wait_ge(q_ready, 2 * b + 2)
                            pe.wait_ge(k_ready, b + 1)
                        wait_for(pe, prod_done, UNITS * b + u)
                        for grp in range(4):
                            r = slice(32 * grp, 32 * grp + 32)
                            last = pe.matmul(sps[:, grp, 0:2 * P].rearrange("p (a s) -> p a s", a=2),
                                             kT[r, hh, blk * P:(blk + 1) * P],
                                             Qm[r, hh, :, blk * P:(blk + 1) * P], start=True, stop=True)
                        last.then_inc(scores_done, 1)

                    def values(u):
                        blk, hh = divmod(u, HH)
                        pe.wait_ge(prod_done, UNITS * b + u + 1)
                        if hh == 0:
                            wait_for(pe, num_done, 2 * b + blk)
                        for k in range(HALF):
                            hd = hh * HALF + k
                            last = pe.matmul(pvps[:, 0, hd * AUG:(hd + 1) * AUG], C[:, u % 2, k, :],
                                             V1[:, blk, hd, :], start=True, stop=True)
                        last.then_inc(pv_done, 1)

                    decay(0)
                    scores(0)
                    pe.wait_ge(ku_ready, b + 1)
                    pe.wait_ge(v_ready, b + 1)
                    wait_for(pe, num_done, 2 * b)
                    for hh in range(HH):
                        last = pe.matmul(stps[:, 0, hh * W:(hh + 1) * W], KU[:, hh * P:(hh + 1) * P],
                                         V1[:, 0, hh * HALF:(hh + 1) * HALF, :].rearrange("p h a -> p (h a)"),
                                         start=True, stop=True)
                    last.then_inc(state_done, 1)
                    decay(1)
                    scores(1)
                    values(0)
                    decay(2)
                    scores(2)
                    pe.wait_ge(bd_ready, b + 1)
                    for hh in range(HH):
                        for par in range(2):
                            last = pe.matmul(stps[:, 0, hh * W:(hh + 1) * W], Qm[:, hh, par, P:2 * P],
                                             BD[:, hh, :], start=(par == 0), stop=(par == 1))
                    last.then_inc(carry_done, 1)
                    values(1)
                    decay(3)
                    scores(3)
                    values(2)
                    values(3)

                first_then_loop(pe, B, batch)


def quantised_ffn(nc, X, lnT, w1, w2, gains, loads):
    QUARTER = FC // 4
    with ExitStack() as st:
        m = Memory(nc, st)
        q = m.sb("f_q", [P, 2, 2 * S_LEN])
        r = m.sb("f_r", [P, 2, 2 * S_LEN])
        a = m.sb("f_a", [P, FC, S_LEN])
        hps = m.ps("f_hps", 4)
        ops = m.ps("f_ops", 2)
        up_done = m.sem("f_up_done")
        clipped = m.sem("f_clipped")
        rounded = m.sem("f_rounded")
        scaled = m.sem("f_scaled")
        gelu_done = m.sem("f_gelu_done")
        down_done = m.sem("f_down_done")
        x_done = m.sem("f_x_done")
        with nc.Block() as block:
            @block.tensor
            def _(pe):
                for ready in loads:
                    pe.wait_ge(*ready)

                def up(b):
                    for n in range(4):
                        wait_for(pe, clipped, 4 * b)
                        for f in range(QUARTER):
                            fc = n * QUARTER + f
                            for c in range(DC):
                                last = pe.matmul(hps[:, n, f * S_LEN:(f + 1) * S_LEN],
                                                 w1[:, c, fc * P:(fc + 1) * P],
                                                 lnT[:, c, bass.ds(b * S_LEN, S_LEN)],
                                                 start=(c == 0), stop=(c == DC - 1))
                        last.then_inc(up_done, 1)

                def down(b):
                    pe.wait_ge(gelu_done, 4 * b + 4)
                    for tt in range(TPB):
                        wait_for(pe, x_done, TPB * b)
                        for fc in range(FC):
                            last = pe.matmul(ops[:, tt, 0:D], a[:, fc, tt * P:(tt + 1) * P], w2[:, fc, :],
                                             start=(fc == 0), stop=(fc == FC - 1))
                        last.then_inc(down_done, 1)


                def batch(b):
                    up(b)
                    down(b)

                first_then_loop(pe, B, batch)

            @block.vector
            def _(dve):

                def batch(b):
                    for n in range(4):
                        dve.wait_ge(up_done, 4 * b + n + 1)
                        if n >= 2:
                            dve.wait_ge(rounded, 4 * b + n - 1)
                        dve.tensor_scalar(q[:, n % 2, :], hps[:, n, :], 10.0, 32767.0, ALU.mult,
                                          ALU.min).then_inc(clipped, 1)
                        dve.wait_ge(clipped, 4 * b + n + 1)
                        wait_for(dve, gelu_done, 4 * b + max(n - 1, 0))
                        dve.tensor_scalar(r[:, n % 2, :], q[:, n % 2, :], -32768.0, ROUND, ALU.max,
                                          ALU.add).then_inc(rounded, 1)
                    for tt in range(TPB):
                        dve.wait_ge(down_done, TPB * b + tt + 1)
                        dve.scalar_tensor_tensor(out=X[:, b * TPB + tt, :], in0=ops[:, tt, 0:D],
                                                 scalar=gains[:, 2:3], in1=X[:, b * TPB + tt, :],
                                                 op0=ALU.mult, op1=ALU.add).then_inc(x_done, 1)

                first_then_loop(dve, B, batch)

            @block.gpsimd
            def _(pool):
                for b in range(B):
                    for n in range(4):
                        pool.wait_ge(rounded, 4 * b + n + 1)
                        pool.tensor_scalar(r[:, n % 2, :], r[:, n % 2, :], -ROUND, 0.1, ALU.add,
                                           ALU.mult).then_inc(scaled, 1)

            @block.scalar
            def _(act):

                def batch(b):
                    wait_for(act, down_done, TPB * b)
                    for n in range(4):
                        act.wait_ge(scaled, 4 * b + n + 1)
                        act.activation(a[:, n * QUARTER:(n + 1) * QUARTER, :].rearrange("p f s -> p (f s)"),
                                       r[:, n % 2, :], ACT.Gelu_apprx_tanh).then_inc(gelu_done, 1)

                first_then_loop(act, B, batch)


TWO_PI = 2.0 * float(np.pi)
PI_HIGH = 6.28125
PI_MID = float(np.round((TWO_PI - PI_HIGH) * 2.0 ** 21) / 2.0 ** 21)
PI_LOW = TWO_PI - PI_HIGH - PI_MID


def rope_tables(nc, pos, kw, qw, kcos, ksin, qcos, qsin, const, loads):
    NT = 2 * TILES
    with ExitStack() as st:
        m = Memory(nc, st)
        posf = m.sb("r_posf", [P, NT])
        ang = m.sb("r_ang", [P, NT, ROT])
        turns = m.sb("r_turns", [P, NT, ROT])
        rem = m.sb("r_rem", [P, NT, ROT])
        sc = m.sb("r_sc", [P, 2, NT, ROT])
        step = m.sem("r_step")
        arg_ready = m.sem("r_arg_ready")
        sc_done = m.sem("r_sc_done")
        with nc.Block() as block:
            @block.vector
            def _(dve):
                for ready in loads:
                    dve.wait_ge(*ready)
                dve.tensor_copy(posf[:, :], pos[:, :]).then_inc(step, 1)
                dve.wait_ge(step, 1)
                dve.tensor_tensor(ang[:, :, :], posf[:, :].unsqueeze(2).to_broadcast([P, NT, ROT]),
                                  const[:, C_FREQ:C_FREQ + ROT].unsqueeze(1).to_broadcast([P, NT, ROT]),
                                  ALU.mult).then_inc(step, 1)
                done = 2
                for k in range(2):
                    dve.wait_ge(step, done)
                    dve.tensor_scalar(turns[:, :, :], ang[:, :, :], 1.0 / TWO_PI, 0.25 * k, ALU.mult,
                                      ALU.add).then_inc(step, 1)
                    dve.wait_ge(step, done + 1)
                    dve.tensor_scalar(turns[:, :, :], turns[:, :, :], ROUND, None, ALU.add).then_inc(step, 1)
                    dve.wait_ge(step, done + 2)
                    dve.tensor_scalar(turns[:, :, :], turns[:, :, :], ROUND, None, ALU.subtract).then_inc(step, 1)
                    dve.wait_ge(step, done + 3)
                    src = ang
                    for i, part in enumerate((PI_HIGH, PI_MID, PI_LOW)):
                        dve.scalar_tensor_tensor(out=rem[:, :, :], in0=turns[:, :, :], scalar=-part,
                                                 in1=src[:, :, :], op0=ALU.mult, op1=ALU.add).then_inc(step, 1)
                        dve.wait_ge(step, done + 4 + i)
                        src = rem
                    dve.tensor_scalar(rem[:, :, :], rem[:, :, :], 0.25 * k * TWO_PI, PI_CLAMP, ALU.add,
                                      ALU.min).then_inc(step, 1)
                    dve.wait_ge(step, done + 7)
                    dve.tensor_scalar(sc[:, k, :, :], rem[:, :, :], -PI_CLAMP, None,
                                      ALU.max).then_inc(arg_ready, 1)
                    done += 7
                dve.wait_ge(sc_done, 1)
                for cosw, sinw, w, t0, n in ((kcos, ksin, kw, 0, NT), (qcos, qsin, qw, TILES, TILES)):
                    for half in range(2):
                        here = slice(half * ROT, (half + 1) * ROT)
                        other = slice((1 - half) * ROT, (2 - half) * ROT)
                        dve.tensor_tensor(cosw[:, :, here], sc[:, 1, t0:t0 + n, :],
                                          w[:, here].unsqueeze(1).to_broadcast([P, n, ROT]), ALU.mult)
                        if half == 0:
                            dve.scalar_tensor_tensor(out=sinw[:, :, here], in0=sc[:, 0, t0:t0 + n, :], scalar=-1.0,
                                                     in1=w[:, other].unsqueeze(1).to_broadcast([P, n, ROT]),
                                                     op0=ALU.mult, op1=ALU.mult)
                        else:
                            dve.tensor_tensor(sinw[:, :, here], sc[:, 0, t0:t0 + n, :],
                                              w[:, other].unsqueeze(1).to_broadcast([P, n, ROT]), ALU.mult)

            @block.scalar
            def _(act):
                act.wait_ge(arg_ready, 2)
                act.activation(sc[:, :, :, :], sc[:, :, :, :], ACT.Sin).then_inc(sc_done, 1)


def gqa_attention(nc, t, X, lnT, wq, wk, wv, wo, kcos, ksin, qcos, qsin, gains, const, ident, loads):
    ROPES = KT_TILES + TPB * KV_HEADS
    UNITS = TPB * HEADS
    GROUPS = UNITS // REP
    with ExitStack() as st:
        m = Memory(nc, st)
        kvT = m.sb("c_kvT", [P, DC, KEYS])
        raw = m.sb("c_raw", [P, 2, 512])
        sq = m.sb("c_sq", [P, 512])
        t1 = m.sb("c_t1", [P, 512])
        t2 = m.sb("c_t2", [P, 512])
        y = m.sb("c_y", [P, 2, 512])
        ss = m.sb("c_ss", [P, ROPES, REP])
        ve = m.sb("c_ve", [P, ROPES, REP])
        rn = m.sb("c_rn", [P, ROPES, REP])
        scale = m.sb("c_scale", [P, UNITS])
        KT = m.sb("c_KT", [P, KV_HEADS, KEYS])
        qT = m.sb("c_qT", [P, TPB, HEADS, P])
        V = m.sb("c_V", [P, KT_TILES, KV_HEADS * HD])
        probs = m.sb("c_probs", [P, 3, KEYS])
        PT = m.sb("c_PT", [P, 2, KT_TILES, REP, P])
        attnT = m.sb("c_attnT", [P, HEADS, P])
        nmax = m.sb("c_nmax", [P, UNITS])
        bias = m.sb("c_bias", [P, UNITS])
        total = m.sb("c_total", [P, UNITS])
        inv = m.sb("c_inv", [P, UNITS])
        sps = m.ps("c_sps", 3)
        tps = m.ps("c_tps", 2)
        ops = m.ps("c_ops", 1)
        wps = m.ps("c_wps", 1)
        names = ("ctx_in ln_copied proj_done raw_done squared summed products roped ve_done rn_done scaled "
                 "turned stored v_done v_stored scale_done s_done max_done bias_done exp_done inv_done normed "
                 "pt_turned pt_even pt_odd pv_done at_stored wo_done x_done k_stored").split()
        (ctx_in, ln_copied, proj_done, raw_done, squared, summed, products, roped, ve_done, rn_done, scaled,
         turned, stored, v_done, v_stored, scale_done, s_done, max_done, bias_done, exp_done, inv_done, normed,
         pt_turned, pt_even, pt_odd, pv_done, at_stored, wo_done, x_done, k_stored) = (m.sem("c_" + n) for n in names)
        with nc.Block() as block:
            @block.sync
            def _(sp):
                for b in range(B):
                    wait_for(sp, proj_done, ROPES * b)
                    wait_for(sp, v_done, KT_TILES * b)
                    sp.dma_start(kvT[:, :, 0:S_LEN],
                                 t["ctxT"].rearrange("(c p) s -> p c s", p=P)[:, :, bass.ds(b * S_LEN, S_LEN)]
                                 ).then_inc(ctx_in, 16)

            @block.gpsimd
            def _(pool):
                for b in range(B):
                    wait_for(pool, proj_done, ROPES * b)
                    wait_for(pool, v_done, KT_TILES * b)
                    pool.tensor_scalar(kvT[:, :, S_LEN:KEYS], lnT[:, :, bass.ds(b * S_LEN, S_LEN)], 1.0, 1.0,
                                       ALU.mult, ALU.mult).then_inc(ln_copied, 1)
                    for r in range(ROPES):
                        pool.wait_ge(summed, ROPES * b + r + 1)
                        pool.tensor_scalar(ve[:, r, :], ss[:, r, :], 1.0 / HD, EPS, ALU.mult,
                                           ALU.add).then_inc(ve_done, 1)
                        pool.wait_ge(ve_done, ROPES * b + r + 1)
                        pool.tensor_tensor(rn[:, r, :], ve[:, r, :], const[:, C_NEGHALF:C_NEGHALF + REP],
                                           ALU.pow).then_inc(rn_done, 1)
                        if r < KT_TILES:
                            pool.wait_ge(rn_done, ROPES * b + r + 1)
                            pool.wait_ge(roped, ROPES * b + r + 1)
                            for k in range(KV_HEADS):
                                last = pool.tensor_scalar(y[:, r % 2, k * HD:(k + 1) * HD],
                                                          y[:, r % 2, k * HD:(k + 1) * HD],
                                                          rn[:, r, k:k + 1], 1.0, ALU.mult, ALU.mult)
                            last.then_inc(scaled, 1)
                    pool.wait_ge(rn_done, ROPES * (b + 1))
                    pool.tensor_scalar(scale[:, :], rn[:, KT_TILES:ROPES, :].rearrange("p r k -> p (r k)"),
                                       float(HD) ** -0.5, 1.0, ALU.mult, ALU.mult).then_inc(scale_done, 1)
                    for i in range(UNITS):
                        pool.wait_ge(inv_done, UNITS * b + i + 1)
                        pool.tensor_scalar(probs[:, i % 3, :], probs[:, i % 3, :], inv[:, i:i + 1], 1.0, ALU.mult,
                                           ALU.mult).then_inc(normed, 1)

            @block.scalar
            def _(act):

                def batch(b):
                    def raw_copy(r):
                        act.wait_ge(proj_done, ROPES * b + r + 1)
                        wait_for(act, roped, ROPES * b + max(r - 1, 0))
                        act.activation(raw[:, r % 2, :], sps[:, r % 3, :], ACT.Copy).then_inc(raw_done, 1)
                        act.wait_ge(raw_done, ROPES * b + r + 1)
                        wait_for(act, summed, ROPES * b + r)
                        act.activation(sq[:, :], raw[:, r % 2, :], ACT.Square).then_inc(squared, 1)

                    def v_copy(k):
                        act.wait_ge(v_done, KT_TILES * b + k + 1)
                        act.activation(V[:, k, :], ops[:, 0, :], ACT.Copy).then_inc(v_stored, 1)

                    def turned_copy(r):
                        act.wait_ge(turned, ROPES * b + r + 1)
                        src = tps[:, r % 2, :].rearrange("p (k s) -> p k s", k=REP)
                        if r < KT_TILES:
                            act.activation(KT[:, :, r * P:(r + 1) * P], src, ACT.Copy).then_inc(stored, 1)
                        else:
                            qt, n = divmod(r - KT_TILES, KV_HEADS)
                            act.activation(qT[:, qt, n * REP:(n + 1) * REP, :], src, ACT.Copy).then_inc(stored, 1)

                    def exponential(i):
                        act.wait_ge(bias_done, UNITS * b + i + 1)
                        wait_for(act, pt_turned, UNITS * b + max(i - 2, 0))
                        act.activation(probs[:, i % 3, :], sps[:, i % 3, :], ACT.Exp, bias=bias[:, i:i + 1],
                                       scale=scale[:, i:i + 1], accum_out=total[:, i:i + 1]).then_inc(exp_done, 1)

                    def pt_copy(i):
                        act.wait_ge(pt_turned, UNITS * b + i + 1)
                        grp = i // REP
                        act.activation(PT[:, grp % 2, :, i % REP, :],
                                       tps[:, i % 2, :].rearrange("p (k s) -> p k s", k=KT_TILES),
                                       ACT.Copy).then_inc(pt_odd, 1)

                    def attn_copy(grp):
                        act.wait_ge(pv_done, GROUPS * b + grp + 1)
                        kv = grp % KV_HEADS
                        act.activation(attnT[:, kv * REP:(kv + 1) * REP, :].rearrange("p h s -> p (h s)"),
                                       ops[:, 0, :], ACT.Copy).then_inc(at_stored, 1)

                    for r in range(ROPES + 2):
                        if r < ROPES:
                            raw_copy(r)
                        if r < KT_TILES:
                            v_copy(r)
                        if r >= 2:
                            turned_copy(r - 2)
                    act.wait_ge(scale_done, b + 1)
                    for i in range(UNITS + 5):
                        if i < UNITS:
                            exponential(i)
                        if 2 <= i < UNITS + 2 and (i - 2) % 2 == 1:
                            pt_copy(i - 2)
                        if i >= 6 and (i - 6) % REP == 0:
                            attn_copy((i - 6) // REP)

                first_then_loop(act, B, batch)

            @block.vector
            def _(dve):

                def batch(b):
                    def rope(r):
                        if r < KT_TILES:
                            tile = (b * TPB + r) if r < TPB else (TILES + b * TPB + r - TPB)
                            cosw, sinw = kcos[:, tile, :], ksin[:, tile, :]
                        else:
                            tile = b * TPB + (r - KT_TILES) // KV_HEADS
                            cosw, sinw = qcos[:, tile, :], qsin[:, tile, :]
                        src = raw[:, r % 2, :].rearrange("p (k d) -> p k d", k=REP)
                        dve.wait_ge(squared, ROPES * b + r + 1)
                        dve.tensor_reduce(ss[:, r, :], sq[:, :].rearrange("p (k d) -> p k d", k=REP), AX.X,
                                          ALU.add).then_inc(summed, 1)
                        dve.wait_ge(raw_done, ROPES * b + r + 1)
                        wait_for(dve, roped, ROPES * b + r)
                        dve.tensor_tensor(t1[:, :].rearrange("p (k d) -> p k d", k=REP), src,
                                          cosw.unsqueeze(1).to_broadcast([P, REP, HD]),
                                          ALU.mult).then_inc(products, 1)
                        for half in range(2):
                            here = slice(half * ROT, (half + 1) * ROT)
                            other = slice((1 - half) * ROT, (2 - half) * ROT)
                            dve.tensor_tensor(t2[:, :].rearrange("p (k d) -> p k d", k=REP)[:, :, here],
                                              src[:, :, other],
                                              sinw[:, here].unsqueeze(1).to_broadcast([P, REP, ROT]),
                                              ALU.mult).then_inc(products, 1)
                        dve.wait_ge(products, 3 * (ROPES * b + r + 1))
                        wait_for(dve, turned, ROPES * b + max(r - 1, 0))
                        dve.tensor_tensor(y[:, r % 2, :], t1[:, :], t2[:, :], ALU.add).then_inc(roped, 1)

                    def maximum(i):
                        dve.wait_ge(s_done, UNITS * b + i + 1)
                        dve.tensor_reduce(nmax[:, i:i + 1], sps[:, i % 3, :], AX.X, ALU.max,
                                          negate=True).then_inc(max_done, 1)
                        dve.wait_ge(max_done, UNITS * b + i + 1)
                        dve.tensor_tensor(bias[:, i:i + 1], nmax[:, i:i + 1], scale[:, i:i + 1],
                                          ALU.mult).then_inc(bias_done, 1)

                    def inverse(i):
                        dve.wait_ge(exp_done, UNITS * b + i + 1)
                        dve.reciprocal(inv[:, i:i + 1], total[:, i:i + 1]).then_inc(inv_done, 1)

                    def pt_copy(i):
                        dve.wait_ge(pt_turned, UNITS * b + i + 1)
                        grp = i // REP
                        dve.tensor_copy(PT[:, grp % 2, :, i % REP, :],
                                        tps[:, i % 2, :].rearrange("p (k s) -> p k s", k=KT_TILES)
                                        ).then_inc(pt_even, 1)

                    def add_x(qt):
                        dve.wait_ge(wo_done, TPB * b + qt + 1)
                        dve.scalar_tensor_tensor(out=X[:, b * TPB + qt, :], in0=wps[:, 0, 0:D],
                                                 scalar=gains[:, 1:2], in1=X[:, b * TPB + qt, :],
                                                 op0=ALU.mult, op1=ALU.add).then_inc(x_done, 1)

                    for r in range(ROPES):
                        rope(r)
                    dve.wait_ge(scale_done, b + 1)
                    for i in range(UNITS + 3):
                        if i < UNITS:
                            maximum(i)
                        if 1 <= i <= UNITS:
                            inverse(i - 1)
                        if 2 <= i < UNITS + 2 and (i - 2) % 2 == 0:
                            pt_copy(i - 2)
                        if i == HEADS + 7:
                            add_x(0)
                    add_x(1)

                first_then_loop(dve, B, batch)

            @block.tensor
            def _(pe):
                for ready in loads:
                    pe.wait_ge(*ready)

                def batch(b):
                    def project(r):
                        wait_for(pe, exp_done, UNITS * b)
                        wait_for(pe, raw_done, ROPES * b + max(r - 2, 0))
                        for c in range(DC):
                            if r < KT_TILES:
                                tok, w = r, wk[:, c, :]
                            else:
                                qt, n = divmod(r - KT_TILES, KV_HEADS)
                                tok, w = TPB + qt, wq[:, c, n * 512:(n + 1) * 512]
                            last = pe.matmul(sps[:, r % 3, :], kvT[:, c, tok * P:(tok + 1) * P], w,
                                             start=(c == 0), stop=(c == DC - 1))
                        last.then_inc(proj_done, 1)

                    def project_v(k):
                        wait_for(pe, v_stored, KT_TILES * b + k)
                        for c in range(DC):
                            last = pe.matmul(ops[:, 0, :], kvT[:, c, k * P:(k + 1) * P], wv[:, c, :],
                                             start=(c == 0), stop=(c == DC - 1))
                        last.then_inc(v_done, 1)

                    def turn(r):
                        if r < KT_TILES:
                            pe.wait_ge(scaled, KT_TILES * b + r + 1)
                        else:
                            pe.wait_ge(roped, ROPES * b + r + 1)
                        wait_for(pe, stored, ROPES * b + max(r - 1, 0))
                        for k in range(REP):
                            last = pe.transpose(tps[:, r % 2, k * P:(k + 1) * P], y[:, r % 2, k * HD:(k + 1) * HD],
                                                ident)
                        last.then_inc(turned, 1)

                    def scores(i):
                        qt, hd = divmod(i, HEADS)
                        if i < 3:
                            pe.wait_ge(stored, ROPES * (b + 1))
                        wait_for(pe, exp_done, UNITS * b + max(i - 2, 0))
                        pe.matmul(sps[:, i % 3, :], qT[:, qt, hd, :], KT[:, hd // REP, :], start=True,
                                  stop=True).then_inc(s_done, 1)

                    def turn_probs(i):
                        pe.wait_ge(normed, UNITS * b + i + 1)
                        done = pt_even if i % 2 == 0 else pt_odd
                        wait_for(pe, done, UNITS // 2 * b + i // 2)
                        for k in range(KT_TILES):
                            last = pe.transpose(tps[:, i % 2, k * P:(k + 1) * P],
                                                probs[:, i % 3, k * P:(k + 1) * P], ident)
                        last.then_inc(pt_turned, 1)

                    def values(grp):
                        pe.wait_ge(pt_even, UNITS // 2 * b + 2 * grp + 2)
                        pe.wait_ge(pt_odd, UNITS // 2 * b + 2 * grp + 2)
                        wait_for(pe, at_stored, GROUPS * b + grp)
                        kv = grp % KV_HEADS
                        for k in range(KT_TILES):
                            last = pe.matmul(ops[:, 0, :], V[:, k, kv * HD:(kv + 1) * HD],
                                             PT[:, grp % 2, k, :, :].rearrange("p h s -> p (h s)"),
                                             start=(k == 0), stop=(k == KT_TILES - 1))
                        last.then_inc(pv_done, 1)

                    def output(qt):
                        pe.wait_ge(at_stored, GROUPS * b + (qt + 1) * KV_HEADS)
                        wait_for(pe, x_done, TPB * b + qt)
                        for h in range(HEADS):
                            last = pe.matmul(wps[:, 0, 0:D], attnT[:, h, :], wo[:, h, :], start=(h == 0),
                                             stop=(h == HEADS - 1))
                        last.then_inc(wo_done, 1)

                    pe.wait_ge(ctx_in, 16 * b + 16)
                    pe.wait_ge(ln_copied, b + 1)
                    for r in range(ROPES + 2):
                        if r < ROPES:
                            project(r)
                        if r < KT_TILES:
                            project_v(r)
                        if r >= 2:
                            turn(r - 2)
                    pe.wait_ge(v_stored, KT_TILES * (b + 1))
                    for i in range(UNITS + 4):
                        if i < UNITS:
                            scores(i)
                        if i >= 6 and (i - 6) % REP == 0:
                            values((i - 6) // REP)
                        if 2 <= i < UNITS + 2:
                            turn_probs(i - 2)
                        if i == HEADS + 4:
                            output(0)
                    output(1)

                first_then_loop(pe, B, batch)


def route(nc, lnT, ln, router, slot, expert, sorted_x, const, loads, zeroed):
    with ExitStack() as st:
        m = Memory(nc, st)
        logits = m.sb("e_logits", [P, TILES, EXPERTS])
        best = m.sb("e_best", [P, TILES])
        first = m.sb("e_first", [P, TILES])
        cand = m.sb("e_cand", [P, TILES, EXPERTS])
        hot = m.sb("e_hot", [P, TILES, EXPERTS])
        count = m.sb("e_count", [P, TILES, EXPERTS])
        before = m.sb("e_before", [P, TILES + 1, EXPERTS])
        tiles = m.sb("e_tiles", [P, EXPERTS])
        ends = m.sb("e_ends", [P, EXPERTS])
        base = m.sb("e_base", [P, EXPERTS])
        where = m.sb("e_where", [P, TILES, EXPERTS])
        slotf = m.sb("e_slotf", [P, TILES])
        over = m.sb("e_over", [1, SLOT_TILES, EXPERTS])
        expf = m.sb("e_expf", [1, SLOT_TILES])
        lps = m.ps("e_lps", 1)
        rps = m.ps("e_rps", 1)
        cps = m.ps("e_cps", 1)
        logits_done = m.sem("e_logits_done")
        step = m.sem("e_step")
        hot_done = m.sem("e_hot_done")
        ranked = m.sem("e_ranked")
        slots_done = m.sem("e_slots_done")
        scattered = m.sem("e_scattered")
        ids = const[:, C_EXP:C_EXP + EXPERTS]
        all_tiles = [P, TILES, EXPERTS]
        with nc.Block() as block:
            @block.tensor
            def _(pe):
                for ready in loads:
                    pe.wait_ge(*ready)
                for t in range(TILES):
                    for c in range(DC):
                        last = pe.matmul(lps[:, 0, t * EXPERTS:(t + 1) * EXPERTS], lnT[:, c, t * P:(t + 1) * P],
                                         router[:, c, :], start=(c == 0), stop=(c == DC - 1))
                last.then_inc(logits_done, 1)
                pe.wait_ge(hot_done, 1)
                hot2 = hot[:, :, :].rearrange("p t e -> p (t e)")
                pe.matmul(rps[:, 0, 0:TILES * EXPERTS], const[:, C_TRI:C_TRI + P], hot2, start=True, stop=True)
                pe.matmul(cps[:, 0, 0:TILES * EXPERTS], const[:, C_ONES:C_ONES + P], hot2, start=True,
                          stop=True).then_inc(ranked, 1)

            @block.vector
            def _(dve):
                n = 0

                def after(ins):
                    nonlocal n
                    ins.then_inc(step, 1)
                    n += 1
                    dve.wait_ge(step, n)

                dve.wait_ge(logits_done, 1)
                after(dve.tensor_copy(logits[:, :, :].rearrange("p t e -> p (t e)"),
                                      lps[:, 0, 0:TILES * EXPERTS]))
                after(dve.tensor_reduce(best[:, :], logits[:, :, :], AX.X, ALU.max))
                after(dve.tensor_tensor(cand[:, :, :], logits[:, :, :], best[:, :].unsqueeze(2).to_broadcast(all_tiles),
                                        ALU.is_equal))
                after(dve.tensor_scalar(base[:, :], ids, float(-EXPERTS), None, ALU.add))
                after(dve.tensor_tensor(cand[:, :, :], cand[:, :, :], base[:, :].unsqueeze(1).to_broadcast(all_tiles),
                                        ALU.mult))
                after(dve.tensor_reduce(first[:, :], cand[:, :, :], AX.X, ALU.min))
                dve.tensor_tensor(hot[:, :, :], first[:, :].unsqueeze(2).to_broadcast(all_tiles),
                                  base[:, :].unsqueeze(1).to_broadcast(all_tiles),
                                  ALU.is_equal).then_inc(hot_done, 1)
                dve.wait_ge(ranked, 1)
                after(dve.tensor_copy(count[:, :, :].rearrange("p t e -> p (t e)"),
                                      cps[:, 0, 0:TILES * EXPERTS]))
                after(dve.memset(before[:, 0, :], 0.0))
                for t in range(TILES):
                    after(dve.tensor_tensor(before[:, t + 1, :], before[:, t, :], count[:, t, :], ALU.add))
                after(dve.tensor_scalar(tiles[:, :], before[:, TILES, :], 1.0 / P, 0.5 - 1.0 / (2 * P), ALU.mult,
                                        ALU.add))
                after(dve.tensor_scalar(tiles[:, :], tiles[:, :], ROUND, None, ALU.add))
                after(dve.tensor_scalar(tiles[:, :], tiles[:, :], ROUND, None, ALU.subtract))
                after(dve.tensor_tensor_scan(ends[:, :], const[:, C_ONES:C_ONES + EXPERTS], tiles[:, :], 0.0,
                                             ALU.mult, ALU.add))
                after(dve.tensor_tensor(base[:, :], ends[:, :], tiles[:, :], ALU.subtract))
                after(dve.tensor_scalar(base[:, :], base[:, :], float(P), None, ALU.mult))
                after(dve.tensor_tensor(where[:, :, :].rearrange("p t e -> p (t e)"), rps[:, 0, 0:TILES * EXPERTS],
                                        before[:, 0:TILES, :].rearrange("p t e -> p (t e)"), ALU.add))
                after(dve.tensor_tensor(where[:, :, :], where[:, :, :], base[:, :].unsqueeze(1).to_broadcast(all_tiles),
                                        ALU.add))
                after(dve.tensor_tensor(where[:, :, :], where[:, :, :], hot[:, :, :], ALU.mult))
                after(dve.tensor_reduce(slotf[:, :], where[:, :, :], AX.X, ALU.add))
                dve.tensor_copy(slot[:, :], slotf[:, :]).then_inc(slots_done, 1)
                shape = [1, SLOT_TILES, EXPERTS]
                after(dve.tensor_tensor(over[:, :, :], ends[0:1, :].unsqueeze(1).to_broadcast(shape),
                                        const[0:1, C_TILE:C_TILE + SLOT_TILES].unsqueeze(2).to_broadcast(shape),
                                        ALU.is_le))
                after(dve.tensor_reduce(expf[:, :], over[:, :, :], AX.X, ALU.add))
                after(dve.tensor_scalar(expert[:, :], expf[:, :], float(EXPERTS - 1), None, ALU.min))

            @block.gpsimd
            def _(pool):
                pool.wait_ge(slots_done, 1)
                pool.wait_ge(*zeroed)
                for t in range(TILES):
                    pool.indirect_dma_start(sorted_x, bass.IndirectOffsetOnAxis(slot[:, t:t + 1], 0),
                                            ln[:, t, :], None).then_inc(scattered, 16)
                pool.wait_ge(scattered, 16 * TILES)


def experts(nc, X, gate, up, down, expert, slot, sorted_x, sorted_y, gains, ident, out, loads):
    LAST = SLOT_TILES - 1
    assert LAST % 2 == 0
    with ExitStack() as st:
        m = Memory(nc, st)
        xs = m.sb("g_xs", [P, 2, D])
        xT = m.sb("g_xT", [P, 2, DC, P])
        act_g = m.sb("g_act", [P, 2, INNER])
        h = m.sb("g_h", [P, 2, INNER])
        hT = m.sb("g_hT", [P, 2, IC, P])
        ys = m.sb("g_ys", [P, 2, D])
        yg = m.sb("g_yg", [P, TILES, D])
        xps = m.ps("g_xps", 1)
        gps = m.ps("g_gps", 2)
        ups = m.ps("g_ups", 2)
        hps = m.ps("g_hps", 1)
        yps = m.ps("g_yps", 2)
        xs_in = [m.sem(f"g_xs_in{k}") for k in range(2)]
        x_turned = m.sem("g_x_turned")
        x_stored = m.sem("g_x_stored")
        g_done = m.sem("g_g_done")
        u_done = m.sem("g_u_done")
        silu_done = m.sem("g_silu_done")
        h_done = m.sem("g_h_done")
        h_turned = m.sem("g_h_turned")
        h_stored = m.sem("g_h_stored")
        y_done = m.sem("g_y_done")
        y_copied = m.sem("g_y_copied")
        y_out = [m.sem(f"g_y_out{k}") for k in range(2)]
        gathered = m.sem("g_gathered")
        x_done = m.sem("g_x_done")
        stored = m.sem("g_stored")
        with nc.Block() as block:
            @block.sync
            def _(sp):
                def load(i, par, rnd):
                    if rnd is not None:
                        wait_for(sp, x_turned, i - 1)
                    sp.dma_start(xs[:, par, :], sorted_x[bass.ds(i * P, P), :]).then_inc(xs_in[par], 16)

                def store(i, par):
                    sp.wait_ge(y_copied, i + 1)
                    sp.dma_start(sorted_y[bass.ds(i * P, P), :], ys[:, par, :]).then_inc(y_out[par], 16)

                load(0, 0, None)
                load(1, 1, None)
                for j in range(LAST // 2 - 1):
                    for par in range(2):
                        load(2 * j + par + 2, par, j)
                        store(2 * j + par, par)
                load(LAST, 0, 0)
                store(LAST - 2, 0)
                store(LAST - 1, 1)
                store(LAST, 0)
                for par in range(2):
                    sp.wait_ge(y_out[par], 16 * ((SLOT_TILES + 1 - par) // 2))
                sp.sem_inc(y_copied, 1)
                for t in range(TILES):
                    sp.wait_ge(x_done, t + 1)
                    sp.dma_start(out[t * P:(t + 1) * P, :], X[:, t, :]).then_inc(stored, 16)
                sp.wait_ge(stored, 16 * TILES)

            @block.tensor
            def _(pe):
                for ready in loads:
                    pe.wait_ge(*ready)

                def turn_x(i, par, rnd):
                    pe.wait_ge(xs_in[par], 16 * rnd + 16)
                    wait_for(pe, x_stored, i)
                    for c in range(DC):
                        last = pe.transpose(xps[:, 0, c * P:(c + 1) * P], xs[:, par, c * P:(c + 1) * P], ident)
                    last.then_inc(x_turned, 1)

                def up_proj(i, par):
                    e = pe.value_load(expert[0:1, bass.ds(i, 1)], min_val=0, max_val=EXPERTS - 1)
                    pe.wait_ge(x_stored, i + 1)
                    if par is not None:
                        pass
                    for c in range(DC):
                        last = pe.matmul(gps[:, par, :], xT[:, par, c, :], gate[:, c, bass.ds(e * INNER, INNER)],
                                         start=(c == 0), stop=(c == DC - 1))
                    last.then_inc(g_done, 1)
                    for c in range(DC):
                        last = pe.matmul(ups[:, par, :], xT[:, par, c, :], up[:, c, bass.ds(e * INNER, INNER)],
                                         start=(c == 0), stop=(c == DC - 1))
                    last.then_inc(u_done, 1)

                def down_proj(i, par):
                    e = pe.value_load(expert[0:1, bass.ds(i, 1)], min_val=0, max_val=EXPERTS - 1)
                    pe.wait_ge(h_done, i + 1)
                    wait_for(pe, h_stored, i)
                    for c in range(IC):
                        last = pe.transpose(hps[:, 0, c * P:(c + 1) * P], h[:, par, c * P:(c + 1) * P], ident)
                    last.then_inc(h_turned, 1)
                    pe.wait_ge(h_stored, i + 1)
                    wait_for(pe, y_copied, i)
                    for c in range(IC):
                        last = pe.matmul(yps[:, par, 0:D], hT[:, par, c, :], down[:, c, bass.ds(e * D, D)],
                                         start=(c == 0), stop=(c == IC - 1))
                    last.then_inc(y_done, 1)

                turn_x(0, 0, 0)
                up_proj(0, 0)

                def pair(j):
                    for par in range(2):
                        i = 2 * j + par
                        turn_x(i + 1, 1 - par, j + par)
                        up_proj(i + 1, 1 - par)
                        down_proj(i, par)

                first_then_loop(pe, LAST // 2, pair)
                down_proj(LAST, 0)

            @block.scalar
            def _(act):
                def step(i, par):
                    act.wait_ge(x_turned, i + 1)
                    act.activation(xT[:, par, :, :], xps[:, 0, 0:D].rearrange("p (c s) -> p c s", c=DC),
                                   ACT.Copy).then_inc(x_stored, 1)
                    wait_for(act, h_done, i)
                    act.wait_ge(g_done, i + 1)
                    act.activation(act_g[:, par, :], gps[:, par, :], ACT.Silu).then_inc(silu_done, 1)


                def pair(j):
                    for par in range(2):
                        step(2 * j + par, par)

                first_then_loop(act, LAST // 2, pair)
                step(LAST, 0)

            @block.vector
            def _(dve):
                def finish(i, par):
                    dve.wait_ge(h_turned, i + 1)
                    dve.tensor_copy(hT[:, par, :, :].rearrange("p c s -> p (c s)"), hps[:, 0, :]).then_inc(h_stored, 1)
                    dve.wait_ge(y_done, i + 1)
                    dve.tensor_copy(ys[:, par, :], yps[:, par, 0:D]).then_inc(y_copied, 1)

                def product(i, par):
                    dve.wait_ge(silu_done, i + 1)
                    dve.wait_ge(u_done, i + 1)
                    dve.tensor_tensor(h[:, par, :], act_g[:, par, :], ups[:, par, :], ALU.mult).then_inc(h_done, 1)

                product(0, 0)
                product(1, 1)
                finish(0, 0)
                product(2, 0)
                finish(1, 1)
                with dve.Fori(1, LAST // 2) as j:
                    for par in range(2):
                        product(2 * j + par + 1, 1 - par)
                        wait_for(dve, y_out[par], 16 * j)
                        finish(2 * j + par, par)
                dve.wait_ge(y_out[0], 16 * (LAST // 2))
                finish(LAST, 0)
                for t in range(TILES):
                    dve.wait_ge(gathered, 16 * TILES)
                    dve.scalar_tensor_tensor(out=X[:, t, :], in0=yg[:, t, :], scalar=gains[:, 3:4], in1=X[:, t, :],
                                             op0=ALU.mult, op1=ALU.add).then_inc(x_done, 1)

            @block.gpsimd
            def _(pool):
                pool.wait_ge(y_copied, SLOT_TILES + 1)
                for t in range(TILES):
                    pool.indirect_dma_start(yg[:, t, :], None, sorted_y,
                                            bass.IndirectOffsetOnAxis(slot[:, t:t + 1], 0)).then_inc(gathered, 16)


def flamingo(nc, t, out):
    with ExitStack() as stack:
        mem = Memory(nc, stack)
        X = mem.sb("X", [P, TILES, D])
        const = mem.sb("const", [P, C_WIDE])
        gains = mem.sb("gains", [P, 4])
        ident = const[:, C_IDENT:C_IDENT + P]
        x_in = mem.sem("x_in")
        const_in = mem.sem("const_in")
        gains_in = mem.sem("gains_in")
        sorted_x = nc.dram_tensor("sorted_x", (SLOTS, D), F32, kind="Internal").ap()
        sorted_y = nc.dram_tensor("sorted_y", (SLOTS, D), F32, kind="Internal").ap()

        aw = stack.enter_context(ExitStack())
        wq = Memory(nc, aw).sb("wq", [P, DC, HEADS * HD])
        wk = Memory(nc, aw).sb("wk", [P, DC, KV_HEADS * HD])
        wv = Memory(nc, aw).sb("wv", [P, DC, KV_HEADS * HD])
        wo = Memory(nc, aw).sb("wo", [P, HEADS, D])
        wq_in = mem.sem("wq_in")
        wk_in = mem.sem("wk_in")
        wv_in = mem.sem("wv_in")
        wo_in = mem.sem("wo_in")
        fw = stack.enter_context(ExitStack())
        w1 = Memory(nc, fw).sb("w1", [P, DC, FF])
        w2 = Memory(nc, fw).sb("w2", [P, FC, D])
        w1_in = mem.sem("w1_in")
        w2_in = mem.sem("w2_in")

        with ExitStack() as lstm:
            m = Memory(nc, lstm)
            ctx = m.sb("ctx", [P, TILES, D])
            ctxT = m.sb("ctxT", [P, DC, TOK])
            lnT = m.sb("lnT0", [P, DC, TOK])
            gate_w = m.sb("gate_w", [P, 3 * DC, 32])
            gate_b = m.sb("gate_b", [32, 1])
            sel = m.sb("sel", [32, M_HEADS * P])
            selr = m.sb("selr", [32, M_HEADS * P], F32R)
            scale_row = m.sb("scale_row", [P, D])
            cols = m.sb("cols", [P, B, 4, 32])
            Gr = m.sb("Gr", [32, TOK], F32R)
            Mr = m.sb("Mr", [32, TOK], F32R)
            ctx_in = m.sem("ctx_in")
            ctxT_in = m.sem("ctxT_in")
            gate_in = m.sem("gate_in")
            bias_in = m.sem("bias_in")
            sel_in = m.sem("sel_in")
            scale_in = m.sem("scale_in")
            tanh_done = m.sem("tanh_done")
            with nc.Block() as block:
                @block.sync
                def _(sp):
                    sp.dma_start(X[:, :, :], t["x"].rearrange("(t p) d -> p t d", p=P)).then_inc(x_in, 16)
                    sp.dma_start(const[:, :], t["const"]).then_inc(const_in, 16)
                    sp.dma_start(ctxT[:, :, :], t["ctxT"].rearrange("(c p) s -> p c s", p=P)).then_inc(ctxT_in, 16)
                    sp.dma_start(gate_w[:, :, :], t["gate_w"].rearrange("(c p) n -> p c n", p=P)).then_inc(gate_in, 16)
                    sp.dma_start(gate_b[:, :], t["gate_b"]).then_inc(bias_in, 16)
                    sp.dma_start(sel[:, :], t["sel"]).then_inc(sel_in, 16)
                    sp.dma_start(ctx[:, :, :], t["ctx"].rearrange("(t p) d -> p t d", p=P)).then_inc(ctx_in, 16)
                    sp.dma_start(w1[:, :, :], t["w1T"].rearrange("(c p) f -> p c f", p=P)).then_inc(w1_in, 16)
                    sp.dma_start(w2[:, :, :], t["w2T"].rearrange("(c p) d -> p c d", p=P)).then_inc(w2_in, 16)
                    sp.dma_start(wk[:, :, :], t["wkT"].rearrange("(c p) n -> p c n", p=P)).then_inc(wk_in, 16)
                    sp.dma_start(wv[:, :, :], t["wvT"].rearrange("(c p) n -> p c n", p=P)).then_inc(wv_in, 16)
                    sp.dma_start(wq[:, :, :], t["wqT"].rearrange("(c p) n -> p c n", p=P)).then_inc(wq_in, 16)
                    sp.dma_start(wo[:, :, :], t["woT"].rearrange("(h p) n -> p h n", p=P)).then_inc(wo_in, 16)

                @block.scalar
                def _(act):
                    act.dma_start(gains[:, :], t["gains"].partition_broadcast(P)).then_inc(gains_in, 16)
                    act.dma_start(scale_row[:, :], t["ln_scale"].partition_broadcast(P)).then_inc(scale_in, 16)
                    act.wait_ge(gains_in, 16)
                    act.activation(gains[:, :], gains[:, :], ACT.Tanh).then_inc(tanh_done, 1)

                @block.vector
                def _(dve):
                    dve.wait_ge(scale_in, 16)
                    dve.wait_ge(tanh_done, 1)
                    dve.tensor_scalar(scale_row[:, :], scale_row[:, :], gains[:, 0:1], None, ALU.mult)
            layernorm_transposed(nc, "l0", X, lnT, ident, const, (const_in, 16), (x_in, 16))
            mlstm_rows(nc, m, lnT, ctxT, gate_w, gate_b, sel, const, cols, Gr, Mr, selr, ident,
                       [(ctxT_in, 16), (gate_in, 16), (bias_in, 16), (sel_in, 16), (ctx_in, 16), (const_in, 16)])
            mlstm_heads(nc, m, X, lnT, ctx, ctxT, cols, Gr, Mr, selr, scale_row, const)

        with ExitStack() as ffn:
            m = Memory(nc, ffn)
            lnT = m.sb("lnT1", [P, DC, TOK])
            layernorm_transposed(nc, "l1", X, lnT, ident, const)
            quantised_ffn(nc, X, lnT, w1, w2, gains, [(w1_in, 16), (w2_in, 16)])
        fw.close()

        with ExitStack() as attn:
            m = Memory(nc, attn)
            kcos = m.sb("kcos", [P, 2 * TILES, HD])
            ksin = m.sb("ksin", [P, 2 * TILES, HD])
            qcos = m.sb("qcos", [P, TILES, HD])
            qsin = m.sb("qsin", [P, TILES, HD])
            with ExitStack() as tables:
                n = Memory(nc, tables)
                pos = n.sb("pos", [P, 2 * TILES], I32)
                kw = n.sb("kw", [P, HD])
                qw = n.sb("qw", [P, HD])
                pos_in = m.sem("pos_in")
                kw_in = m.sem("kw_in")
                qw_in = m.sem("qw_in")
                with nc.Block() as block:
                    @block.sync
                    def _(sp):
                        sp.dma_start(pos[:, :], t["pos"]).then_inc(pos_in, 16)
                        sp.dma_start(kw[:, :], t["k_norm"].partition_broadcast(P)).then_inc(kw_in, 16)
                        sp.dma_start(qw[:, :], t["q_norm"].partition_broadcast(P)).then_inc(qw_in, 16)
                rope_tables(nc, pos, kw, qw, kcos, ksin, qcos, qsin, const,
                            [(pos_in, 16), (kw_in, 16), (qw_in, 16)])
            lnT = m.sb("lnT2", [P, DC, TOK])
            layernorm_transposed(nc, "l2", X, lnT, ident, const)
            gqa_attention(nc, t, X, lnT, wq, wk, wv, wo, kcos, ksin, qcos, qsin, gains, const, ident,
                          [(wq_in, 16), (wk_in, 16), (wv_in, 16), (wo_in, 16)])

        aw.close()
        with ExitStack() as moe:
            m = Memory(nc, moe)
            gate = m.sb("gate", [P, DC, EXPERTS * INNER])
            up = m.sb("up", [P, DC, EXPERTS * INNER])
            down = m.sb("down", [P, IC, EXPERTS * D])
            router = m.sb("router", [P, DC, EXPERTS])
            lnT = m.sb("lnT3", [P, DC, TOK])
            ln = m.sb("ln3", [P, TILES, D])
            slot = m.sb("slot", [P, TILES], U32)
            expert = m.sb("expert", [1, SLOT_TILES], I32)
            zero = m.sb("zero", [P, D])
            router_in = m.sem("router_in")
            gate_in = m.sem("gate_in2")
            up_in = m.sem("up_in")
            down_in = m.sem("down_in")
            zero_done = m.sem("zero_done")
            zeroed = m.sem("zeroed")
            with nc.Block() as block:
                @block.gpsimd
                def _(pool):
                    pool.memset(zero[:, :], 0.0).then_inc(zero_done, 1)

                @block.sync
                def _(sp):
                    sp.wait_ge(zero_done, 1)
                    sp.dma_start(sorted_x.rearrange("(t p) d -> p t d", p=P),
                                 zero[:, :].unsqueeze(1).to_broadcast([P, SLOT_TILES, D])).then_inc(zeroed, 16)
                    sp.dma_start(router[:, :, :], t["router"].rearrange("(c p) e -> p c e", p=P)
                                 ).then_inc(router_in, 16)
                    for e in range(EXPERTS):
                        i, d = slice(e * INNER, (e + 1) * INNER), slice(e * D, (e + 1) * D)
                        sp.dma_start(gate[:, :, i], t["gate"][e].rearrange("(c p) i -> p c i", p=P)
                                     ).then_inc(gate_in, 16)
                        sp.dma_start(up[:, :, i], t["up"][e].rearrange("(c p) i -> p c i", p=P)
                                     ).then_inc(up_in, 16)
                        sp.dma_start(down[:, :, d], t["down"][e].rearrange("(c p) d -> p c d", p=P)
                                     ).then_inc(down_in, 16)
            layernorm_transposed(nc, "l3", X, lnT, ident, const, kept=ln)
            route(nc, lnT, ln, router, slot, expert, sorted_x, const, [(router_in, 16)], (zeroed, 16))
            experts(nc, X, gate, up, down, expert, slot, sorted_x, sorted_y, gains, ident, out,
                    [(gate_in, 16 * EXPERTS), (up_in, 16 * EXPERTS), (down_in, 16 * EXPERTS)])


def kernel(**inputs):
    import numpy as _np
    import concourse.bacc as _bacc
    from concourse import mybir as _mybir
    from concourse.bass_utils import run_bass_kernel_spmd as _run

    i = {k: _np.asarray(v) for k, v in inputs.items()}
    const, sel = host_constants()
    laid = {
        "x": i["x"].reshape(TOK, D),
        "ctx": i["ctx_2048"].reshape(TOK, D),
        "ctxT": i["ctx_2048"].reshape(TOK, D).T,
        "const": const,
        "sel": sel,
        "gains": _np.concatenate([i["g_xattn"], i["g_ffn"]]),
        "gate_w": _np.concatenate([i["L0_xattn_Wi"], i["L0_xattn_Wf"]], axis=1),
        "gate_b": _np.concatenate([i["L0_xattn_bi"], i["L0_xattn_bf"]])[:, None],
        "pos": _np.concatenate([i["pos_BxS2"].reshape(TILES, P), i["itok_BxS_4096_4607"].reshape(TILES, P)]).T,
        "k_norm": i["L1_xattn_k_norm_w"],
        "q_norm": i["L1_xattn_q_norm_w"],
        "wqT": i["L1_xattn_Wq"].T,
        "wkT": i["L1_xattn_Wk"].T,
        "wvT": i["L1_xattn_Wv"].T,
        "woT": i["L1_xattn_Wo"].T,
        "router": i["L1_ffn_router_w"],
        "gate": i["L1_ffn_gate_w"],
        "up": i["L1_ffn_up_w"],
        "down": i["L1_ffn_down_w"],
        "w1T": i["L0_ffn_W1"].T,
        "w2T": i["L0_ffn_W2"].T,
        "ln_scale": i["L0_xattn_ln_scale"],
    }
    nc = _bacc.Bacc("TRN2", target_bir_lowering=False, num_devices=1)
    arrays, args = {}, {}
    for name, a in laid.items():
        a = _np.ascontiguousarray(a)
        arrays[f"in_{name}"] = a
        args[name] = nc.dram_tensor(f"in_{name}", a.shape, _mybir.dt.from_np(a.dtype), kind="ExternalInput").ap()
    out = nc.dram_tensor("out", (TOK, D), F32, kind="ExternalOutput").ap()
    flamingo(nc, args, out)
    r = _run(nc, [arrays], core_ids=[0])
    return r.results[0]["out"].reshape(B, S_LEN, D)
```

```python
from contextlib import ExitStack

import concourse.bass as bass
from concourse import mybir
from concourse.alu_op_type import AluOpType as ALU
import numpy as np

F32 = mybir.dt.float32
F32R = mybir.dt.float32r
I32 = mybir.dt.int32
U32 = mybir.dt.uint32
ACT = mybir.ActivationFunctionType
AX = mybir.AxisListType

P = 128
B = 4
S_LEN = 256
D = 256
TOK = B * S_LEN
TILES = TOK // P
DC = D // P
TPB = S_LEN // P

M_HEADS = 16
M_DH = D // M_HEADS
HALF = P // M_DH
AUG = M_DH + 1

FF = 1024
FC = FF // P

HEADS = 16
KV_HEADS = 4
HD = 128
REP = HEADS // KV_HEADS
KEYS = 2 * S_LEN
KT_TILES = KEYS // P
ROT = HD // 2

EXPERTS = 8
INNER = 512
IC = INNER // P
SLOT_TILES = (TOK - EXPERTS) // P + EXPERTS
SLOTS = SLOT_TILES * P

LN_EPS = 1e-5
EPS = 1e-6
ROUND = 12582912.0
PI_CLAMP = 3.1415925
TWO_PI = 2.0 * float(np.pi)
PI_HIGH = 6.28125
PI_MID = float(np.round((TWO_PI - PI_HIGH) * 2.0 ** 21) / 2.0 ** 21)
PI_LOW = TWO_PI - PI_HIGH - PI_MID

C_IDENT = 0
C_ONES = C_IDENT + P
C_TRI = C_ONES + P
C_PAR = C_TRI + P
C_BDM = C_PAR + 4
C_SPLIT = C_BDM + HALF * AUG
C_FREQ = C_SPLIT + 2
C_NEGHALF = C_FREQ + ROT
C_TILE = C_NEGHALF + 64
C_EXP = C_TILE + SLOT_TILES
C_WIDE = C_EXP + EXPERTS


def host_constants():
    c = np.zeros((P, C_WIDE), np.float32)
    p = np.arange(P)
    c[:, C_IDENT:C_IDENT + P] = np.eye(P)
    c[:, C_ONES:C_ONES + P] = 1.0
    c[:, C_TRI:C_TRI + P] = p[:, None] < p[None, :]
    for n in range(4):
        c[:, C_PAR + n] = np.where((p // M_DH) % 4 == n, float(M_DH) ** -0.5, 0.0)
    c[:, C_BDM:C_BDM + HALF * AUG] = np.repeat(p[:, None] // M_DH == np.arange(HALF)[None, :], AUG, 1)
    c[:, C_SPLIT] = p % 32 >= 16
    c[:, C_SPLIT + 1] = np.where(p % 32 >= 16, -1.0, 1.0)
    freq = np.float32(1.0) / np.float32(10000.0) ** (np.arange(0, HD, 2, dtype=np.float32) / np.float32(HD))
    c[:, C_FREQ:C_FREQ + ROT] = freq
    c[:, C_NEGHALF:C_NEGHALF + 64] = -0.5
    c[:, C_TILE:C_TILE + SLOT_TILES] = np.arange(SLOT_TILES)
    c[:, C_EXP:C_EXP + EXPERTS] = np.arange(EXPERTS)
    sel = np.zeros((32, M_HEADS, P), np.float32)
    for h in range(M_HEADS):
        sel[h, h] = 1.0
        sel[16 + h, h] = 1.0
    return c, sel.reshape(32, M_HEADS * P)


class Memory:

    def __init__(self, nc, stack):
        self.nc, self.stack = nc, stack

    def sb(self, name, shape, dt=F32):
        return self.stack.enter_context(self.nc.sbuf_tensor(name, shape, dt))

    def ps(self, name, banks):
        return self.stack.enter_context(self.nc.psum_tensor(name, [P, banks, 512], F32))

    def sem(self, name):
        return self.stack.enter_context(self.nc.semaphore(name))


def first_then_loop(eng, n, body):
    body(0)
    with eng.Fori(1, n) as j:
        body(j)


def wait_for(eng, sem, count):
    if not (isinstance(count, int) and count == 0):
        eng.wait_ge(sem, count)


def layernorm_transposed(nc, tag, X, lnT, ident, const, const_ready=None, x_ready=None, kept=None, meanwhile=None,
                         follow=None):
    with ExitStack() as st:
        m = Memory(nc, st)
        stats = m.sb(f"{tag}_stats", [P, TILES, 6])
        mv = m.sb(f"{tag}_mv", [P, TILES, 2])
        ve = m.sb(f"{tag}_ve", [P, TILES])
        rstd = m.sb(f"{tag}_rstd", [P, TILES])
        ln = m.sb(f"{tag}_ln", [P, 2, TPB, D]) if kept is None else None
        lnps = m.ps(f"{tag}_lnps", 2)
        stats_done = m.sem(f"{tag}_stats_done")
        mv_done = m.sem(f"{tag}_mv_done")
        ve_done = m.sem(f"{tag}_ve_done")
        rstd_done = m.sem(f"{tag}_rstd_done")
        ln_done = m.sem(f"{tag}_ln_done")
        turned = m.sem(f"{tag}_turned")
        stored = m.sem(f"{tag}_stored")
        with nc.Block() as block:
            if meanwhile is not None:
                block.sync(meanwhile)

            @block.vector
            def _(dve):
                if x_ready is not None:
                    dve.wait_ge(*x_ready)
                for t in range(TILES):
                    dve.bn_stats(stats[:, t, :], X[:, t, :]).then_inc(stats_done, 1)
                dve.wait_ge(stats_done, TILES)
                for t in range(TILES):
                    dve.bn_aggr(mv[:, t, :], stats[:, t, :]).then_inc(mv_done, 1)
                dve.wait_ge(rstd_done, 1)

                for t in range(TILES):
                    j, tt = divmod(t, TPB)
                    if kept is None and j >= 2:
                        dve.wait_ge(turned, j - 1)
                    dve.tensor_scalar(ln[:, j % 2, tt, :] if kept is None else kept[:, t, :],
                                      X[:, t, :], mv[:, t, 0:1], rstd[:, t:t + 1],
                                      ALU.subtract, ALU.mult).then_inc(ln_done, 1)

            @block.gpsimd
            def _(pool):
                if const_ready is not None:
                    pool.wait_ge(*const_ready)
                pool.wait_ge(mv_done, TILES)
                pool.tensor_scalar(ve[:, :], mv[:, :, 1], LN_EPS, 1.0, ALU.add, ALU.mult).then_inc(ve_done, 1)
                pool.wait_ge(ve_done, 1)
                pool.tensor_tensor(rstd[:, :], ve[:, :], const[:, C_NEGHALF:C_NEGHALF + TILES],
                                   ALU.pow).then_inc(rstd_done, 1)

            @block.tensor
            def _(pe):
                if const_ready is not None:
                    pe.wait_ge(*const_ready)

                for j in range(TILES // TPB):
                    pe.wait_ge(ln_done, TPB * j + TPB)
                    if j >= 2:
                        pe.wait_ge(stored, j - 1)
                    for tt in range(TPB):
                        src = ln[:, j % 2, tt, :] if kept is None else kept[:, TPB * j + tt, :]
                        for c in range(DC):
                            last = pe.transpose(lnps[:, j % 2, c * S_LEN + tt * P:c * S_LEN + (tt + 1) * P],
                                                src[:, c * P:(c + 1) * P], ident)
                    last.then_inc(turned, 1)
                    if follow is not None and j >= 1:
                        pe.wait_ge(stored, j)
                        for tt in range(TPB):
                            follow(pe, TPB * (j - 1) + tt)
                if follow is not None:
                    pe.wait_ge(stored, TILES // TPB)
                    for tt in range(TPB):
                        follow(pe, TILES - TPB + tt)

            @block.scalar
            def _(act):
                for j in range(TILES // TPB):
                    act.wait_ge(turned, j + 1)
                    act.activation(lnT[:, :, j * S_LEN:(j + 1) * S_LEN],
                                   lnps[:, j % 2, :].rearrange("p (c s) -> p c s", c=DC),
                                   ACT.Copy).then_inc(stored, 1)


def mlstm_rows(nc, mem, lnT, ctxT, gate_w, gate_b, sel, const, cols, Gr, Mr, selr, ident, loads):
    with ExitStack() as st:
        m = Memory(nc, st)
        z = m.sb("a_z", [32, TOK])
        soft = m.sb("a_soft", [32, TOK])
        logf = m.sb("a_logf", [32, TOK])
        F = m.sb("a_F", [32, TOK])
        Fs = m.sb("a_Fs", [32, TOK])
        g = m.sb("a_g", [32, TOK])
        M = m.sb("a_M", [32, TOK])
        dup = m.sb("a_dup", [32, TOK])
        hi = m.sb("a_hi", [32, TOK], F32R)
        low = m.sb("a_low", [32, TOK])
        ones = m.sb("a_ones", [32, S_LEN])
        ex = m.sb("a_ex", [32, B, 4, P])
        zps = m.ps("a_zps", 2)
        cps = m.ps("a_cps", 1)
        gates_done = m.sem("a_gates_done")
        z_done = m.sem("a_z_done")
        act_step = m.sem("a_act_step")
        row_step = m.sem("a_row_step")
        ones_done = m.sem("a_ones_done")
        arg_done = m.sem("a_arg_done")
        ex_done = m.sem("a_ex_done")
        cols_turned = m.sem("a_cols_turned")
        shift = [16 + i for i in range(16)] + [16 + i for i in range(16)]
        twice = [i % 16 for i in range(32)]
        with nc.Block() as block:
            @block.tensor
            def _(pe):
                for ready in loads:
                    pe.wait_ge(*ready)
                for half in range(2):
                    for c in range(3 * DC):
                        src = lnT if c < DC else ctxT
                        last = pe.matmul(zps[0:32, half, :], gate_w[:, c, :],
                                         src[:, c % DC, half * 512:(half + 1) * 512],
                                         start=(c == 0), stop=(c == 3 * DC - 1))
                last.then_inc(gates_done, 1)
                pe.wait_ge(ex_done, 1)
                for b in range(B):
                    for kind in range(4):
                        last = pe.transpose(cps[:, 0, (b * 4 + kind) * 32:(b * 4 + kind + 1) * 32],
                                            ex[:, b, kind, :], ident[0:32, 0:32])
                last.then_inc(cols_turned, 1)

            @block.scalar
            def _(act):
                act.wait_ge(z_done, 1)
                act.activation(soft[:, :], z[:, :], ACT.Abs).then_inc(act_step, 1)
                act.wait_ge(act_step, 1)
                act.activation(soft[:, :], soft[:, :], ACT.Exp, scale=-1.0).then_inc(act_step, 1)
                act.wait_ge(act_step, 2)
                act.activation(soft[:, :], soft[:, :], ACT.Ln, bias=1.0).then_inc(act_step, 1)
                act.wait_ge(arg_done, 4)
                act.activation(ex[:, :, :, :], ex[:, :, :, :], ACT.Exp).then_inc(ex_done, 1)
                act.wait_ge(cols_turned, 1)
                act.activation(cols[:, :, :, :].rearrange("p b k r -> p (b k r)"), cps[:, 0, :], ACT.Copy)

            @block.vector
            def _(dve):
                dve.memset(ones[:, :], 1.0).then_inc(ones_done, 1)
                for ready in loads:
                    dve.wait_ge(*ready)
                dve.tensor_copy(selr[:, :], sel[:, :])
                dve.wait_ge(gates_done, 1)
                dve.tensor_scalar(z[:, :], zps[0:32, :, :].rearrange("p a n -> p (a n)"), gate_b[:, 0:1], None,
                                  ALU.add).then_inc(z_done, 1)
                dve.wait_ge(z_done, 1)
                dve.wait_ge(act_step, 3)
                dve.scalar_tensor_tensor(out=logf[:, :], in0=z[:, :], scalar=0.0, in1=soft[:, :],
                                         op0=ALU.min, op1=ALU.subtract).then_inc(row_step, 1)
                dve.wait_ge(row_step, 1)
                dve.wait_ge(ones_done, 1)
                for b in range(B):
                    s = slice(b * S_LEN, (b + 1) * S_LEN)
                    dve.tensor_tensor_scan(F[:, s], ones[:, :], logf[:, s], 0.0, ALU.mult,
                                           ALU.add).then_inc(row_step, 1)
                dve.wait_ge(row_step, 5)
                dve.stream_shuffle(Fs[:, :], F[:, :], shift).then_inc(row_step, 1)
                dve.wait_ge(row_step, 6)
                dve.tensor_tensor(g[:, :], z[:, :], Fs[:, :], ALU.subtract).then_inc(row_step, 1)
                dve.wait_ge(row_step, 7)
                for b in range(B):
                    s = slice(b * S_LEN, (b + 1) * S_LEN)
                    dve.tensor_tensor_scan(M[:, s], g[:, s], g[:, s], -3.0e38, ALU.max,
                                           ALU.max).then_inc(row_step, 1)
                dve.wait_ge(row_step, 11)
                M4 = M[:, :].rearrange("p (b k s) -> p b k s", b=B, k=2)
                F4 = Fs[:, :].rearrange("p (b k s) -> p b k s", b=B, k=2)
                g4 = g[:, :].rearrange("p (b k s) -> p b k s", b=B, k=2)
                last0 = M4[:, :, 0, P - 1:P].to_broadcast([32, B, P])
                for k in range(2):
                    dve.scalar_tensor_tensor(out=ex[:, :, k, :], in0=M4[:, :, k, :], scalar=-1.0,
                                             in1=F4[:, :, k, :], op0=ALU.mult,
                                             op1=ALU.subtract).then_inc(arg_done, 1)
                dve.tensor_tensor(ex[:, :, 2, :], g4[:, :, 0, :], last0, ALU.subtract).then_inc(arg_done, 1)
                dve.tensor_tensor(ex[:, :, 3, :], last0, M4[:, :, 1, :], ALU.subtract).then_inc(arg_done, 1)
                step = 11
                for src, sign, dst in ((g, 1.0, Gr), (M, -1.0, Mr)):
                    dve.stream_shuffle(dup[:, :], src[:, :], twice).then_inc(row_step, 1)
                    dve.wait_ge(row_step, step + 1)
                    dve.tensor_scalar(hi[:, :], dup[:, :], sign, None, ALU.mult).then_inc(row_step, 1)
                    dve.tensor_scalar(low[:, :], dup[:, :], const[0:32, C_SPLIT:C_SPLIT + 1], sign, ALU.mult,
                                      ALU.mult).then_inc(row_step, 1)
                    dve.wait_ge(row_step, step + 3)
                    dve.scalar_tensor_tensor(out=dst[:, :], in0=hi[:, :].bitcast(F32),
                                             scalar=const[0:32, C_SPLIT + 1:C_SPLIT + 2], in1=low[:, :],
                                             op0=ALU.mult, op1=ALU.add).then_inc(row_step, 1)
                    step += 4


def mlstm_and_ffn(nc, X, lnT, ctx, ctxT, cols, Gr, Mr, selr, scale_row, const, ident, w1, w2, gains, lnT2, loads, pos,
                  pos_ready, sc):
    HH = M_HEADS // HALF
    W = HALF * AUG
    ROWS = TPB * M_HEADS
    UNITS = TPB * HH
    QTR = FC // 4
    TAIL = 8
    with ExitStack() as st:
        m = Memory(nc, st)
        kT = m.sb("b_kT", [P, DC, S_LEN])
        Gb = m.sb("b_Gb", [32, S_LEN], F32R)
        Qm = m.sb("b_Qm", [P, DC, 4, S_LEN])
        V1 = m.sb("b_V1", [P, TPB, M_HEADS, AUG])
        KU = m.sb("b_KU", [P, D])
        BD = m.sb("b_BD", [P, HH, W])
        E = m.sb("b_E", [P, 2, HALF, P])
        C = m.sb("b_C", [P, 2, HALF, P])
        num = m.sb("b_num", [P, TPB, M_HEADS, AUG])
        carried = m.sb("b_carried", [P, M_HEADS, AUG])
        den = m.sb("b_den", [P, TPB, M_HEADS])
        rden = m.sb("b_rden", [P, TPB, M_HEADS])
        h = m.sb("b_h", [P, ROWS, M_DH])
        hc = m.sb("b_hc", [P, ROWS, M_DH])
        sq = m.sb("b_sq", [P, ROWS, M_DH])
        hsum = m.sb("b_hsum", [P, ROWS])
        vsum = m.sb("b_vsum", [P, ROWS])
        hve = m.sb("b_hve", [P, ROWS])
        rs = m.sb("b_rs", [P, ROWS])
        hn = m.sb("b_hn", [P, TPB, D])
        held = m.sb("f_held", [P, 1])
        stats = m.sb("f_stats", [P, 2, TPB, 6])
        mv = m.sb("f_mv", [P, 2, TPB, 2])
        lve = m.sb("f_lve", [P, 2, TPB])
        rstd = m.sb("f_rstd", [P, 2, TPB])
        ln = m.sb("f_ln", [P, 2, TPB, D])
        lnTb = m.sb("f_lnTb", [P, DC, S_LEN])
        q = m.sb("f_q", [P, 2, 512])
        r = m.sb("f_r", [P, 2, 512])
        a = m.sb("f_a", [P, FC, S_LEN])
        posf = m.sb("r_posf", [P, 2 * TILES])
        ang = m.sb("r_ang", [P, 2 * TILES, ROT])
        turns = m.sb("r_turns", [P, 2 * TILES, ROT])
        angle_step = m.sem("r_angle_step")
        arg_ready = m.sem("r_arg_ready")
        sps = m.ps("b_sps", 2)
        eps_ = m.ps("b_eps", 2)
        pvps = m.ps("b_pvps", 1)
        stps = m.ps("b_stps", 1)
        fps = m.ps("f_fps", 2)
        ones_in = m.sem("b_ones_in")
        k_ready = m.sem("b_k_ready")
        g_ready = m.sem("b_g_ready")
        q_ready = m.sem("b_q_ready")
        v_ready = m.sem("b_v_ready")
        ku_ready = m.sem("b_ku_ready")
        state_done = m.sem("b_state_done")
        bd_ready = m.sem("b_bd_ready")
        decay_done = m.sem("b_decay_done")
        scores_done = m.sem("b_scores_done")
        exp_done = m.sem("b_exp_done")
        masked = m.sem("b_masked")
        prod_done = m.sem("b_prod_done")
        pv_done = m.sem("b_pv_done")
        carry_done = m.sem("b_carry_done")
        num_done = m.sem("b_num_done")
        carried_done = m.sem("b_carried_done")
        step = m.sem("b_step")
        centred = m.sem("b_centred")
        squared = m.sem("b_squared")
        var_done = m.sem("b_var_done")
        hve_done = m.sem("b_hve_done")
        rs_done = m.sem("b_rs_done")
        stats_done = [m.sem(f"f_stats_done{n}") for n in range(2)]
        mv_done = [m.sem(f"f_mv_done{n}") for n in range(2)]
        lve_done = [m.sem(f"f_lve_done{n}") for n in range(2)]
        rstd_done = [m.sem(f"f_rstd_done{n}") for n in range(2)]
        ln_done = [m.sem(f"f_ln_done{n}") for n in range(2)]
        turned = [m.sem(f"f_turned{n}") for n in range(2)]
        lnT_ready = [m.sem(f"f_lnT_ready{n}") for n in range(2)]
        up_done = m.sem("f_up_done")
        clipped = m.sem("f_clipped")
        rounded = m.sem("f_rounded")
        scaled = m.sem("f_scaled")
        gelu_done = m.sem("f_gelu_done")
        down_done = m.sem("f_down_done")
        x_done = [m.sem(f"f_x_done{n}") for n in range(2)]

        def steps(eng, body):
            body(0, True, False, False)
            body(1, True, True, False)
            with eng.Fori(2, B) as k:
                body(k, True, True, True)
            body(B, False, True, True)
            body(B + 1, False, False, True)

        with nc.Block() as block:
            @block.gpsimd
            def _(pool):
                def rsqrt_ln(b, n):
                    pool.wait_ge(mv_done[n], TPB * b + TPB)
                    pool.tensor_scalar(lve[:, n, :], mv[:, n, :, 1], LN_EPS, 1.0, ALU.add,
                                       ALU.mult).then_inc(lve_done[n], 1)
                    pool.wait_ge(lve_done[n], b + 1)
                    pool.tensor_tensor(rstd[:, n, :], lve[:, n, :], const[:, C_NEGHALF:C_NEGHALF + TPB],
                                       ALU.pow).then_inc(rstd_done[n], 1)

                def rsqrt_heads(b, tt):
                    pool.wait_ge(hve_done, b + 1)
                    pool.tensor_tensor(rs[:, tt * M_HEADS:(tt + 1) * M_HEADS], hve[:, tt * M_HEADS:(tt + 1) * M_HEADS],
                                       const[:, C_NEGHALF:C_NEGHALF + M_HEADS], ALU.pow).then_inc(rs_done, 1)

                def mask(b, u):
                    pool.wait_ge(exp_done, UNITS * b + u + 1)
                    pool.affine_select(out=E[:, u % 2, :, :], in_=E[:, u % 2, :, :], compare_op=ALU.is_ge,
                                       fill=0.0, base=0, pattern=[[0, HALF], [1, P]],
                                       channel_multiplier=-1).then_inc(masked, 1)

                for k in range(B + 2):
                    heads, ffn, rest = k < B, 1 <= k <= B, k >= 2
                    if heads:
                        wait_for(pool, scores_done, UNITS * k)
                        pool.tensor_scalar(kT[:, :, :], ctxT[:, :, k * S_LEN:(k + 1) * S_LEN], 1.0, 1.0,
                                           ALU.mult, ALU.mult).then_inc(k_ready, 1)
                        mask(k, 0)
                    if ffn:
                        pool.wait_ge(var_done, k)
                        pool.tensor_scalar(hve[:, :], vsum[:, :], 1.0 / M_DH, EPS, ALU.mult,
                                           ALU.add).then_inc(hve_done, 1)
                        rsqrt_heads(k - 1, 0)
                    if heads:
                        mask(k, 1)
                    if ffn:
                        rsqrt_heads(k - 1, 1)
                    if heads:
                        mask(k, 2)
                    if ffn:
                        rsqrt_ln(k - 1, 0)
                    if rest:
                        rsqrt_ln(k - 2, 1)
                    if heads:
                        mask(k, 3)
                    if ffn:
                        for n in range(4):
                            pool.wait_ge(rounded, 4 * k - 4 + n + 1)
                            pool.tensor_scalar(r[:, n % 2, :], r[:, n % 2, :], -ROUND, 0.1, ALU.add,
                                               ALU.mult).then_inc(scaled, 1)

            @block.scalar
            def _(act):
                act.wait_ge(ones_in, 1)

                def exponential(b, u):
                    act.wait_ge(decay_done, UNITS * b + u + 1)
                    wait_for(act, prod_done, UNITS * b + u - 1 if u > 0 else UNITS * b)
                    act.activation(E[:, u % 2, :, :].rearrange("p (a h) s -> p a (h s)", a=2),
                                   eps_[:, :, :], ACT.Exp).then_inc(exp_done, 1)

                def body(k, heads, ffn, rest):
                    if heads:
                        wait_for(act, pv_done, UNITS * k)
                        act.activation(V1[:, :, :, 0:M_DH].rearrange("p t h d -> p (t h) d"),
                                       ctx[:, bass.ds(k * TPB, TPB), :].rearrange("p t (h d) -> p (t h) d", d=M_DH),
                                       ACT.Copy).then_inc(v_ready, 1)
                        exponential(k, 0)
                    if ffn:
                        act.wait_ge(centred, k)
                        act.activation(sq[:, :, :], hc[:, :, :], ACT.Square).then_inc(squared, 1)
                    if heads:
                        for u in range(1, UNITS):
                            exponential(k, u)
                    if not ffn and not rest:
                        act.wait_ge(arg_ready, 2)
                        act.activation(sc[:, :, :, :], sc[:, :, :, :], ACT.Sin)
                    if ffn:
                        act.wait_ge(turned[0], k)
                        act.activation(lnTb[:, :, :], fps[:, 0, :].rearrange("p (c s) -> p c s", c=DC),
                                       ACT.Copy).then_inc(lnT_ready[0], 1)
                    if rest:
                        act.wait_ge(turned[1], k - 1)
                        act.activation(lnT2[:, :, bass.ds((k - 2) * S_LEN, S_LEN)],
                                       fps[:, 1, :].rearrange("p (c s) -> p c s", c=DC),
                                       ACT.Copy).then_inc(lnT_ready[1], 1)
                    if ffn:
                        for n in range(4):
                            act.wait_ge(scaled, 4 * k - 4 + n + 1)
                            act.activation(a[:, n * QTR:(n + 1) * QTR, :].rearrange("p f s -> p (f s)"),
                                           r[:, n % 2, :], ACT.Gelu_apprx_tanh).then_inc(gelu_done, 1)

                steps(act, body)

            @block.vector
            def _(dve):
                dve.memset(V1[:, :, :, M_DH:AUG], 1.0).then_inc(ones_in, 1)

                def prepare(b):
                    wait_for(dve, decay_done, UNITS * b)
                    dve.tensor_copy(Gb[:, :], Gr[:, bass.ds(b * S_LEN, S_LEN)].bitcast(F32)).then_inc(g_ready, 1)
                    wait_for(dve, scores_done, UNITS * b)
                    wait_for(dve, carry_done, b)
                    for n in range(4):
                        dve.tensor_scalar(Qm[:, :, n, :], lnT[:, :, bass.ds(b * S_LEN, S_LEN)],
                                          const[:, C_PAR + n:C_PAR + n + 1], None, ALU.mult).then_inc(q_ready, 1)
                    wait_for(dve, state_done, b)
                    dve.tensor_tensor(KU[:, :].rearrange("p (h d) -> p h d", d=M_DH),
                                      ctx[:, b * TPB, :].rearrange("p (h d) -> p h d", d=M_DH),
                                      cols[:, b, 2, 0:M_HEADS].unsqueeze(2).to_broadcast([P, M_HEADS, M_DH]),
                                      ALU.mult).then_inc(ku_ready, 1)

                def state(b):
                    dve.wait_ge(state_done, b + 1)
                    dve.tensor_tensor(BD[:, :, :], stps[:, 0, 0:HH * W].rearrange("p (a w) -> p a w", a=HH),
                                      const[:, C_BDM:C_BDM + W].unsqueeze(1).to_broadcast([P, HH, W]),
                                      ALU.mult).then_inc(bd_ready, 1)

                def product(b, u):
                    dve.wait_ge(scores_done, UNITS * b + u + 1)
                    dve.wait_ge(masked, UNITS * b + u + 1)
                    if u >= 2:
                        dve.wait_ge(pv_done, UNITS * b + u - 1)
                    dve.tensor_tensor(C[:, u % 2, :, :].rearrange("p (a h) s -> p a (h s)", a=2), sps[:, :, :],
                                      E[:, u % 2, :, :].rearrange("p (a h) s -> p a (h s)", a=2),
                                      ALU.mult).then_inc(prod_done, 1)

                def first_sums(b):
                    dve.wait_ge(pv_done, UNITS * b + 2)
                    dve.tensor_copy(num[:, 0, :, :].rearrange("p h a -> p (h a)"),
                                    pvps[:, 0, 0:HH * W]).then_inc(num_done, 1)

                def carry(b):
                    dve.wait_ge(carry_done, b + 1)
                    dve.tensor_tensor(carried[:, :, :], stps[:, 0, 0:HH * W].rearrange("p (h a) -> p h a", a=AUG),
                                      cols[:, b, 3, 0:M_HEADS].unsqueeze(2).to_broadcast([P, M_HEADS, AUG]),
                                      ALU.mult).then_inc(carried_done, 1)

                def second_sums(b):
                    dve.wait_ge(carried_done, b + 1)
                    dve.wait_ge(pv_done, UNITS * b + 4)
                    dve.tensor_tensor(num[:, 1, :, :].rearrange("p h a -> p (h a)"), pvps[:, 0, 0:HH * W],
                                      carried[:, :, :].rearrange("p h a -> p (h a)"),
                                      ALU.add).then_inc(num_done, 1)

                def normalise_rows(b):
                    dve.wait_ge(num_done, 2 * b + 2)
                    dve.scalar_tensor_tensor(out=den[:, :, :], in0=num[:, :, :, M_DH], scalar=-1.0,
                                             in1=num[:, :, :, M_DH], op0=ALU.mult,
                                             op1=ALU.max).then_inc(step, 1)
                    dve.wait_ge(step, TAIL * b + 1)
                    dve.tensor_tensor(den[:, :, :], den[:, :, :], cols[:, b, 0:TPB, 0:M_HEADS],
                                      ALU.max).then_inc(step, 1)
                    dve.wait_ge(step, TAIL * b + 2)
                    dve.tensor_scalar(den[:, :, :], den[:, :, :], EPS, None, ALU.add).then_inc(step, 1)
                    dve.wait_ge(step, TAIL * b + 3)
                    dve.reciprocal(rden[:, :, :], den[:, :, :]).then_inc(step, 1)
                    dve.wait_ge(step, TAIL * b + 4)
                    dve.tensor_tensor(h[:, :, :], num[:, :, :, 0:M_DH].rearrange("p t h d -> p (t h) d"),
                                      rden[:, :, :].rearrange("p t h -> p (t h)").unsqueeze(2)
                                      .to_broadcast([P, ROWS, M_DH]), ALU.mult).then_inc(step, 1)
                    dve.wait_ge(step, TAIL * b + 5)
                    dve.tensor_reduce(hsum[:, :], h[:, :, :], AX.X, ALU.add).then_inc(step, 1)
                    dve.wait_ge(step, TAIL * b + 6)
                    dve.scalar_tensor_tensor(out=hc[:, :, :], in0=hsum[:, :].unsqueeze(2).to_broadcast([P, ROWS, M_DH]),
                                             scalar=-1.0 / M_DH, in1=h[:, :, :], op0=ALU.mult,
                                             op1=ALU.add).then_inc(centred, 1)

                def variance(b):
                    dve.wait_ge(squared, b + 1)
                    dve.tensor_reduce(vsum[:, :], sq[:, :, :], AX.X, ALU.add).then_inc(var_done, 1)

                def add_heads(b):
                    dve.wait_ge(rs_done, TPB * b + TPB)
                    dve.tensor_tensor(hn[:, :, :].rearrange("p t (h d) -> p (t h) d", d=M_DH), hc[:, :, :],
                                      rs[:, :].unsqueeze(2).to_broadcast([P, ROWS, M_DH]),
                                      ALU.mult).then_inc(step, 1)
                    dve.wait_ge(step, TAIL * b + 7)
                    dve.tensor_tensor(hn[:, :, :], hn[:, :, :],
                                      scale_row[:, :].unsqueeze(1).to_broadcast([P, TPB, D]),
                                      ALU.mult).then_inc(step, 1)
                    dve.wait_ge(step, TAIL * b + 8)
                    dve.tensor_tensor(X[:, bass.ds(b * TPB, TPB), :], X[:, bass.ds(b * TPB, TPB), :],
                                      hn[:, :, :], ALU.add).then_inc(x_done[0], 1)

                def ln_stats(b, n):
                    dve.wait_ge(x_done[n], b + 1 if n == 0 else TPB * b + TPB)
                    dve.tensor_copy(held[:, :], const[:, C_ONES:C_ONES + 1])
                    for tt in range(TPB):
                        dve.bn_stats(stats[:, n, tt, :], X[:, b * TPB + tt, :]).then_inc(stats_done[n], 1)
                    dve.wait_ge(stats_done[n], TPB * b + TPB)
                    dve.tensor_copy(held[:, :], const[:, C_ONES:C_ONES + 1])
                    for tt in range(TPB):
                        dve.bn_aggr(mv[:, n, tt, :], stats[:, n, tt, :]).then_inc(mv_done[n], 1)

                def ln_normalise(b, n):
                    dve.wait_ge(rstd_done[n], b + 1)
                    for tt in range(TPB):
                        dve.tensor_scalar(ln[:, n, tt, :], X[:, b * TPB + tt, :], mv[:, n, tt, 0:1],
                                          rstd[:, n, tt:tt + 1], ALU.subtract, ALU.mult).then_inc(ln_done[n], 1)

                def clip(b, n):
                    dve.wait_ge(up_done, 4 * b + n + 1)
                    if n >= 2:
                        dve.wait_ge(rounded, 4 * b + n - 1)
                    dve.tensor_scalar(q[:, n % 2, :], fps[:, n % 2, :], 10.0, 32767.0, ALU.mult,
                                      ALU.min).then_inc(clipped, 1)

                def quantise(b, n):
                    dve.wait_ge(clipped, 4 * b + n + 1)
                    if n >= 2:
                        dve.wait_ge(gelu_done, 4 * b + n - 1)
                    dve.tensor_scalar(r[:, n % 2, :], q[:, n % 2, :], -32768.0, ROUND, ALU.max,
                                      ALU.add).then_inc(rounded, 1)

                def add_ffn(b):
                    dve.wait_ge(down_done, b + 1)
                    for tt in range(TPB):
                        dve.scalar_tensor_tensor(out=X[:, b * TPB + tt, :], in0=fps[:, 0, tt * D:(tt + 1) * D],
                                                 scalar=gains[:, 2:3], in1=X[:, b * TPB + tt, :],
                                                 op0=ALU.mult, op1=ALU.add).then_inc(x_done[1], 1)

                def angles(k):
                    shape = [P, 2 * TILES, ROT]
                    if k == 0:
                        dve.wait_ge(*pos_ready)
                        dve.tensor_copy(posf[:, :], pos[:, :]).then_inc(angle_step, 1)
                        dve.wait_ge(angle_step, 1)
                        dve.tensor_tensor(ang[:, :, :], posf[:, :].unsqueeze(2).to_broadcast(shape),
                                          const[:, C_FREQ:C_FREQ + ROT].unsqueeze(1).to_broadcast(shape),
                                          ALU.mult).then_inc(angle_step, 1)
                    done = 2 + 7 * k
                    arg = sc[:, k, :, :]
                    dve.wait_ge(angle_step, done)
                    dve.tensor_scalar(turns[:, :, :], ang[:, :, :], 1.0 / TWO_PI, 0.25 * k, ALU.mult,
                                      ALU.add).then_inc(angle_step, 1)
                    dve.wait_ge(angle_step, done + 1)
                    dve.tensor_scalar(turns[:, :, :], turns[:, :, :], ROUND, None, ALU.add).then_inc(angle_step, 1)
                    dve.wait_ge(angle_step, done + 2)
                    dve.tensor_scalar(turns[:, :, :], turns[:, :, :], ROUND, None,
                                      ALU.subtract).then_inc(angle_step, 1)
                    dve.wait_ge(angle_step, done + 3)
                    src = ang[:, :, :]
                    for i, part in enumerate((PI_HIGH, PI_MID, PI_LOW)):
                        dve.scalar_tensor_tensor(out=arg, in0=turns[:, :, :], scalar=-part, in1=src, op0=ALU.mult,
                                                 op1=ALU.add).then_inc(angle_step, 1)
                        dve.wait_ge(angle_step, done + 4 + i)
                        src = arg
                    dve.tensor_scalar(arg, arg, 0.25 * k * TWO_PI, PI_CLAMP, ALU.add,
                                      ALU.min).then_inc(angle_step, 1)
                    dve.wait_ge(angle_step, done + 7)
                    dve.tensor_scalar(arg, arg, -PI_CLAMP, None, ALU.max).then_inc(arg_ready, 1)

                def body(k, heads, ffn, rest):
                    if heads:
                        prepare(k)
                    if ffn:
                        second_sums(k - 1)
                        normalise_rows(k - 1)
                    if heads:
                        product(k, 0)
                        state(k)
                    if ffn:
                        variance(k - 1)
                    if not ffn and not rest:
                        angles(0)
                    if heads:
                        product(k, 1)
                    if not ffn and not rest:
                        angles(1)
                    if ffn:
                        add_heads(k - 1)
                        ln_stats(k - 1, 0)
                    if heads:
                        product(k, 2)
                    if ffn:
                        ln_normalise(k - 1, 0)
                    if rest:
                        add_ffn(k - 2)
                        ln_stats(k - 2, 1)
                    if heads:
                        first_sums(k)
                        carry(k)
                    if rest:
                        ln_normalise(k - 2, 1)
                    if heads:
                        product(k, 3)
                    if ffn:
                        for n in range(4):
                            clip(k - 1, n)
                            quantise(k - 1, n)

                steps(dve, body)

            @block.tensor
            def _(pe):
                for ready in loads:
                    pe.wait_ge(*ready)

                def decay(b, u):
                    blk, hh = divmod(u, HH)
                    if u == 0:
                        pe.wait_ge(g_ready, b + 1)
                    wait_for(pe, exp_done, UNITS * b + u)
                    for half in range(2):
                        pe.matmul(eps_[:, half, :], Gb[:, blk * P:(blk + 1) * P],
                                  selr[:, (hh * 2 + half) * 512:(hh * 2 + half + 1) * 512], start=True, stop=False)
                        for n in range(4):
                            hd = hh * HALF + half * 4 + n
                            last = pe.matmul(eps_[:, half, n * P:(n + 1) * P], selr[:, hd * P:(hd + 1) * P],
                                             Mr[:, bass.ds(b * S_LEN + blk * P, P)], start=False,
                                             stop=(n == 3))
                    last.then_inc(decay_done, 1)

                def scores(b, u):
                    blk, hh = divmod(u, HH)
                    if u == 0:
                        pe.wait_ge(q_ready, 4 * b + 4)
                        pe.wait_ge(k_ready, b + 1)
                    wait_for(pe, prod_done, UNITS * b + u)
                    for half in range(2):
                        rows = slice(64 * half, 64 * half + 64)
                        last = pe.matmul(sps[:, half, :].rearrange("p (n s) -> p n s", n=4),
                                         kT[rows, hh, blk * P:(blk + 1) * P],
                                         Qm[rows, hh, :, blk * P:(blk + 1) * P], start=True, stop=True)
                    last.then_inc(scores_done, 1)

                def values(b, u):
                    blk, hh = divmod(u, HH)
                    pe.wait_ge(prod_done, UNITS * b + u + 1)
                    if hh == 0:
                        wait_for(pe, num_done, 2 * b + blk)
                    for n in range(HALF):
                        hd = hh * HALF + n
                        last = pe.matmul(pvps[:, 0, hd * AUG:(hd + 1) * AUG], C[:, u % 2, n, :],
                                         V1[:, blk, hd, :], start=True, stop=True)
                    last.then_inc(pv_done, 1)

                def state(b):
                    pe.wait_ge(ku_ready, b + 1)
                    pe.wait_ge(v_ready, b + 1)
                    wait_for(pe, carried_done, b)
                    for hh in range(HH):
                        last = pe.matmul(stps[:, 0, hh * W:(hh + 1) * W], KU[:, hh * P:(hh + 1) * P],
                                         V1[:, 0, hh * HALF:(hh + 1) * HALF, :].rearrange("p h a -> p (h a)"),
                                         start=True, stop=True)
                    last.then_inc(state_done, 1)

                def carry(b):
                    pe.wait_ge(bd_ready, b + 1)
                    for hh in range(HH):
                        for n in range(4):
                            last = pe.matmul(stps[:, 0, hh * W:(hh + 1) * W], Qm[:, hh, n, P:2 * P],
                                             BD[:, hh, :], start=(n == 0), stop=(n == 3))
                    last.then_inc(carry_done, 1)

                def turn(b, n):
                    pe.wait_ge(ln_done[n], TPB * b + TPB)
                    for tt in range(TPB):
                        for c in range(DC):
                            last = pe.transpose(fps[:, n, c * S_LEN + tt * P:c * S_LEN + (tt + 1) * P],
                                                ln[:, n, tt, c * P:(c + 1) * P], ident)
                    last.then_inc(turned[n], 1)

                def up(b, n):
                    if n == 0:
                        pe.wait_ge(lnT_ready[0], b + 1)
                    if n >= 2:
                        pe.wait_ge(clipped, 4 * b + n - 1)
                    for f in range(QTR):
                        fc = n * QTR + f
                        for c in range(DC):
                            last = pe.matmul(fps[:, n % 2, f * S_LEN:(f + 1) * S_LEN],
                                             w1[:, c, fc * P:(fc + 1) * P], lnTb[:, c, :],
                                             start=(c == 0), stop=(c == DC - 1))
                    last.then_inc(up_done, 1)

                def down(b, first, end):
                    if first == 0:
                        pe.wait_ge(gelu_done, 4 * b + 4)
                    for j in range(first, end):
                        tt, fc = divmod(j, FC)
                        last = pe.matmul(fps[:, 0, tt * D:(tt + 1) * D], a[:, fc, tt * P:(tt + 1) * P],
                                         w2[:, fc, :], start=(fc == 0), stop=(fc == FC - 1))
                    if end == TPB * FC:
                        last.then_inc(down_done, 1)

                def body(k, heads, ffn, rest):
                    if heads:
                        decay(k, 0)
                    if rest:
                        down(k - 2, 0, 4)
                    if heads:
                        scores(k, 0)
                        state(k)
                    if rest:
                        down(k - 2, 4, 7)
                    if heads:
                        decay(k, 1)
                        scores(k, 1)
                    if rest:
                        down(k - 2, 7, 10)
                    if heads:
                        values(k, 0)
                    if rest:
                        down(k - 2, 10, 13)
                    if heads:
                        decay(k, 2)
                        scores(k, 2)
                    if rest:
                        down(k - 2, 13, 16)
                    if heads:
                        values(k, 1)
                        carry(k)
                        decay(k, 3)
                    if ffn:
                        if rest:
                            pe.wait_ge(x_done[1], TPB * k - TPB)
                        turn(k - 1, 0)
                    if heads:
                        scores(k, 3)
                    if rest:
                        turn(k - 2, 1)
                    if heads:
                        values(k, 2)
                    if ffn:
                        for n in range(4):
                            if n == 1 and rest:
                                pe.wait_ge(lnT_ready[1], k - 1)
                            up(k - 1, n)
                    if heads:
                        values(k, 3)

                steps(pe, body)


def rope_tables(dve, sc, kw, qw, kcos, ksin, qcos, qsin, loads, done):
    for ready in loads:
        dve.wait_ge(*ready)
    for cosw, sinw, w, t0, n in ((kcos, ksin, kw, 0, 2 * TILES), (qcos, qsin, qw, TILES, TILES)):
        for half in range(2):
            here = slice(half * ROT, (half + 1) * ROT)
            other = slice((1 - half) * ROT, (2 - half) * ROT)
            dve.tensor_tensor(cosw[:, :, here], sc[:, 1, t0:t0 + n, :],
                              w[:, here].unsqueeze(1).to_broadcast([P, n, ROT]), ALU.mult).then_inc(done, 1)
            if half == 0:
                dve.scalar_tensor_tensor(out=sinw[:, :, here], in0=sc[:, 0, t0:t0 + n, :], scalar=-1.0,
                                         in1=w[:, other].unsqueeze(1).to_broadcast([P, n, ROT]),
                                         op0=ALU.mult, op1=ALU.mult).then_inc(done, 1)
            else:
                dve.tensor_tensor(sinw[:, :, here], sc[:, 0, t0:t0 + n, :],
                                  w[:, other].unsqueeze(1).to_broadcast([P, n, ROT]), ALU.mult).then_inc(done, 1)
    dve.wait_ge(done, 8)


def gqa_attention(nc, t, X, lnT, wq, wk, wv, wo, kcos, ksin, qcos, qsin, gains, const, ident, loads, sc, kw, qw,
                  rope_loads, load_gate):
    ROPES = KT_TILES + TPB * KV_HEADS
    UNITS = TPB * HEADS
    PAIRS = UNITS // 2
    with ExitStack() as st:
        m = Memory(nc, st)
        kvT = m.sb("c_kvT", [P, DC, KEYS])
        raw = m.sb("c_raw", [P, 2, 512])
        sq = m.sb("c_sq", [P, 512])
        t1 = m.sb("c_t1", [P, 512])
        t2 = m.sb("c_t2", [P, 512])
        y = m.sb("c_y", [P, 2, 512])
        ss = m.sb("c_ss", [P, ROPES, REP])
        ve = m.sb("c_ve", [P, ROPES, REP])
        rn = m.sb("c_rn", [P, ROPES, REP])
        scale = m.sb("c_scale", [P, UNITS])
        KT = m.sb("c_KT", [P, KV_HEADS, KEYS])
        qT = m.sb("c_qT", [P, TPB, HEADS, P])
        Vh = m.sb("c_Vh", [P, KT_TILES, KV_HEADS * HD], F32R)
        Vl = m.sb("c_Vl", [P, KT_TILES, KV_HEADS * HD], F32R)
        probs = m.sb("c_probs", [P, 3, KEYS])
        PTh = m.sb("c_PTh", [P, 2, KT_TILES, 2, P], F32R)
        PTl = m.sb("c_PTl", [P, 2, KT_TILES, 2, P], F32R)
        attnT = m.sb("c_attnT", [P, 4, P])
        nmax = m.sb("c_nmax", [P, UNITS])
        bias = m.sb("c_bias", [P, UNITS])
        total = m.sb("c_total", [P, UNITS])
        inv = m.sb("c_inv", [P, UNITS])
        sps = m.ps("c_sps", 3)
        tps = m.ps("c_tps", 2)
        ops = m.ps("c_ops", 2)
        wps = m.ps("c_wps", 1)
        tables_done = m.sem("c_tables_done")
        names = ("ctx_in ln_copied proj_done raw_done squared summed products roped ve_done rn_done scaled "
                 "turned stored v_done v_stored scale_done s_done max_done bias_done exp_done inv_done normed "
                 "pt_turned pt_high pt_low v_low pv_done at_stored wo_done x_done k_stored").split()
        (ctx_in, ln_copied, proj_done, raw_done, squared, summed, products, roped, ve_done, rn_done, scaled,
         turned, stored, v_done, v_stored, scale_done, s_done, max_done, bias_done, exp_done, inv_done, normed,
         pt_turned, pt_high, pt_low, v_low, pv_done, at_stored, wo_done, x_done, k_stored) = (m.sem("c_" + n) for n in names)
        with nc.Block() as block:
            @block.sync
            def _(sp):
                for b in range(B):
                    if b == 1:
                        load_gate(sp)
                    wait_for(sp, proj_done, ROPES * b)
                    wait_for(sp, v_done, KT_TILES * b)
                    sp.dma_start(kvT[:, :, 0:S_LEN],
                                 t["ctxT"].rearrange("(c p) s -> p c s", p=P)[:, :, bass.ds(b * S_LEN, S_LEN)]
                                 ).then_inc(ctx_in, 16)

            @block.gpsimd
            def _(pool):
                for b in range(B):
                    wait_for(pool, proj_done, ROPES * b)
                    wait_for(pool, v_done, KT_TILES * b)
                    pool.tensor_scalar(kvT[:, :, S_LEN:KEYS], lnT[:, :, bass.ds(b * S_LEN, S_LEN)], 1.0, 1.0,
                                       ALU.mult, ALU.mult).then_inc(ln_copied, 1)
                    for r in range(ROPES):
                        pool.wait_ge(summed, ROPES * b + r + 1)
                        pool.tensor_scalar(ve[:, r, :], ss[:, r, :], 1.0 / HD, EPS, ALU.mult,
                                           ALU.add).then_inc(ve_done, 1)
                        pool.wait_ge(ve_done, ROPES * b + r + 1)
                        pool.tensor_tensor(rn[:, r, :], ve[:, r, :], const[:, C_NEGHALF:C_NEGHALF + REP],
                                           ALU.pow).then_inc(rn_done, 1)
                        if r < KT_TILES:
                            pool.wait_ge(rn_done, ROPES * b + r + 1)
                            pool.wait_ge(roped, ROPES * b + r + 1)
                            for k in range(KV_HEADS):
                                last = pool.tensor_scalar(y[:, r % 2, k * HD:(k + 1) * HD],
                                                          y[:, r % 2, k * HD:(k + 1) * HD],
                                                          rn[:, r, k:k + 1], 1.0, ALU.mult, ALU.mult)
                            last.then_inc(scaled, 1)
                    pool.wait_ge(rn_done, ROPES * (b + 1))
                    pool.tensor_scalar(scale[:, :], rn[:, KT_TILES:ROPES, :].rearrange("p r k -> p (r k)"),
                                       float(HD) ** -0.5, 1.0, ALU.mult, ALU.mult).then_inc(scale_done, 1)
                    for i in range(UNITS):
                        pool.wait_ge(inv_done, UNITS * b + i + 1)
                        pool.tensor_scalar(probs[:, i % 3, :], probs[:, i % 3, :], inv[:, i:i + 1], 1.0, ALU.mult,
                                           ALU.mult).then_inc(normed, 1)

            @block.scalar
            def _(act):

                def batch(b):
                    def raw_copy(r):
                        act.wait_ge(proj_done, ROPES * b + r + 1)
                        wait_for(act, roped, ROPES * b + max(r - 1, 0))
                        act.activation(raw[:, r % 2, :], sps[:, r % 3, :], ACT.Copy).then_inc(raw_done, 1)
                        act.wait_ge(raw_done, ROPES * b + r + 1)
                        wait_for(act, summed, ROPES * b + r)
                        act.activation(sq[:, :], raw[:, r % 2, :], ACT.Square).then_inc(squared, 1)

                    def v_copy(k):
                        act.wait_ge(v_done, KT_TILES * b + k + 1)
                        act.activation(Vh[:, k, :], ops[:, k % 2, :], ACT.Copy).then_inc(v_stored, 1)

                    def turned_copy(r):
                        act.wait_ge(turned, ROPES * b + r + 1)
                        src = tps[:, r % 2, :].rearrange("p (k s) -> p k s", k=REP)
                        if r < KT_TILES:
                            act.activation(KT[:, :, r * P:(r + 1) * P], src, ACT.Copy).then_inc(stored, 1)
                        else:
                            qt, n = divmod(r - KT_TILES, KV_HEADS)
                            act.activation(qT[:, qt, n * REP:(n + 1) * REP, :], src, ACT.Copy).then_inc(stored, 1)

                    def exponential(i):
                        act.wait_ge(bias_done, UNITS * b + i + 1)
                        wait_for(act, pt_turned, UNITS * b + max(i - 2, 0))
                        act.activation(probs[:, i % 3, :], sps[:, i % 3, :], ACT.Exp, bias=bias[:, i:i + 1],
                                       scale=scale[:, i:i + 1], accum_out=total[:, i:i + 1]).then_inc(exp_done, 1)

                    def pt_copy(i):
                        act.wait_ge(pt_turned, UNITS * b + i + 1)
                        act.activation(PTh[:, i // 2 % 2, :, i % 2, :],
                                       tps[:, i % 2, :].rearrange("p (k s) -> p k s", k=KT_TILES),
                                       ACT.Copy).then_inc(pt_high, 1)

                    def attn_copy(pair):
                        act.wait_ge(pv_done, PAIRS * b + pair + 1)
                        h = 2 * pair % 4
                        act.activation(attnT[:, h:h + 2, :].rearrange("p h s -> p (h s)"),
                                       ops[:, pair % 2, 0:2 * P], ACT.Copy).then_inc(at_stored, 1)

                    for r in range(ROPES + 2):
                        if r < ROPES:
                            raw_copy(r)
                        if r < KT_TILES:
                            v_copy(r)
                        if r >= 2:
                            turned_copy(r - 2)
                    act.wait_ge(scale_done, b + 1)
                    for i in range(UNITS + 6):
                        if i < UNITS:
                            exponential(i)
                        if 2 <= i < UNITS + 2:
                            pt_copy(i - 2)
                        if i >= 7 and i % 2 == 1:
                            attn_copy((i - 7) // 2)

                first_then_loop(act, B, batch)

            @block.vector
            def _(dve):

                def batch(b):
                    def rope(r):
                        if r < KT_TILES:
                            tile = (b * TPB + r) if r < TPB else (TILES + b * TPB + r - TPB)
                            cosw, sinw = kcos[:, tile, :], ksin[:, tile, :]
                        else:
                            tile = b * TPB + (r - KT_TILES) // KV_HEADS
                            cosw, sinw = qcos[:, tile, :], qsin[:, tile, :]
                        src = raw[:, r % 2, :].rearrange("p (k d) -> p k d", k=REP)
                        dve.wait_ge(squared, ROPES * b + r + 1)
                        dve.tensor_reduce(ss[:, r, :], sq[:, :].rearrange("p (k d) -> p k d", k=REP), AX.X,
                                          ALU.add).then_inc(summed, 1)
                        dve.wait_ge(raw_done, ROPES * b + r + 1)
                        wait_for(dve, roped, ROPES * b + r)
                        dve.tensor_tensor(t1[:, :].rearrange("p (k d) -> p k d", k=REP), src,
                                          cosw.unsqueeze(1).to_broadcast([P, REP, HD]),
                                          ALU.mult).then_inc(products, 1)
                        for half in range(2):
                            here = slice(half * ROT, (half + 1) * ROT)
                            other = slice((1 - half) * ROT, (2 - half) * ROT)
                            dve.tensor_tensor(t2[:, :].rearrange("p (k d) -> p k d", k=REP)[:, :, here],
                                              src[:, :, other],
                                              sinw[:, here].unsqueeze(1).to_broadcast([P, REP, ROT]),
                                              ALU.mult).then_inc(products, 1)
                        dve.wait_ge(products, 3 * (ROPES * b + r + 1))
                        wait_for(dve, turned, ROPES * b + max(r - 1, 0))
                        dve.tensor_tensor(y[:, r % 2, :], t1[:, :], t2[:, :], ALU.add).then_inc(roped, 1)

                    def maximum(i):
                        dve.wait_ge(s_done, UNITS * b + i + 1)
                        dve.tensor_reduce(nmax[:, i:i + 1], sps[:, i % 3, :], AX.X, ALU.max,
                                          negate=True).then_inc(max_done, 1)
                        dve.wait_ge(max_done, UNITS * b + i + 1)
                        dve.tensor_tensor(bias[:, i:i + 1], nmax[:, i:i + 1], scale[:, i:i + 1],
                                          ALU.mult).then_inc(bias_done, 1)

                    def inverse(i):
                        dve.wait_ge(exp_done, UNITS * b + i + 1)
                        dve.reciprocal(inv[:, i:i + 1], total[:, i:i + 1]).then_inc(inv_done, 1)

                    def pt_low_part(i):
                        dve.wait_ge(pt_high, UNITS * b + i + 1)
                        high = PTh[:, i // 2 % 2, :, i % 2, :].bitcast(F32)
                        dve.tensor_tensor(PTl[:, i // 2 % 2, :, i % 2, :],
                                          tps[:, i % 2, :].rearrange("p (k s) -> p k s", k=KT_TILES), high,
                                          ALU.subtract).then_inc(pt_low, 1)

                    def v_low_part(k):
                        dve.wait_ge(v_stored, KT_TILES * b + k + 1)
                        dve.tensor_tensor(Vl[:, k, :], ops[:, k % 2, :], Vh[:, k, :].bitcast(F32),
                                          ALU.subtract).then_inc(v_low, 1)

                    def add_x(qt):
                        dve.wait_ge(wo_done, TPB * b + qt + 1)
                        dve.scalar_tensor_tensor(out=X[:, b * TPB + qt, :], in0=wps[:, 0, 0:D],
                                                 scalar=gains[:, 1:2], in1=X[:, b * TPB + qt, :],
                                                 op0=ALU.mult, op1=ALU.add).then_inc(x_done, 1)

                    for r in range(ROPES):
                        rope(r)
                        if r < KT_TILES:
                            v_low_part(r)
                    dve.wait_ge(scale_done, b + 1)
                    for i in range(UNITS + 3):
                        if i < UNITS:
                            maximum(i)
                        if 1 <= i <= UNITS:
                            inverse(i - 1)
                        if i >= 3:
                            pt_low_part(i - 3)
                        if i == HEADS + 7:
                            add_x(0)
                    add_x(1)

                rope_tables(dve, sc, kw, qw, kcos, ksin, qcos, qsin, rope_loads, tables_done)
                first_then_loop(dve, B, batch)

            @block.tensor
            def _(pe):
                for ready in loads:
                    pe.wait_ge(*ready)

                def batch(b):
                    def project(r):
                        wait_for(pe, exp_done, UNITS * b)
                        wait_for(pe, raw_done, ROPES * b + max(r - 2, 0))
                        for c in range(DC):
                            if r < KT_TILES:
                                tok, w = r, wk[:, c, :]
                            else:
                                qt, n = divmod(r - KT_TILES, KV_HEADS)
                                tok, w = TPB + qt, wq[:, c, n * 512:(n + 1) * 512]
                            last = pe.matmul(sps[:, r % 3, :], kvT[:, c, tok * P:(tok + 1) * P], w,
                                             start=(c == 0), stop=(c == DC - 1))
                        last.then_inc(proj_done, 1)

                    def project_v(k):
                        wait_for(pe, v_low, KT_TILES * b + max(k - 1, 0))
                        for c in range(DC):
                            last = pe.matmul(ops[:, k % 2, :], kvT[:, c, k * P:(k + 1) * P], wv[:, c, :],
                                             start=(c == 0), stop=(c == DC - 1))
                        last.then_inc(v_done, 1)

                    def turn(r):
                        if r < KT_TILES:
                            pe.wait_ge(scaled, KT_TILES * b + r + 1)
                        else:
                            pe.wait_ge(roped, ROPES * b + r + 1)
                        wait_for(pe, stored, ROPES * b + max(r - 1, 0))
                        for k in range(REP):
                            last = pe.transpose(tps[:, r % 2, k * P:(k + 1) * P], y[:, r % 2, k * HD:(k + 1) * HD],
                                                ident)
                        last.then_inc(turned, 1)

                    def scores(i):
                        qt, hd = divmod(i, HEADS)
                        if i < 3:
                            pe.wait_ge(stored, ROPES * (b + 1))
                        wait_for(pe, exp_done, UNITS * b + max(i - 2, 0))
                        pe.matmul(sps[:, i % 3, :], qT[:, qt, hd, :], KT[:, hd // REP, :], start=True,
                                  stop=True).then_inc(s_done, 1)

                    def turn_probs(i):
                        pe.wait_ge(normed, UNITS * b + i + 1)
                        wait_for(pe, pt_low, UNITS * b + max(i - 1, 0))
                        for k in range(KT_TILES):
                            last = pe.transpose(tps[:, i % 2, k * P:(k + 1) * P],
                                                probs[:, i % 3, k * P:(k + 1) * P], ident)
                        last.then_inc(pt_turned, 1)

                    def values(pair, half):
                        if half == 0:
                            pe.wait_ge(pt_low, UNITS * b + 2 * pair + 2)
                            wait_for(pe, at_stored, PAIRS * b + max(pair - 1, 0))
                        kv = 2 * pair % HEADS // REP
                        for k in range(2 * half, 2 * half + 2):
                            for n, (v, pt) in enumerate(((Vh, PTh), (Vh, PTl), (Vl, PTh))):
                                last = pe.matmul(ops[:, pair % 2, 0:2 * P], v[:, k, kv * HD:(kv + 1) * HD],
                                                 pt[:, pair % 2, k, :, :].rearrange("p h s -> p (h s)"),
                                                 start=(k == 0 and n == 0), stop=(k == KT_TILES - 1 and n == 2))
                        if half == 1:
                            last.then_inc(pv_done, 1)

                    def output(j):
                        qt, h = divmod(j, HEADS)
                        if h % 2 == 0:
                            pe.wait_ge(at_stored, PAIRS * b + j // 2 + 1)
                        if h == 0:
                            wait_for(pe, x_done, TPB * b + qt)
                        last = pe.matmul(wps[:, 0, 0:D], attnT[:, h % 4, :], wo[:, h, :], start=(h == 0),
                                         stop=(h == HEADS - 1))
                        if h == HEADS - 1:
                            last.then_inc(wo_done, 1)

                    pe.wait_ge(ctx_in, 16 * b + 16)
                    pe.wait_ge(ln_copied, b + 1)
                    for r in range(ROPES + 2):
                        if r < ROPES:
                            project(r)
                        if r < KT_TILES:
                            project_v(r)
                        if r >= 2:
                            turn(r - 2)
                    pe.wait_ge(v_low, KT_TILES * (b + 1))
                    for i in range(UNITS + 8):
                        if i < UNITS:
                            scores(i)
                        if 5 <= i < UNITS + 5:
                            values((i - 5) // 2, (i - 5) % 2)
                        if 2 <= i < UNITS + 2:
                            turn_probs(i - 2)
                        if i >= 8:
                            output(i - 8)

                first_then_loop(pe, B, batch)


def route(nc, lps, logits_done, ln, slot, expert, sorted_x, const, zeroed):
    with ExitStack() as st:
        m = Memory(nc, st)
        logits = m.sb("e_logits", [P, TILES, EXPERTS])
        best = m.sb("e_best", [P, TILES])
        first = m.sb("e_first", [P, TILES])
        cand = m.sb("e_cand", [P, TILES, EXPERTS])
        hot = m.sb("e_hot", [P, TILES, EXPERTS])
        count = m.sb("e_count", [P, TILES, EXPERTS])
        before = m.sb("e_before", [P, TILES + 1, EXPERTS])
        tiles = m.sb("e_tiles", [P, EXPERTS])
        ends = m.sb("e_ends", [P, EXPERTS])
        base = m.sb("e_base", [P, EXPERTS])
        where = m.sb("e_where", [P, TILES, EXPERTS])
        slotf = m.sb("e_slotf", [P, TILES])
        over = m.sb("e_over", [1, SLOT_TILES, EXPERTS])
        expf = m.sb("e_expf", [1, SLOT_TILES])
        rps = m.ps("e_rps", 1)
        cps = m.ps("e_cps", 1)
        step = m.sem("e_step")
        hot_done = m.sem("e_hot_done")
        ranked = m.sem("e_ranked")
        slots_done = m.sem("e_slots_done")
        scattered = m.sem("e_scattered")
        ids = const[:, C_EXP:C_EXP + EXPERTS]
        all_tiles = [P, TILES, EXPERTS]
        with nc.Block() as block:
            @block.tensor
            def _(pe):
                pe.wait_ge(hot_done, 1)
                hot2 = hot[:, :, :].rearrange("p t e -> p (t e)")
                pe.matmul(rps[:, 0, 0:TILES * EXPERTS], const[:, C_TRI:C_TRI + P], hot2, start=True, stop=True)
                pe.matmul(cps[:, 0, 0:TILES * EXPERTS], const[:, C_ONES:C_ONES + P], hot2, start=True,
                          stop=True).then_inc(ranked, 1)

            @block.vector
            def _(dve):
                n = 0

                def after(ins):
                    nonlocal n
                    ins.then_inc(step, 1)
                    n += 1
                    dve.wait_ge(step, n)

                dve.wait_ge(logits_done, 1)
                after(dve.tensor_copy(logits[:, :, :].rearrange("p t e -> p (t e)"),
                                      lps[:, 0, 0:TILES * EXPERTS]))
                after(dve.tensor_reduce(best[:, :], logits[:, :, :], AX.X, ALU.max))
                after(dve.tensor_tensor(cand[:, :, :], logits[:, :, :], best[:, :].unsqueeze(2).to_broadcast(all_tiles),
                                        ALU.is_equal))
                after(dve.tensor_scalar(base[:, :], ids, float(-EXPERTS), None, ALU.add))
                after(dve.tensor_tensor(cand[:, :, :], cand[:, :, :], base[:, :].unsqueeze(1).to_broadcast(all_tiles),
                                        ALU.mult))
                after(dve.tensor_reduce(first[:, :], cand[:, :, :], AX.X, ALU.min))
                dve.tensor_tensor(hot[:, :, :], first[:, :].unsqueeze(2).to_broadcast(all_tiles),
                                  base[:, :].unsqueeze(1).to_broadcast(all_tiles),
                                  ALU.is_equal).then_inc(hot_done, 1)
                dve.wait_ge(ranked, 1)
                after(dve.tensor_copy(count[:, :, :].rearrange("p t e -> p (t e)"),
                                      cps[:, 0, 0:TILES * EXPERTS]))
                after(dve.memset(before[:, 0, :], 0.0))
                for t in range(TILES):
                    after(dve.tensor_tensor(before[:, t + 1, :], before[:, t, :], count[:, t, :], ALU.add))
                after(dve.tensor_scalar(tiles[:, :], before[:, TILES, :], 1.0 / P, 0.5 - 1.0 / (2 * P), ALU.mult,
                                        ALU.add))
                after(dve.tensor_scalar(tiles[:, :], tiles[:, :], ROUND, None, ALU.add))
                after(dve.tensor_scalar(tiles[:, :], tiles[:, :], ROUND, None, ALU.subtract))
                after(dve.tensor_tensor_scan(ends[:, :], const[:, C_ONES:C_ONES + EXPERTS], tiles[:, :], 0.0,
                                             ALU.mult, ALU.add))
                after(dve.tensor_tensor(base[:, :], ends[:, :], tiles[:, :], ALU.subtract))
                after(dve.tensor_scalar(base[:, :], base[:, :], float(P), None, ALU.mult))
                after(dve.tensor_tensor(where[:, :, :].rearrange("p t e -> p (t e)"), rps[:, 0, 0:TILES * EXPERTS],
                                        before[:, 0:TILES, :].rearrange("p t e -> p (t e)"), ALU.add))
                after(dve.tensor_tensor(where[:, :, :], where[:, :, :], base[:, :].unsqueeze(1).to_broadcast(all_tiles),
                                        ALU.add))
                after(dve.tensor_tensor(where[:, :, :], where[:, :, :], hot[:, :, :], ALU.mult))
                after(dve.tensor_reduce(slotf[:, :], where[:, :, :], AX.X, ALU.add))
                dve.tensor_copy(slot[:, :], slotf[:, :]).then_inc(slots_done, 1)
                shape = [1, SLOT_TILES, EXPERTS]
                after(dve.tensor_tensor(over[:, :, :], ends[0:1, :].unsqueeze(1).to_broadcast(shape),
                                        const[0:1, C_TILE:C_TILE + SLOT_TILES].unsqueeze(2).to_broadcast(shape),
                                        ALU.is_le))
                after(dve.tensor_reduce(expf[:, :], over[:, :, :], AX.X, ALU.add))
                after(dve.tensor_scalar(expert[:, :], expf[:, :], float(EXPERTS - 1), None, ALU.min))

            @block.gpsimd
            def _(pool):
                pool.wait_ge(slots_done, 1)
                pool.wait_ge(*zeroed)
                for t in range(TILES):
                    pool.indirect_dma_start(sorted_x, bass.IndirectOffsetOnAxis(slot[:, t:t + 1], 0),
                                            ln[:, t, :], None).then_inc(scattered, 16)
                pool.wait_ge(scattered, 16 * TILES)


def experts(nc, X, gate, up, down, expert, slot, sorted_x, sorted_y, gains, ident, out, loads):
    LAST = SLOT_TILES - 1
    assert LAST % 2 == 0
    with ExitStack() as st:
        m = Memory(nc, st)
        xs = m.sb("g_xs", [P, 2, D])
        xT = m.sb("g_xT", [P, 2, DC, P])
        act_g = m.sb("g_act", [P, 2, INNER])
        h = m.sb("g_h", [P, 2, INNER])
        hT = m.sb("g_hT", [P, 2, IC, P])
        ys = m.sb("g_ys", [P, 2, D])
        yg = m.sb("g_yg", [P, TILES, D])
        xps = m.ps("g_xps", 1)
        gps = m.ps("g_gps", 2)
        ups = m.ps("g_ups", 2)
        hps = m.ps("g_hps", 1)
        yps = m.ps("g_yps", 2)
        xs_in = [m.sem(f"g_xs_in{k}") for k in range(2)]
        x_turned = m.sem("g_x_turned")
        x_stored = m.sem("g_x_stored")
        g_done = m.sem("g_g_done")
        u_done = m.sem("g_u_done")
        silu_done = m.sem("g_silu_done")
        h_done = m.sem("g_h_done")
        h_turned = m.sem("g_h_turned")
        h_stored = m.sem("g_h_stored")
        y_done = m.sem("g_y_done")
        y_copied = m.sem("g_y_copied")
        y_out = [m.sem(f"g_y_out{k}") for k in range(2)]
        gathered = [m.sem(f"g_gathered{k}") for k in range(TILES)]
        x_done = m.sem("g_x_done")
        stored = m.sem("g_stored")
        with nc.Block() as block:
            @block.sync
            def _(sp):
                def load(i, par, rnd):
                    if rnd is not None:
                        wait_for(sp, x_turned, i - 1)
                    sp.dma_start(xs[:, par, :], sorted_x[bass.ds(i * P, P), :]).then_inc(xs_in[par], 16)

                def store(i, par):
                    sp.wait_ge(y_copied, i + 1)
                    sp.dma_start(sorted_y[bass.ds(i * P, P), :], ys[:, par, :]).then_inc(y_out[par], 16)

                load(0, 0, None)
                load(1, 1, None)
                for j in range(LAST // 2 - 1):
                    for par in range(2):
                        load(2 * j + par + 2, par, j)
                        store(2 * j + par, par)
                load(LAST, 0, 0)
                store(LAST - 2, 0)
                store(LAST - 1, 1)
                store(LAST, 0)
                for par in range(2):
                    sp.wait_ge(y_out[par], 16 * ((SLOT_TILES + 1 - par) // 2))
                sp.sem_inc(y_copied, 1)
                for t in range(TILES):
                    sp.wait_ge(x_done, t + 1)
                    sp.dma_start(out[t * P:(t + 1) * P, :], X[:, t, :]).then_inc(stored, 16)
                sp.wait_ge(stored, 16 * TILES)

            @block.tensor
            def _(pe):
                for ready in loads:
                    pe.wait_ge(*ready)

                def turn_x(i, par, rnd):
                    pe.wait_ge(xs_in[par], 16 * rnd + 16)
                    wait_for(pe, x_stored, i)
                    for c in range(DC):
                        last = pe.transpose(xps[:, 0, c * P:(c + 1) * P], xs[:, par, c * P:(c + 1) * P], ident)
                    last.then_inc(x_turned, 1)

                def project(i, par, w, banks, done):
                    e = pe.value_load(expert[0:1, bass.ds(i, 1)], min_val=0, max_val=EXPERTS - 1)
                    for c in range(DC):
                        last = pe.matmul(banks[:, par, :], xT[:, par, c, :], w[:, c, bass.ds(e * INNER, INNER)],
                                         start=(c == 0), stop=(c == DC - 1))
                    last.then_inc(done, 1)

                def turn_h(i, par):
                    pe.wait_ge(h_done, i + 1)
                    wait_for(pe, h_stored, i)
                    for c in range(IC):
                        last = pe.transpose(hps[:, 0, c * P:(c + 1) * P], h[:, par, c * P:(c + 1) * P], ident)
                    last.then_inc(h_turned, 1)

                def down_proj(i, par):
                    e = pe.value_load(expert[0:1, bass.ds(i, 1)], min_val=0, max_val=EXPERTS - 1)
                    pe.wait_ge(h_stored, i + 1)
                    wait_for(pe, y_copied, i)
                    for c in range(IC):
                        last = pe.matmul(yps[:, par, 0:D], hT[:, par, c, :], down[:, c, bass.ds(e * D, D)],
                                         start=(c == 0), stop=(c == IC - 1))
                    last.then_inc(y_done, 1)

                def ahead(i, par, rnd, turn_next):
                    pe.wait_ge(x_stored, i + 2)
                    project(i + 1, 1 - par, gate, gps, g_done)
                    turn_h(i, par)
                    project(i + 1, 1 - par, up, ups, u_done)
                    down_proj(i, par)
                    if turn_next:
                        turn_x(i + 2, par, rnd + 1)

                turn_x(0, 0, 0)
                turn_x(1, 1, 0)
                pe.wait_ge(x_stored, 1)
                project(0, 0, gate, gps, g_done)
                project(0, 0, up, ups, u_done)

                def pair(j):
                    for par in range(2):
                        ahead(2 * j + par, par, j, True)

                first_then_loop(pe, LAST // 2 - 1, pair)
                ahead(LAST - 2, 0, LAST // 2 - 1, True)
                ahead(LAST - 1, 1, LAST // 2 - 1, False)
                turn_h(LAST, 0)
                down_proj(LAST, 0)

            @block.scalar
            def _(act):
                def copy_x(i, par):
                    act.wait_ge(x_turned, i + 1)
                    act.activation(xT[:, par, :, :], xps[:, 0, 0:D].rearrange("p (c s) -> p c s", c=DC),
                                   ACT.Copy).then_inc(x_stored, 1)

                def silu(i, par):
                    if not (isinstance(i, int) and i < 2):
                        act.wait_ge(h_done, i - 1)
                    act.wait_ge(g_done, i + 1)
                    act.activation(act_g[:, par, :], gps[:, par, :], ACT.Silu).then_inc(silu_done, 1)

                copy_x(0, 0)
                copy_x(1, 1)
                silu(0, 0)
                silu(1, 1)

                def pair(j):
                    for par in range(2):
                        copy_x(2 * j + par + 2, par)
                        silu(2 * j + par + 2, par)

                first_then_loop(act, LAST // 2 - 1, pair)
                copy_x(LAST, 0)
                silu(LAST, 0)

            @block.vector
            def _(dve):
                def copy_h(i, par):
                    dve.wait_ge(h_turned, i + 1)
                    dve.tensor_copy(hT[:, par, :, :].rearrange("p c s -> p (c s)"), hps[:, 0, :]).then_inc(h_stored, 1)

                def copy_y(i, par):
                    dve.wait_ge(y_done, i + 1)
                    dve.tensor_copy(ys[:, par, :], yps[:, par, 0:D]).then_inc(y_copied, 1)

                def product(i, par):
                    dve.wait_ge(silu_done, i + 1)
                    dve.wait_ge(u_done, i + 1)
                    dve.tensor_tensor(h[:, par, :], act_g[:, par, :], ups[:, par, :], ALU.mult).then_inc(h_done, 1)

                product(0, 0)
                for i in range(2):
                    copy_h(i, i)
                    product(i + 1, 1 - i)
                    copy_y(i, i)
                with dve.Fori(1, LAST // 2) as j:
                    for par in range(2):
                        copy_h(2 * j + par, par)
                        product(2 * j + par + 1, 1 - par)
                        dve.wait_ge(y_out[par], 16 * j)
                        copy_y(2 * j + par, par)
                copy_h(LAST, 0)
                dve.wait_ge(y_out[0], 16 * (LAST // 2))
                copy_y(LAST, 0)
                for t in range(TILES):
                    dve.wait_ge(gathered[t], 16)
                    dve.scalar_tensor_tensor(out=X[:, t, :], in0=yg[:, t, :], scalar=gains[:, 3:4], in1=X[:, t, :],
                                             op0=ALU.mult, op1=ALU.add).then_inc(x_done, 1)

            @block.gpsimd
            def _(pool):
                pool.wait_ge(y_copied, SLOT_TILES + 1)
                for t in range(TILES):
                    pool.indirect_dma_start(yg[:, t, :], None, sorted_y,
                                            bass.IndirectOffsetOnAxis(slot[:, t:t + 1], 0)).then_inc(gathered[t], 16)


def flamingo(nc, t, out):
    with ExitStack() as stack:
        mem = Memory(nc, stack)
        X = mem.sb("X", [P, TILES, D])
        const = mem.sb("const", [P, C_WIDE])
        gains = mem.sb("gains", [P, 4])
        ident = const[:, C_IDENT:C_IDENT + P]
        x_in = mem.sem("x_in")
        const_in = mem.sem("const_in")
        gains_in = mem.sem("gains_in")
        sorted_x = nc.dram_tensor("sorted_x", (SLOTS, D), F32, kind="Internal").ap()
        sorted_y = nc.dram_tensor("sorted_y", (SLOTS, D), F32, kind="Internal").ap()

        shared = mem.sb("shared", [P, DC * EXPERTS * INNER])
        lnT = shared[:, 0:DC * TOK].rearrange("p (c s) -> p c s", c=DC)
        ctxT = shared[:, DC * TOK:2 * DC * TOK].rearrange("p (c s) -> p c s", c=DC)
        ctx = shared[:, 2 * DC * TOK:3 * DC * TOK].rearrange("p (t d) -> p t d", t=TILES)
        w1 = shared[:, 3 * DC * TOK:3 * DC * TOK + DC * FF].rearrange("p (c f) -> p c f", c=DC)
        gate = shared[:, :].rearrange("p (c n) -> p c n", c=DC)
        gate_in = mem.sem("expert_gate_in")

        aw = stack.enter_context(ExitStack())
        wq = Memory(nc, aw).sb("wq", [P, DC, HEADS * HD])
        wk = Memory(nc, aw).sb("wk", [P, DC, KV_HEADS * HD])
        wv = Memory(nc, aw).sb("wv", [P, DC, KV_HEADS * HD])
        wo = Memory(nc, aw).sb("wo", [P, HEADS, D])
        wq_in = mem.sem("wq_in")
        wk_in = mem.sem("wk_in")
        wv_in = mem.sem("wv_in")
        wo_in = mem.sem("wo_in")
        pos = Memory(nc, aw).sb("pos", [P, 2 * TILES], I32)
        kw = Memory(nc, aw).sb("kw", [P, HD])
        qw = Memory(nc, aw).sb("qw", [P, HD])
        sc = Memory(nc, aw).sb("sc", [P, 2, 2 * TILES, ROT])
        pos_in = mem.sem("pos_in")
        kw_in = mem.sem("kw_in")
        qw_in = mem.sem("qw_in")
        lnT2 = Memory(nc, aw).sb("lnT2", [P, DC, TOK])
        fw = stack.enter_context(ExitStack())
        w2 = Memory(nc, fw).sb("w2", [P, FC, D])
        w1_in = mem.sem("w1_in")
        w2_in = mem.sem("w2_in")

        with ExitStack() as lstm:
            m = Memory(nc, lstm)
            gate_w = m.sb("gate_w", [P, 3 * DC, 32])
            gate_b = m.sb("gate_b", [32, 1])
            selr = m.sb("selr", [32, M_HEADS * P], F32R)
            scale_row = m.sb("scale_row", [P, D])
            cols = m.sb("cols", [P, B, 4, 32])
            Gr = m.sb("Gr", [32, TOK], F32R)
            Mr = m.sb("Mr", [32, TOK], F32R)
            rows = lstm.enter_context(ExitStack())
            sel = Memory(nc, rows).sb("sel", [32, M_HEADS * P])
            ctx_in = m.sem("ctx_in")
            ctxT_in = m.sem("ctxT_in")
            gate_in = m.sem("gate_in")
            bias_in = m.sem("bias_in")
            sel_in = m.sem("sel_in")
            scale_in = m.sem("scale_in")
            tanh_done = m.sem("tanh_done")
            with nc.Block() as block:
                @block.sync
                def _(sp):
                    sp.dma_start(X[:, :, :], t["x"].rearrange("(t p) d -> p t d", p=P)).then_inc(x_in, 16)
                    sp.dma_start(const[:, :], t["const"]).then_inc(const_in, 16)
                    sp.dma_start(ctxT[:, :, :], t["ctxT"].rearrange("(c p) s -> p c s", p=P)).then_inc(ctxT_in, 16)
                    sp.dma_start(gate_w[:, :, :], t["gate_w"].rearrange("(c p) n -> p c n", p=P)).then_inc(gate_in, 16)
                    sp.dma_start(gate_b[:, :], t["gate_b"]).then_inc(bias_in, 16)
                    sp.dma_start(sel[:, :], t["sel"]).then_inc(sel_in, 16)
                    sp.dma_start(ctx[:, :, :], t["ctx"].rearrange("(t p) d -> p t d", p=P)).then_inc(ctx_in, 16)
                    sp.dma_start(w1[:, :, :], t["w1T"].rearrange("(c p) f -> p c f", p=P)).then_inc(w1_in, 16)
                    sp.dma_start(w2[:, :, :], t["w2T"].rearrange("(c p) d -> p c d", p=P)).then_inc(w2_in, 16)
                    sp.dma_start(wk[:, :, :], t["wkT"].rearrange("(c p) n -> p c n", p=P)).then_inc(wk_in, 16)
                    sp.dma_start(wv[:, :, :], t["wvT"].rearrange("(c p) n -> p c n", p=P)).then_inc(wv_in, 16)
                    sp.dma_start(wq[:, :, :], t["wqT"].rearrange("(c p) n -> p c n", p=P)).then_inc(wq_in, 16)
                    sp.dma_start(wo[:, :, :], t["woT"].rearrange("(h p) n -> p h n", p=P)).then_inc(wo_in, 16)

                @block.scalar
                def _(act):
                    act.dma_start(gains[:, :], t["gains"].partition_broadcast(P)).then_inc(gains_in, 16)
                    act.dma_start(scale_row[:, :], t["ln_scale"].partition_broadcast(P)).then_inc(scale_in, 16)
                    act.dma_start(pos[:, :], t["pos"]).then_inc(pos_in, 16)
                    act.dma_start(kw[:, :], t["k_norm"].partition_broadcast(P)).then_inc(kw_in, 16)
                    act.dma_start(qw[:, :], t["q_norm"].partition_broadcast(P)).then_inc(qw_in, 16)
                    act.wait_ge(gains_in, 16)
                    act.activation(gains[:, :], gains[:, :], ACT.Tanh).then_inc(tanh_done, 1)

                @block.vector
                def _(dve):
                    dve.wait_ge(scale_in, 16)
                    dve.wait_ge(tanh_done, 1)
                    dve.tensor_scalar(scale_row[:, :], scale_row[:, :], gains[:, 0:1], None, ALU.mult)
            layernorm_transposed(nc, "l0", X, lnT, ident, const, (const_in, 16), (x_in, 16))
            mlstm_rows(nc, m, lnT, ctxT, gate_w, gate_b, sel, const, cols, Gr, Mr, selr, ident,
                       [(ctxT_in, 16), (gate_in, 16), (bias_in, 16), (sel_in, 16), (ctx_in, 16), (const_in, 16)])
            rows.close()
            mlstm_and_ffn(nc, X, lnT, ctx, ctxT, cols, Gr, Mr, selr, scale_row, const, ident, w1, w2, gains,
                          lnT2, [(w1_in, 16), (w2_in, 16)], pos, (pos_in, 16), sc)
        fw.close()

        with ExitStack() as attn:
            m = Memory(nc, attn)
            kcos = m.sb("kcos", [P, 2 * TILES, HD])
            ksin = m.sb("ksin", [P, 2 * TILES, HD])
            qcos = m.sb("qcos", [P, TILES, HD])
            qsin = m.sb("qsin", [P, TILES, HD])

            def load_gate(sp):
                for e in range(EXPERTS):
                    sp.dma_start(gate[:, :, e * INNER:(e + 1) * INNER],
                                 t["gate"][e].rearrange("(c p) i -> p c i", p=P)).then_inc(gate_in, 16)

            gqa_attention(nc, t, X, lnT2, wq, wk, wv, wo, kcos, ksin, qcos, qsin, gains, const, ident,
                          [(wq_in, 16), (wk_in, 16), (wv_in, 16), (wo_in, 16)], sc, kw, qw,
                          [(kw_in, 16), (qw_in, 16)], load_gate)

        aw.close()
        with ExitStack() as moe:
            m = Memory(nc, moe)
            up = m.sb("up", [P, DC, EXPERTS * INNER])
            down = m.sb("down", [P, IC, EXPERTS * D])
            router = m.sb("router", [P, DC, EXPERTS])
            lnT = m.sb("lnT3", [P, DC, TOK])
            ln = m.sb("ln3", [P, TILES, D])
            slot = m.sb("slot", [P, TILES], U32)
            expert = m.sb("expert", [1, SLOT_TILES], I32)
            zero = m.sb("zero", [P, D])
            router_in = m.sem("router_in")
            up_in = m.sem("up_in")
            down_in = m.sem("down_in")
            logits_done = m.sem("logits_done")
            logits_bank = moe.enter_context(ExitStack())
            lps = Memory(nc, logits_bank).ps("e_lps", 1)
            zero_in = m.sem("zero_in")
            zeroed = m.sem("zeroed")
            zero_rows = zero[:, :].unsqueeze(1).to_broadcast([P, SLOT_TILES, D])

            def load_experts(sp):
                sp.dma_start(router[:, :, :], t["router"].rearrange("(c p) e -> p c e", p=P)
                             ).then_inc(router_in, 16)
                sp.dma_start(zero[:, :], t["zero"]).then_inc(zero_in, 16)
                for e in range(EXPERTS):
                    i, d = slice(e * INNER, (e + 1) * INNER), slice(e * D, (e + 1) * D)
                    sp.dma_start(up[:, :, i], t["up"][e].rearrange("(c p) i -> p c i", p=P)
                                 ).then_inc(up_in, 16)
                    sp.dma_start(down[:, :, d], t["down"][e].rearrange("(c p) d -> p c d", p=P)
                                 ).then_inc(down_in, 16)
                    if e == 0:
                        sp.wait_ge(zero_in, 16)
                        sp.dma_start(sorted_x.rearrange("(t p) d -> p t d", p=P), zero_rows).then_inc(zeroed, 16)

            def route_logits(pe, n):
                if n == 0:
                    pe.wait_ge(router_in, 16)
                for c in range(DC):
                    last = pe.matmul(lps[:, 0, n * EXPERTS:(n + 1) * EXPERTS], lnT[:, c, n * P:(n + 1) * P],
                                     router[:, c, :], start=(c == 0), stop=(c == DC - 1))
                if n == TILES - 1:
                    last.then_inc(logits_done, 1)

            layernorm_transposed(nc, "l3", X, lnT, ident, const, kept=ln, meanwhile=load_experts,
                                 follow=route_logits)
            route(nc, lps, logits_done, ln, slot, expert, sorted_x, const, (zeroed, 16))
            logits_bank.close()
            experts(nc, X, gate, up, down, expert, slot, sorted_x, sorted_y, gains, ident, out,
                    [(gate_in, 16 * EXPERTS), (up_in, 16 * EXPERTS), (down_in, 16 * EXPERTS)])


def kernel(**inputs):
    import numpy as _np
    import concourse.bacc as _bacc
    from concourse import mybir as _mybir
    from concourse.bass_utils import run_bass_kernel_spmd as _run

    i = {k: _np.asarray(v) for k, v in inputs.items()}
    const, sel = host_constants()
    laid = {
        "x": i["x"].reshape(TOK, D),
        "ctx": i["ctx_2048"].reshape(TOK, D),
        "ctxT": i["ctx_2048"].reshape(TOK, D).T,
        "const": const,
        "zero": _np.zeros((P, D), _np.float32),
        "sel": sel,
        "gains": _np.concatenate([i["g_xattn"], i["g_ffn"]]),
        "gate_w": _np.concatenate([i["L0_xattn_Wi"], i["L0_xattn_Wf"]], axis=1),
        "gate_b": _np.concatenate([i["L0_xattn_bi"], i["L0_xattn_bf"]])[:, None],
        "pos": _np.concatenate([i["pos_BxS2"].reshape(TILES, P), i["itok_BxS_4096_4607"].reshape(TILES, P)]).T,
        "k_norm": i["L1_xattn_k_norm_w"],
        "q_norm": i["L1_xattn_q_norm_w"],
        "wqT": i["L1_xattn_Wq"].T,
        "wkT": i["L1_xattn_Wk"].T,
        "wvT": i["L1_xattn_Wv"].T,
        "woT": i["L1_xattn_Wo"].T,
        "router": i["L1_ffn_router_w"],
        "gate": i["L1_ffn_gate_w"],
        "up": i["L1_ffn_up_w"],
        "down": i["L1_ffn_down_w"],
        "w1T": i["L0_ffn_W1"].T,
        "w2T": i["L0_ffn_W2"].T,
        "ln_scale": i["L0_xattn_ln_scale"],
    }
    nc = _bacc.Bacc("TRN2", target_bir_lowering=False, num_devices=1)
    arrays, args = {}, {}
    for name, a in laid.items():
        a = _np.ascontiguousarray(a)
        arrays[f"in_{name}"] = a
        args[name] = nc.dram_tensor(f"in_{name}", a.shape, _mybir.dt.from_np(a.dtype), kind="ExternalInput").ap()
    out = nc.dram_tensor("out", (TOK, D), F32, kind="ExternalOutput").ap()
    flamingo(nc, args, out)
    r = _run(nc, [arrays], core_ids=[0])
    return r.results[0]["out"].reshape(B, S_LEN, D)
```

```python
from contextlib import ExitStack

import concourse.bass as bass
from concourse import mybir
from concourse.alu_op_type import AluOpType as ALU
import numpy as np

F32 = mybir.dt.float32
F32R = mybir.dt.float32r
I32 = mybir.dt.int32
U32 = mybir.dt.uint32
ACT = mybir.ActivationFunctionType
AX = mybir.AxisListType

P = 128
B = 4
S_LEN = 256
D = 256
TOK = B * S_LEN
TILES = TOK // P
DC = D // P
TPB = S_LEN // P

M_HEADS = 16
M_DH = D // M_HEADS
HALF = P // M_DH
AUG = M_DH + 1

FF = 1024
FC = FF // P

HEADS = 16
KV_HEADS = 4
HD = 128
REP = HEADS // KV_HEADS
KEYS = 2 * S_LEN
KT_TILES = KEYS // P
ROT = HD // 2

EXPERTS = 8
INNER = 512
IC = INNER // P
SLOT_TILES = (TOK - EXPERTS) // P + EXPERTS
SLOTS = SLOT_TILES * P

LN_EPS = 1e-5
EPS = 1e-6
ROUND = 12582912.0
PI_CLAMP = 3.1415925
TWO_PI = 2.0 * float(np.pi)
PI_HIGH = 6.28125
PI_MID = float(np.round((TWO_PI - PI_HIGH) * 2.0 ** 21) / 2.0 ** 21)
PI_LOW = TWO_PI - PI_HIGH - PI_MID

C_IDENT = 0
C_ONES = C_IDENT + P
C_TRI = C_ONES + P
C_PAR = C_TRI + P
C_BDM = C_PAR + 4
C_SPLIT = C_BDM + HALF * AUG
C_FREQ = C_SPLIT + 2
C_NEGHALF = C_FREQ + ROT
C_TILE = C_NEGHALF + 64
C_EXP = C_TILE + SLOT_TILES
C_WIDE = C_EXP + EXPERTS


def host_constants():
    c = np.zeros((P, C_WIDE), np.float32)
    p = np.arange(P)
    c[:, C_IDENT:C_IDENT + P] = np.eye(P)
    c[:, C_ONES:C_ONES + P] = 1.0
    c[:, C_TRI:C_TRI + P] = p[:, None] < p[None, :]
    for n in range(4):
        c[:, C_PAR + n] = np.where((p // M_DH) % 4 == n, float(M_DH) ** -0.5, 0.0)
    c[:, C_BDM:C_BDM + HALF * AUG] = np.repeat(p[:, None] // M_DH == np.arange(HALF)[None, :], AUG, 1)
    c[:, C_SPLIT] = p % 32 >= 16
    c[:, C_SPLIT + 1] = np.where(p % 32 >= 16, -1.0, 1.0)
    freq = np.float32(1.0) / np.float32(10000.0) ** (np.arange(0, HD, 2, dtype=np.float32) / np.float32(HD))
    c[:, C_FREQ:C_FREQ + ROT] = freq
    c[:, C_NEGHALF:C_NEGHALF + 64] = -0.5
    c[:, C_TILE:C_TILE + SLOT_TILES] = np.arange(SLOT_TILES)
    c[:, C_EXP:C_EXP + EXPERTS] = np.arange(EXPERTS)
    sel = np.zeros((32, M_HEADS, P), np.float32)
    for h in range(M_HEADS):
        sel[h, h] = 1.0
        sel[16 + h, h] = 1.0
    return c, sel.reshape(32, M_HEADS * P)


class Memory:

    def __init__(self, nc, stack):
        self.nc, self.stack = nc, stack

    def sb(self, name, shape, dt=F32):
        return self.stack.enter_context(self.nc.sbuf_tensor(name, shape, dt))

    def ps(self, name, banks):
        return self.stack.enter_context(self.nc.psum_tensor(name, [P, banks, 512], F32))

    def sem(self, name):
        return self.stack.enter_context(self.nc.semaphore(name))


def first_then_loop(eng, n, body):
    body(0)
    with eng.Fori(1, n) as j:
        body(j)


def wait_for(eng, sem, count):
    if not (isinstance(count, int) and count == 0):
        eng.wait_ge(sem, count)


def layernorm_transposed(nc, tag, X, lnT, ident, const, const_ready=None, x_ready=None, kept=None, meanwhile=None,
                         follow=None, first=None):
    HALF = TILES // 2
    with ExitStack() as st:
        m = Memory(nc, st)
        stats = m.sb(f"{tag}_stats", [P, TILES, 6])
        mv = m.sb(f"{tag}_mv", [P, TILES, 2])
        ve = m.sb(f"{tag}_ve", [P, TILES])
        rstd = m.sb(f"{tag}_rstd", [P, TILES])
        ln = m.sb(f"{tag}_ln", [P, 2, TPB, D]) if kept is None else None
        lnps = m.ps(f"{tag}_lnps", 2)
        stats_done = m.sem(f"{tag}_stats_done")
        mv_done = m.sem(f"{tag}_mv_done")
        ve_done = m.sem(f"{tag}_ve_done")
        rstd_done = m.sem(f"{tag}_rstd_done")
        ln_done = m.sem(f"{tag}_ln_done")
        turned = m.sem(f"{tag}_turned")
        stored = m.sem(f"{tag}_stored")
        with nc.Block() as block:
            if meanwhile is not None:
                block.sync(meanwhile)

            @block.vector
            def _(dve):
                if x_ready is not None:
                    dve.wait_ge(*x_ready)
                for g in range(2):
                    for t in range(g * HALF, g * HALF + HALF):
                        dve.bn_stats(stats[:, t, :], X[:, t, :]).then_inc(stats_done, 1)
                    dve.wait_ge(stats_done, g * HALF + HALF)
                    for t in range(g * HALF, g * HALF + HALF):
                        dve.bn_aggr(mv[:, t, :], stats[:, t, :]).then_inc(mv_done, 1)

                for t in range(TILES):
                    if t % HALF == 0:
                        dve.wait_ge(rstd_done, t // HALF + 1)
                    j, tt = divmod(t, TPB)
                    if kept is None and j >= 2:
                        dve.wait_ge(turned, j - 1)
                    dve.tensor_scalar(ln[:, j % 2, tt, :] if kept is None else kept[:, t, :],
                                      X[:, t, :], mv[:, t, 0:1], rstd[:, t:t + 1],
                                      ALU.subtract, ALU.mult).then_inc(ln_done, 1)

            @block.gpsimd
            def _(pool):
                if const_ready is not None:
                    pool.wait_ge(*const_ready)
                for g in range(2):
                    tiles = slice(g * HALF, g * HALF + HALF)
                    pool.wait_ge(mv_done, g * HALF + HALF)
                    pool.tensor_scalar(ve[:, tiles], mv[:, tiles, 1], LN_EPS, 1.0, ALU.add,
                                       ALU.mult).then_inc(ve_done, 1)
                    pool.wait_ge(ve_done, g + 1)
                    pool.tensor_tensor(rstd[:, tiles], ve[:, tiles], const[:, C_NEGHALF:C_NEGHALF + HALF],
                                       ALU.pow).then_inc(rstd_done, 1)

            @block.tensor
            def _(pe):
                if first is not None:
                    first(pe)
                if const_ready is not None:
                    pe.wait_ge(*const_ready)
                for j in range(TILES // TPB):
                    pe.wait_ge(ln_done, TPB * j + TPB)
                    if j >= 2:
                        pe.wait_ge(stored, j - 1)
                    for tt in range(TPB):
                        src = ln[:, j % 2, tt, :] if kept is None else kept[:, TPB * j + tt, :]
                        for c in range(DC):
                            last = pe.transpose(lnps[:, j % 2, c * S_LEN + tt * P:c * S_LEN + (tt + 1) * P],
                                                src[:, c * P:(c + 1) * P], ident)
                    last.then_inc(turned, 1)
                    if follow is not None and j >= 1:
                        pe.wait_ge(stored, j)
                        for tt in range(TPB):
                            follow(pe, TPB * (j - 1) + tt)
                if follow is not None:
                    pe.wait_ge(stored, TILES // TPB)
                    for tt in range(TPB):
                        follow(pe, TILES - TPB + tt)

            @block.scalar
            def _(act):
                for j in range(TILES // TPB):
                    act.wait_ge(turned, j + 1)
                    act.activation(lnT[:, :, j * S_LEN:(j + 1) * S_LEN],
                                   lnps[:, j % 2, :].rearrange("p (c s) -> p c s", c=DC),
                                   ACT.Copy).then_inc(stored, 1)


def mlstm_rows(nc, zps, gates_done, gate_b, sel, const, cols, Gr, Mr, selr, ident, loads):
    with ExitStack() as st:
        m = Memory(nc, st)
        z = m.sb("a_z", [P, S_LEN])
        soft = m.sb("a_soft", [P, S_LEN])
        logf = m.sb("a_logf", [P, S_LEN])
        F = m.sb("a_F", [P, S_LEN])
        Fs = m.sb("a_Fs", [P, S_LEN])
        g = m.sb("a_g", [P, S_LEN])
        M = m.sb("a_M", [P, S_LEN])
        dup = m.sb("a_dup", [P, 2, S_LEN])
        hi = m.sb("a_hi", [P, 2, S_LEN], F32R)
        low = m.sb("a_low", [P, 2, S_LEN])
        ones = m.sb("a_ones", [P, S_LEN])
        ex = m.sb("a_ex", [P, 4, P])
        cps = m.ps("a_cps", 1)
        z_done = m.sem("a_z_done")
        act_step = m.sem("a_act_step")
        row_step = m.sem("a_row_step")
        ones_done = m.sem("a_ones_done")
        arg_done = m.sem("a_arg_done")
        ex_done = m.sem("a_ex_done")
        cols_turned = m.sem("a_cols_turned")
        shift = [16 + i for i in range(16)] + [16 + i for i in range(16)]
        twice = [i % 16 for i in range(32)]
        with nc.Block() as block:
            @block.tensor
            def _(pe):
                pe.wait_ge(ex_done, 1)
                for kind in range(4):
                    last = pe.transpose(cps[:, 0, kind * P:(kind + 1) * P], ex[:, kind, :], ident)
                last.then_inc(cols_turned, 1)

            @block.scalar
            def _(act):
                act.wait_ge(z_done, 1)
                act.activation(soft[:, :], z[:, :], ACT.Abs).then_inc(act_step, 1)
                act.wait_ge(act_step, 1)
                act.activation(soft[:, :], soft[:, :], ACT.Exp, scale=-1.0).then_inc(act_step, 1)
                act.wait_ge(act_step, 2)
                act.activation(soft[:, :], soft[:, :], ACT.Ln, bias=1.0).then_inc(act_step, 1)
                act.wait_ge(arg_done, 4)
                act.activation(ex[:, :, :], ex[:, :, :], ACT.Exp).then_inc(ex_done, 1)
                act.wait_ge(cols_turned, 1)
                act.activation(cols[:, :, :, :], cps[:, 0, :].rearrange("p (k b r) -> p b k r", k=4, b=B), ACT.Copy)

            @block.vector
            def _(dve):
                for ready in loads:
                    dve.wait_ge(*ready)
                dve.wait_ge(gates_done, 1)
                dve.tensor_scalar(z[:, :], zps[:, 0, 0:S_LEN], gate_b[:, 0:1], None, ALU.add).then_inc(z_done, 1)
                dve.memset(ones[:, :], 1.0).then_inc(ones_done, 1)
                dve.tensor_copy(selr[:, :], sel[:, :])
                dve.wait_ge(z_done, 1)
                dve.wait_ge(act_step, 3)
                dve.scalar_tensor_tensor(out=logf[:, :], in0=z[:, :], scalar=0.0, in1=soft[:, :],
                                         op0=ALU.min, op1=ALU.subtract).then_inc(row_step, 1)
                dve.wait_ge(row_step, 1)
                dve.wait_ge(ones_done, 1)
                dve.tensor_tensor_scan(F[:, :], ones[:, :], logf[:, :], 0.0, ALU.mult, ALU.add).then_inc(row_step, 1)
                dve.wait_ge(row_step, 2)
                dve.stream_shuffle(Fs[:, :], F[:, :], shift).then_inc(row_step, 1)
                dve.wait_ge(row_step, 3)
                dve.tensor_tensor(g[:, :], z[:, :], Fs[:, :], ALU.subtract).then_inc(row_step, 1)
                dve.wait_ge(row_step, 4)
                dve.tensor_tensor_scan(M[:, :], g[:, :], g[:, :], -3.0e38, ALU.max, ALU.max).then_inc(row_step, 1)
                dve.wait_ge(row_step, 5)
                last0 = M[:, P - 1:P].to_broadcast([P, P])
                dve.scalar_tensor_tensor(out=ex[:, 0:2, :], in0=M[:, :].rearrange("p (k s) -> p k s", k=2), scalar=-1.0,
                                         in1=Fs[:, :].rearrange("p (k s) -> p k s", k=2), op0=ALU.mult,
                                         op1=ALU.subtract).then_inc(arg_done, 2)
                dve.tensor_tensor(ex[:, 2, :], g[:, 0:P], last0, ALU.subtract).then_inc(arg_done, 1)
                dve.tensor_tensor(ex[:, 3, :], last0, M[:, P:2 * P], ALU.subtract).then_inc(arg_done, 1)
                parts = ((g, 1.0, Gr), (M, -1.0, Mr))
                for i, (src, sign, dst) in enumerate(parts):
                    dve.stream_shuffle(dup[:, i, :], src[:, :], twice).then_inc(row_step, 1)
                for i, (src, sign, dst) in enumerate(parts):
                    dve.wait_ge(row_step, 7)
                    dve.tensor_scalar(hi[:, i, :], dup[:, i, :], sign, None, ALU.mult).then_inc(row_step, 1)
                    dve.tensor_scalar(low[:, i, :], dup[:, i, :], const[:, C_SPLIT:C_SPLIT + 1], sign, ALU.mult,
                                      ALU.mult).then_inc(row_step, 1)
                dve.wait_ge(row_step, 11)
                for b in range(B):
                    rows = slice(32 * b, 32 * b + 32)
                    for i, (src, sign, dst) in enumerate(parts):
                        dve.scalar_tensor_tensor(out=dst[:, b * S_LEN:(b + 1) * S_LEN], in0=hi[rows, i, :].bitcast(F32),
                                                 scalar=const[rows, C_SPLIT + 1:C_SPLIT + 2], in1=low[rows, i, :],
                                                 op0=ALU.mult, op1=ALU.add)


def mlstm_and_ffn(nc, X, lnT, ctx, ctxT, cols, Gr, Mr, selr, scale_row, const, ident, w1, w2, gains, lnT2, loads, pos,
                  pos_ready, sc):
    HH = M_HEADS // HALF
    W = HALF * AUG
    ROWS = TPB * M_HEADS
    UNITS = TPB * HH
    QTR = FC // 4
    TAIL = 8
    with ExitStack() as st:
        m = Memory(nc, st)
        kT = m.sb("b_kT", [P, DC, S_LEN])
        Gb = m.sb("b_Gb", [32, S_LEN], F32R)
        Qm = m.sb("b_Qm", [P, DC, 4, S_LEN])
        V1 = m.sb("b_V1", [P, TPB, M_HEADS, AUG])
        KU = m.sb("b_KU", [P, D])
        BD = m.sb("b_BD", [P, HH, W])
        E = m.sb("b_E", [P, 2, HALF, P])
        C = m.sb("b_C", [P, 2, HALF, P])
        num = m.sb("b_num", [P, TPB, M_HEADS, AUG])
        carried = m.sb("b_carried", [P, M_HEADS, AUG])
        den = m.sb("b_den", [P, TPB, M_HEADS])
        rden = m.sb("b_rden", [P, TPB, M_HEADS])
        h = m.sb("b_h", [P, ROWS, M_DH])
        hc = m.sb("b_hc", [P, ROWS, M_DH])
        sq = m.sb("b_sq", [P, ROWS, M_DH])
        hsum = m.sb("b_hsum", [P, ROWS])
        vsum = m.sb("b_vsum", [P, ROWS])
        hve = m.sb("b_hve", [P, ROWS])
        rs = m.sb("b_rs", [P, ROWS])
        hn = m.sb("b_hn", [P, TPB, D])
        held = m.sb("f_held", [P, 1])
        stats = m.sb("f_stats", [P, 2, TPB, 6])
        mv = m.sb("f_mv", [P, 2, TPB, 2])
        lve = m.sb("f_lve", [P, 2, TPB])
        rstd = m.sb("f_rstd", [P, 2, TPB])
        ln = m.sb("f_ln", [P, 2, TPB, D])
        lnTb = m.sb("f_lnTb", [P, DC, S_LEN])
        q = m.sb("f_q", [P, 2, 512])
        r = m.sb("f_r", [P, 2, 512])
        a = m.sb("f_a", [P, FC, S_LEN])
        posf = m.sb("r_posf", [P, 2 * TILES])
        ang = m.sb("r_ang", [P, 2 * TILES, ROT])
        turns = m.sb("r_turns", [P, 2 * TILES, ROT])
        angle_step = m.sem("r_angle_step")
        arg_ready = m.sem("r_arg_ready")
        sps = m.ps("b_sps", 2)
        eps_ = m.ps("b_eps", 2)
        pvps = m.ps("b_pvps", 1)
        stps = m.ps("b_stps", 1)
        fps = m.ps("f_fps", 2)
        ones_in = m.sem("b_ones_in")
        k_ready = m.sem("b_k_ready")
        g_ready = m.sem("b_g_ready")
        q_ready = m.sem("b_q_ready")
        v_ready = m.sem("b_v_ready")
        ku_ready = m.sem("b_ku_ready")
        state_done = m.sem("b_state_done")
        bd_ready = m.sem("b_bd_ready")
        decay_done = m.sem("b_decay_done")
        scores_done = m.sem("b_scores_done")
        exp_done = m.sem("b_exp_done")
        masked = m.sem("b_masked")
        prod_done = m.sem("b_prod_done")
        pv_done = m.sem("b_pv_done")
        carry_done = m.sem("b_carry_done")
        num_done = m.sem("b_num_done")
        carried_done = m.sem("b_carried_done")
        step = m.sem("b_step")
        centred = m.sem("b_centred")
        squared = m.sem("b_squared")
        var_done = m.sem("b_var_done")
        hve_done = m.sem("b_hve_done")
        rs_done = m.sem("b_rs_done")
        stats_done = [m.sem(f"f_stats_done{n}") for n in range(2)]
        mv_done = [m.sem(f"f_mv_done{n}") for n in range(2)]
        lve_done = [m.sem(f"f_lve_done{n}") for n in range(2)]
        rstd_done = [m.sem(f"f_rstd_done{n}") for n in range(2)]
        ln_done = [m.sem(f"f_ln_done{n}") for n in range(2)]
        turned = [m.sem(f"f_turned{n}") for n in range(2)]
        lnT_ready = [m.sem(f"f_lnT_ready{n}") for n in range(2)]
        up_done = m.sem("f_up_done")
        clipped = m.sem("f_clipped")
        rounded = m.sem("f_rounded")
        scaled = m.sem("f_scaled")
        gelu_done = m.sem("f_gelu_done")
        down_done = m.sem("f_down_done")
        x_done = [m.sem(f"f_x_done{n}") for n in range(2)]

        def steps(eng, body):
            body(0, True, False, False)
            body(1, True, True, False)
            with eng.Fori(2, B) as k:
                body(k, True, True, True)
            body(B, False, True, True)
            body(B + 1, False, False, True)

        with nc.Block() as block:
            @block.gpsimd
            def _(pool):
                def rsqrt_ln(b, n):
                    pool.wait_ge(mv_done[n], TPB * b + TPB)
                    pool.tensor_scalar(lve[:, n, :], mv[:, n, :, 1], LN_EPS, 1.0, ALU.add,
                                       ALU.mult).then_inc(lve_done[n], 1)
                    pool.wait_ge(lve_done[n], b + 1)
                    pool.tensor_tensor(rstd[:, n, :], lve[:, n, :], const[:, C_NEGHALF:C_NEGHALF + TPB],
                                       ALU.pow).then_inc(rstd_done[n], 1)

                def rsqrt_heads(b, tt):
                    pool.wait_ge(hve_done, b + 1)
                    pool.tensor_tensor(rs[:, tt * M_HEADS:(tt + 1) * M_HEADS], hve[:, tt * M_HEADS:(tt + 1) * M_HEADS],
                                       const[:, C_NEGHALF:C_NEGHALF + M_HEADS], ALU.pow).then_inc(rs_done, 1)

                def mask(b, u):
                    pool.wait_ge(exp_done, UNITS * b + u + 1)
                    pool.affine_select(out=E[:, u % 2, :, :], in_=E[:, u % 2, :, :], compare_op=ALU.is_ge,
                                       fill=0.0, base=0, pattern=[[0, HALF], [1, P]],
                                       channel_multiplier=-1).then_inc(masked, 1)

                for k in range(B + 2):
                    heads, ffn, rest = k < B, 1 <= k <= B, k >= 2
                    if heads:
                        wait_for(pool, scores_done, UNITS * k)
                        pool.tensor_scalar(kT[:, :, :], ctxT[:, :, k * S_LEN:(k + 1) * S_LEN], 1.0, 1.0,
                                           ALU.mult, ALU.mult).then_inc(k_ready, 1)
                        mask(k, 0)
                    if ffn:
                        pool.wait_ge(var_done, k)
                        pool.tensor_scalar(hve[:, :], vsum[:, :], 1.0 / M_DH, EPS, ALU.mult,
                                           ALU.add).then_inc(hve_done, 1)
                        rsqrt_heads(k - 1, 0)
                    if heads:
                        mask(k, 1)
                    if ffn:
                        rsqrt_heads(k - 1, 1)
                    if heads:
                        mask(k, 2)
                    if ffn:
                        rsqrt_ln(k - 1, 0)
                    if rest:
                        rsqrt_ln(k - 2, 1)
                    if heads:
                        mask(k, 3)
                    if ffn:
                        for n in range(4):
                            pool.wait_ge(rounded, 4 * k - 4 + n + 1)
                            pool.tensor_scalar(r[:, n % 2, :], r[:, n % 2, :], -ROUND, 0.1, ALU.add,
                                               ALU.mult).then_inc(scaled, 1)

            @block.scalar
            def _(act):
                act.wait_ge(ones_in, 1)

                def exponential(b, u):
                    act.wait_ge(decay_done, UNITS * b + u + 1)
                    wait_for(act, prod_done, UNITS * b + u - 1 if u > 0 else UNITS * b)
                    act.activation(E[:, u % 2, :, :].rearrange("p (a h) s -> p a (h s)", a=2),
                                   eps_[:, :, :], ACT.Exp).then_inc(exp_done, 1)

                def body(k, heads, ffn, rest):
                    if heads:
                        wait_for(act, pv_done, UNITS * k)
                        act.activation(V1[:, :, :, 0:M_DH].rearrange("p t h d -> p (t h) d"),
                                       ctx[:, bass.ds(k * TPB, TPB), :].rearrange("p t (h d) -> p (t h) d", d=M_DH),
                                       ACT.Copy).then_inc(v_ready, 1)
                        exponential(k, 0)
                    if ffn:
                        act.wait_ge(centred, k)
                        act.activation(sq[:, :, :], hc[:, :, :], ACT.Square).then_inc(squared, 1)
                    if heads:
                        for u in range(1, UNITS):
                            exponential(k, u)
                    if not ffn and not rest:
                        act.wait_ge(arg_ready, 2)
                        act.activation(sc[:, :, :, :], sc[:, :, :, :], ACT.Sin)
                    if ffn:
                        act.wait_ge(turned[0], k)
                        act.activation(lnTb[:, :, :], fps[:, 0, :].rearrange("p (c s) -> p c s", c=DC),
                                       ACT.Copy).then_inc(lnT_ready[0], 1)
                    if rest:
                        act.wait_ge(turned[1], k - 1)
                        act.activation(lnT2[:, :, bass.ds((k - 2) * S_LEN, S_LEN)],
                                       fps[:, 1, :].rearrange("p (c s) -> p c s", c=DC),
                                       ACT.Copy).then_inc(lnT_ready[1], 1)
                    if ffn:
                        for n in range(4):
                            act.wait_ge(scaled, 4 * k - 4 + n + 1)
                            act.activation(a[:, n * QTR:(n + 1) * QTR, :].rearrange("p f s -> p (f s)"),
                                           r[:, n % 2, :], ACT.Gelu_apprx_tanh).then_inc(gelu_done, 1)

                steps(act, body)

            @block.vector
            def _(dve):
                dve.memset(V1[:, :, :, M_DH:AUG], 1.0).then_inc(ones_in, 1)

                def prepare(b):
                    wait_for(dve, decay_done, UNITS * b)
                    dve.tensor_copy(Gb[:, :], Gr[:, bass.ds(b * S_LEN, S_LEN)].bitcast(F32)).then_inc(g_ready, 1)
                    wait_for(dve, scores_done, UNITS * b)
                    wait_for(dve, carry_done, b)
                    for n in range(4):
                        dve.tensor_scalar(Qm[:, :, n, :], lnT[:, :, bass.ds(b * S_LEN, S_LEN)],
                                          const[:, C_PAR + n:C_PAR + n + 1], None, ALU.mult).then_inc(q_ready, 1)
                    wait_for(dve, state_done, b)
                    dve.tensor_tensor(KU[:, :].rearrange("p (h d) -> p h d", d=M_DH),
                                      ctx[:, b * TPB, :].rearrange("p (h d) -> p h d", d=M_DH),
                                      cols[:, b, 2, 0:M_HEADS].unsqueeze(2).to_broadcast([P, M_HEADS, M_DH]),
                                      ALU.mult).then_inc(ku_ready, 1)

                def state(b):
                    dve.wait_ge(state_done, b + 1)
                    dve.tensor_tensor(BD[:, :, :], stps[:, 0, 0:HH * W].rearrange("p (a w) -> p a w", a=HH),
                                      const[:, C_BDM:C_BDM + W].unsqueeze(1).to_broadcast([P, HH, W]),
                                      ALU.mult).then_inc(bd_ready, 1)

                def product(b, u):
                    dve.wait_ge(scores_done, UNITS * b + u + 1)
                    dve.wait_ge(masked, UNITS * b + u + 1)
                    if u >= 2:
                        dve.wait_ge(pv_done, UNITS * b + u - 1)
                    dve.tensor_tensor(C[:, u % 2, :, :].rearrange("p (a h) s -> p a (h s)", a=2), sps[:, :, :],
                                      E[:, u % 2, :, :].rearrange("p (a h) s -> p a (h s)", a=2),
                                      ALU.mult).then_inc(prod_done, 1)

                def first_sums(b):
                    dve.wait_ge(pv_done, UNITS * b + 2)
                    dve.tensor_copy(num[:, 0, :, :].rearrange("p h a -> p (h a)"),
                                    pvps[:, 0, 0:HH * W]).then_inc(num_done, 1)

                def carry(b):
                    dve.wait_ge(carry_done, b + 1)
                    dve.tensor_tensor(carried[:, :, :], stps[:, 0, 0:HH * W].rearrange("p (h a) -> p h a", a=AUG),
                                      cols[:, b, 3, 0:M_HEADS].unsqueeze(2).to_broadcast([P, M_HEADS, AUG]),
                                      ALU.mult).then_inc(carried_done, 1)

                def second_sums(b):
                    dve.wait_ge(carried_done, b + 1)
                    dve.wait_ge(pv_done, UNITS * b + 4)
                    dve.tensor_tensor(num[:, 1, :, :].rearrange("p h a -> p (h a)"), pvps[:, 0, 0:HH * W],
                                      carried[:, :, :].rearrange("p h a -> p (h a)"),
                                      ALU.add).then_inc(num_done, 1)

                def normalise_rows(b):
                    dve.wait_ge(num_done, 2 * b + 2)
                    dve.scalar_tensor_tensor(out=den[:, :, :], in0=num[:, :, :, M_DH], scalar=-1.0,
                                             in1=num[:, :, :, M_DH], op0=ALU.mult,
                                             op1=ALU.max).then_inc(step, 1)
                    dve.wait_ge(step, TAIL * b + 1)
                    dve.tensor_tensor(den[:, :, :], den[:, :, :], cols[:, b, 0:TPB, 0:M_HEADS],
                                      ALU.max).then_inc(step, 1)
                    dve.wait_ge(step, TAIL * b + 2)
                    dve.tensor_scalar(den[:, :, :], den[:, :, :], EPS, None, ALU.add).then_inc(step, 1)
                    dve.wait_ge(step, TAIL * b + 3)
                    dve.reciprocal(rden[:, :, :], den[:, :, :]).then_inc(step, 1)
                    dve.wait_ge(step, TAIL * b + 4)
                    dve.tensor_tensor(h[:, :, :], num[:, :, :, 0:M_DH].rearrange("p t h d -> p (t h) d"),
                                      rden[:, :, :].rearrange("p t h -> p (t h)").unsqueeze(2)
                                      .to_broadcast([P, ROWS, M_DH]), ALU.mult).then_inc(step, 1)
                    dve.wait_ge(step, TAIL * b + 5)
                    dve.tensor_reduce(hsum[:, :], h[:, :, :], AX.X, ALU.add).then_inc(step, 1)
                    dve.wait_ge(step, TAIL * b + 6)
                    dve.scalar_tensor_tensor(out=hc[:, :, :], in0=hsum[:, :].unsqueeze(2).to_broadcast([P, ROWS, M_DH]),
                                             scalar=-1.0 / M_DH, in1=h[:, :, :], op0=ALU.mult,
                                             op1=ALU.add).then_inc(centred, 1)

                def variance(b):
                    dve.wait_ge(squared, b + 1)
                    dve.tensor_reduce(vsum[:, :], sq[:, :, :], AX.X, ALU.add).then_inc(var_done, 1)

                def add_heads(b):
                    dve.wait_ge(rs_done, TPB * b + TPB)
                    dve.tensor_tensor(hn[:, :, :].rearrange("p t (h d) -> p (t h) d", d=M_DH), hc[:, :, :],
                                      rs[:, :].unsqueeze(2).to_broadcast([P, ROWS, M_DH]),
                                      ALU.mult).then_inc(step, 1)
                    dve.wait_ge(step, TAIL * b + 7)
                    dve.tensor_tensor(hn[:, :, :], hn[:, :, :],
                                      scale_row[:, :].unsqueeze(1).to_broadcast([P, TPB, D]),
                                      ALU.mult).then_inc(step, 1)
                    dve.wait_ge(step, TAIL * b + 8)
                    dve.tensor_tensor(X[:, bass.ds(b * TPB, TPB), :], X[:, bass.ds(b * TPB, TPB), :],
                                      hn[:, :, :], ALU.add).then_inc(x_done[0], 1)

                def ln_stats(b, n):
                    dve.wait_ge(x_done[n], b + 1 if n == 0 else TPB * b + TPB)
                    dve.tensor_copy(held[:, :], const[:, C_ONES:C_ONES + 1])
                    for tt in range(TPB):
                        dve.bn_stats(stats[:, n, tt, :], X[:, b * TPB + tt, :]).then_inc(stats_done[n], 1)
                    dve.wait_ge(stats_done[n], TPB * b + TPB)
                    dve.tensor_copy(held[:, :], const[:, C_ONES:C_ONES + 1])
                    for tt in range(TPB):
                        dve.bn_aggr(mv[:, n, tt, :], stats[:, n, tt, :]).then_inc(mv_done[n], 1)

                def ln_normalise(b, n):
                    dve.wait_ge(rstd_done[n], b + 1)
                    for tt in range(TPB):
                        dve.tensor_scalar(ln[:, n, tt, :], X[:, b * TPB + tt, :], mv[:, n, tt, 0:1],
                                          rstd[:, n, tt:tt + 1], ALU.subtract, ALU.mult).then_inc(ln_done[n], 1)

                def clip(b, n):
                    dve.wait_ge(up_done, 4 * b + n + 1)
                    if n >= 2:
                        dve.wait_ge(rounded, 4 * b + n - 1)
                    dve.tensor_scalar(q[:, n % 2, :], fps[:, n % 2, :], 10.0, 32767.0, ALU.mult,
                                      ALU.min).then_inc(clipped, 1)

                def quantise(b, n):
                    dve.wait_ge(clipped, 4 * b + n + 1)
                    if n >= 2:
                        dve.wait_ge(gelu_done, 4 * b + n - 1)
                    dve.tensor_scalar(r[:, n % 2, :], q[:, n % 2, :], -32768.0, ROUND, ALU.max,
                                      ALU.add).then_inc(rounded, 1)

                def add_ffn(b):
                    dve.wait_ge(down_done, b + 1)
                    for tt in range(TPB):
                        dve.scalar_tensor_tensor(out=X[:, b * TPB + tt, :], in0=fps[:, 0, tt * D:(tt + 1) * D],
                                                 scalar=gains[:, 2:3], in1=X[:, b * TPB + tt, :],
                                                 op0=ALU.mult, op1=ALU.add).then_inc(x_done[1], 1)

                def angles(k):
                    shape = [P, 2 * TILES, ROT]
                    if k == 0:
                        dve.wait_ge(*pos_ready)
                        dve.tensor_copy(posf[:, :], pos[:, :]).then_inc(angle_step, 1)
                        dve.wait_ge(angle_step, 1)
                        dve.tensor_tensor(ang[:, :, :], posf[:, :].unsqueeze(2).to_broadcast(shape),
                                          const[:, C_FREQ:C_FREQ + ROT].unsqueeze(1).to_broadcast(shape),
                                          ALU.mult).then_inc(angle_step, 1)
                    done = 2 + 7 * k
                    arg = sc[:, k, :, :]
                    dve.wait_ge(angle_step, done)
                    dve.tensor_scalar(turns[:, :, :], ang[:, :, :], 1.0 / TWO_PI, 0.25 * k, ALU.mult,
                                      ALU.add).then_inc(angle_step, 1)
                    dve.wait_ge(angle_step, done + 1)
                    dve.tensor_scalar(turns[:, :, :], turns[:, :, :], ROUND, None, ALU.add).then_inc(angle_step, 1)
                    dve.wait_ge(angle_step, done + 2)
                    dve.tensor_scalar(turns[:, :, :], turns[:, :, :], ROUND, None,
                                      ALU.subtract).then_inc(angle_step, 1)
                    dve.wait_ge(angle_step, done + 3)
                    src = ang[:, :, :]
                    for i, part in enumerate((PI_HIGH, PI_MID, PI_LOW)):
                        dve.scalar_tensor_tensor(out=arg, in0=turns[:, :, :], scalar=-part, in1=src, op0=ALU.mult,
                                                 op1=ALU.add).then_inc(angle_step, 1)
                        dve.wait_ge(angle_step, done + 4 + i)
                        src = arg
                    dve.tensor_scalar(arg, arg, 0.25 * k * TWO_PI, PI_CLAMP, ALU.add,
                                      ALU.min).then_inc(angle_step, 1)
                    dve.wait_ge(angle_step, done + 7)
                    dve.tensor_scalar(arg, arg, -PI_CLAMP, None, ALU.max).then_inc(arg_ready, 1)

                def body(k, heads, ffn, rest):
                    if heads:
                        prepare(k)
                    if ffn:
                        second_sums(k - 1)
                        normalise_rows(k - 1)
                    if heads:
                        product(k, 0)
                        state(k)
                    if ffn:
                        variance(k - 1)
                    if not ffn and not rest:
                        angles(0)
                    if heads:
                        product(k, 1)
                    if not ffn and not rest:
                        angles(1)
                    if ffn:
                        add_heads(k - 1)
                        ln_stats(k - 1, 0)
                    if heads:
                        product(k, 2)
                    if ffn:
                        ln_normalise(k - 1, 0)
                    if rest:
                        add_ffn(k - 2)
                        ln_stats(k - 2, 1)
                    if heads:
                        first_sums(k)
                        carry(k)
                    if rest:
                        ln_normalise(k - 2, 1)
                    if heads:
                        product(k, 3)
                    if ffn:
                        for n in range(4):
                            clip(k - 1, n)
                            quantise(k - 1, n)

                steps(dve, body)

            @block.tensor
            def _(pe):
                for ready in loads:
                    pe.wait_ge(*ready)

                def decay(b, u):
                    blk, hh = divmod(u, HH)
                    if u == 0:
                        pe.wait_ge(g_ready, b + 1)
                    wait_for(pe, exp_done, UNITS * b + u)
                    for half in range(2):
                        pe.matmul(eps_[:, half, :], Gb[:, blk * P:(blk + 1) * P],
                                  selr[:, (hh * 2 + half) * 512:(hh * 2 + half + 1) * 512], start=True, stop=False)
                        for n in range(4):
                            hd = hh * HALF + half * 4 + n
                            last = pe.matmul(eps_[:, half, n * P:(n + 1) * P], selr[:, hd * P:(hd + 1) * P],
                                             Mr[:, bass.ds(b * S_LEN + blk * P, P)], start=False,
                                             stop=(n == 3))
                    last.then_inc(decay_done, 1)

                def scores(b, u):
                    blk, hh = divmod(u, HH)
                    if u == 0:
                        pe.wait_ge(q_ready, 4 * b + 4)
                        pe.wait_ge(k_ready, b + 1)
                    wait_for(pe, prod_done, UNITS * b + u)
                    for half in range(2):
                        rows = slice(64 * half, 64 * half + 64)
                        last = pe.matmul(sps[:, half, :].rearrange("p (n s) -> p n s", n=4),
                                         kT[rows, hh, blk * P:(blk + 1) * P],
                                         Qm[rows, hh, :, blk * P:(blk + 1) * P], start=True, stop=True)
                    last.then_inc(scores_done, 1)

                def values(b, u):
                    blk, hh = divmod(u, HH)
                    pe.wait_ge(prod_done, UNITS * b + u + 1)
                    if hh == 0:
                        wait_for(pe, num_done, 2 * b + blk)
                    for n in range(HALF):
                        hd = hh * HALF + n
                        last = pe.matmul(pvps[:, 0, hd * AUG:(hd + 1) * AUG], C[:, u % 2, n, :],
                                         V1[:, blk, hd, :], start=True, stop=True)
                    last.then_inc(pv_done, 1)

                def state(b):
                    pe.wait_ge(ku_ready, b + 1)
                    pe.wait_ge(v_ready, b + 1)
                    wait_for(pe, carried_done, b)
                    for hh in range(HH):
                        last = pe.matmul(stps[:, 0, hh * W:(hh + 1) * W], KU[:, hh * P:(hh + 1) * P],
                                         V1[:, 0, hh * HALF:(hh + 1) * HALF, :].rearrange("p h a -> p (h a)"),
                                         start=True, stop=True)
                    last.then_inc(state_done, 1)

                def carry(b):
                    pe.wait_ge(bd_ready, b + 1)
                    for hh in range(HH):
                        for n in range(4):
                            last = pe.matmul(stps[:, 0, hh * W:(hh + 1) * W], Qm[:, hh, n, P:2 * P],
                                             BD[:, hh, :], start=(n == 0), stop=(n == 3))
                    last.then_inc(carry_done, 1)

                def turn(b, n):
                    pe.wait_ge(ln_done[n], TPB * b + TPB)
                    for tt in range(TPB):
                        for c in range(DC):
                            last = pe.transpose(fps[:, n, c * S_LEN + tt * P:c * S_LEN + (tt + 1) * P],
                                                ln[:, n, tt, c * P:(c + 1) * P], ident)
                    last.then_inc(turned[n], 1)

                def up(b, n):
                    if n == 0:
                        pe.wait_ge(lnT_ready[0], b + 1)
                    if n >= 2:
                        pe.wait_ge(clipped, 4 * b + n - 1)
                    for f in range(QTR):
                        fc = n * QTR + f
                        for c in range(DC):
                            last = pe.matmul(fps[:, n % 2, f * S_LEN:(f + 1) * S_LEN],
                                             w1[:, c, fc * P:(fc + 1) * P], lnTb[:, c, :],
                                             start=(c == 0), stop=(c == DC - 1))
                    last.then_inc(up_done, 1)

                def down(b, first, end):
                    if first == 0:
                        pe.wait_ge(gelu_done, 4 * b + 4)
                    for j in range(first, end):
                        tt, fc = divmod(j, FC)
                        last = pe.matmul(fps[:, 0, tt * D:(tt + 1) * D], a[:, fc, tt * P:(tt + 1) * P],
                                         w2[:, fc, :], start=(fc == 0), stop=(fc == FC - 1))
                    if end == TPB * FC:
                        last.then_inc(down_done, 1)

                def body(k, heads, ffn, rest):
                    if heads:
                        decay(k, 0)
                    if rest:
                        down(k - 2, 0, 4)
                    if heads:
                        scores(k, 0)
                        state(k)
                    if rest:
                        down(k - 2, 4, 7)
                    if heads:
                        decay(k, 1)
                        scores(k, 1)
                    if rest:
                        down(k - 2, 7, 10)
                    if heads:
                        values(k, 0)
                    if rest:
                        down(k - 2, 10, 13)
                    if heads:
                        decay(k, 2)
                        scores(k, 2)
                    if rest:
                        down(k - 2, 13, 16)
                    if heads:
                        values(k, 1)
                        carry(k)
                        decay(k, 3)
                    if ffn:
                        if rest:
                            pe.wait_ge(x_done[1], TPB * k - TPB)
                        turn(k - 1, 0)
                    if heads:
                        scores(k, 3)
                    if rest:
                        turn(k - 2, 1)
                    if heads:
                        values(k, 2)
                    if ffn:
                        for n in range(4):
                            if n == 1 and rest:
                                pe.wait_ge(lnT_ready[1], k - 1)
                            up(k - 1, n)
                    if heads:
                        values(k, 3)

                steps(pe, body)


def rope_cos(eng, cosw, w, sc, t0, n, half, done):
    here = slice(half * ROT, (half + 1) * ROT)
    eng.tensor_tensor(cosw[:, :, here], sc[:, 1, t0:t0 + n, :], w[:, here].unsqueeze(1).to_broadcast([P, n, ROT]),
                      ALU.mult).then_inc(done, 1)


def rope_sin(eng, sinw, w, sc, t0, n, half, done):
    here = slice(half * ROT, (half + 1) * ROT)
    weights = w[:, (1 - half) * ROT:(2 - half) * ROT].unsqueeze(1).to_broadcast([P, n, ROT])
    if half == 0:
        eng.scalar_tensor_tensor(out=sinw[:, :, here], in0=sc[:, 0, t0:t0 + n, :], scalar=-1.0, in1=weights,
                                 op0=ALU.mult, op1=ALU.mult).then_inc(done, 1)
    else:
        eng.tensor_tensor(sinw[:, :, here], sc[:, 0, t0:t0 + n, :], weights, ALU.mult).then_inc(done, 1)


def gqa_attention(nc, t, X, lnT, wq, wk, wv, wo, kcos, ksin, qcos, qsin, gains, const, ident, loads, sc, kw, qw,
                  rope_loads, load_gate):
    ROPES = KT_TILES + TPB * KV_HEADS
    FIRST = KT_TILES + 1
    UNITS = TPB * HEADS
    PAIRS = UNITS // 2
    Q_RING = 3
    QUERIES = ROPES - KT_TILES
    OWN = ROPES - FIRST
    LAG = 2
    START = {0: 0, 3: 1, 5: 2, 7: 3, 12: 4, 15: 5, 18: 6, 21: 7, 23: 8, 25: 9, 27: 10, 29: 11}
    COSINES = {1: 0, 4: 1, 6: 2, 9: 3, 13: 4, 16: 5, 19: 6, 22: 7, 25: 8, 26: 9, 28: 10, 30: 11}
    SINES = {1: 0, 5: 1, 7: 2, 10: 3, 14: 4, 17: 5, 20: 6, 23: 7, 25: 8, 27: 9, 29: 10, 31: 11}
    TURN = {2: 0, 6: 1, 9: 2, 12: 3, 16: 4, 19: 5, 22: 6, 25: 7, 27: 8, 29: 9, 31: 10, 33: 11}
    LOW = {3: 0, 7: 1, 10: 2, 14: 3, 18: 4, 21: 5, 24: 6, 34: 11}
    KEYS_AT = {UNITS: 0, UNITS + 1: 1, UNITS + 2: 2, UNITS + 3: 3}
    V_START = {UNITS + 1: 0, UNITS + 2: 1, UNITS + 5: 2}
    with ExitStack() as st:
        m = Memory(nc, st)
        kvT = m.sb("c_kvT", [P, DC, KEYS])
        raw = m.sb("c_raw", [P, 2, 512])
        sq = m.sb("c_sq", [P, 512])
        y = m.sb("c_y", [P, 2, 512])
        ss = m.sb("c_ss", [P, ROPES, REP])
        ve = m.sb("c_ve", [P, ROPES, REP])
        rn = m.sb("c_rn", [P, ROPES, REP])
        scale = m.sb("c_scale", [P, UNITS])
        KTh = m.sb("c_KTh", [P, KV_HEADS, KEYS], F32R)
        KTl = m.sb("c_KTl", [P, KV_HEADS, KEYS], F32R)
        next_KT = sc[:, :, :, :].rearrange("p a t r -> p (a t r)").rearrange("p (k s) -> p k s", k=KV_HEADS)
        qTh = m.sb("c_qTh", [P, Q_RING, REP, P], F32R)
        qTl = m.sb("c_qTl", [P, Q_RING, REP, P], F32R)
        Vh = m.sb("c_Vh", [P, KT_TILES, KV_HEADS * HD], F32R)
        Vl = m.sb("c_Vl", [P, KT_TILES, KV_HEADS * HD], F32R)
        probs = m.sb("c_probs", [P, 3, KEYS])
        PTh = m.sb("c_PTh", [P, 2, KT_TILES, 2, P], F32R)
        PTl = m.sb("c_PTl", [P, 2, KT_TILES, 2, P], F32R)
        attnT = m.sb("c_attnT", [P, 4, P])
        nmax = m.sb("c_nmax", [P, UNITS])
        bias = m.sb("c_bias", [P, UNITS])
        total = m.sb("c_total", [P, UNITS])
        inv = m.sb("c_inv", [P, UNITS])
        sps = m.ps("c_sps", 2)
        pps = m.ps("c_pps", 1)
        rps = m.ps("c_rps", 1)
        tps = m.ps("c_tps", 2)
        ops = m.ps("c_ops", 1)
        wps = m.ps("c_wps", 1)
        k_tables_done = m.sem("c_k_tables_done")
        q_tables_done = m.sem("c_q_tables_done")
        ctx_in = m.sem("c_ctx_in")
        names = ("ln_copied proj_done raw_done squared summed products roped ve_done rn_done scaled "
                 "turned stored q_low k_high k_low v_done v_stored v_low scale_done s_done max_done bias_done exp_done "
                 "inv_done normed pt_turned pt_high pt_low pv_done at_stored wo_done x_done").split()
        (ln_copied, proj_done, raw_done, squared, summed, products, roped, ve_done, rn_done, scaled,
         turned, stored, q_low, k_high, k_low, v_done, v_stored, v_low, scale_done, s_done, max_done, bias_done, exp_done,
         inv_done, normed, pt_turned, pt_high, pt_low, pv_done, at_stored, wo_done, x_done) = (
             m.sem("c_" + n) for n in names)

        def rope_unit(b, j):
            return (b, FIRST + j) if j < OWN else (b + 1, j - OWN)

        def slots(where, i, more):
            j = where.get(i)
            return j if j is not None and (more or j < OWN) else None

        def proj_bank(r, early):
            return (pps[:, 0, :], sps[:, 0, :], sps[:, 1, :])[r % 3] if early else pps[:, 0, :]

        def squares(r, early):
            return probs[:, r % 2, :] if early else sq[:, :]

        def turn_bank(r, early):
            return tps[:, r % 2, :] if early else rps[:, 0, :]

        def v_bank(k, early):
            if early:
                return (ops[:, 0, :], rps[:, 0, :])[k % 2]
            return (pps[:, 0, :], rps[:, 0, :], ops[:, 0, :], wps[:, 0, :])[k]

        def batches(eng, body):
            body(0, True)
            with eng.Fori(1, B - 1) as b:
                body(b, True)
            body(B - 1, False)

        with nc.Block() as block:
            @block.sync
            def _(sp):
                for b in range(B):
                    if b == 1:
                        load_gate(sp)
                    if b > 0:
                        sp.wait_ge(proj_done, ROPES * (b - 1) + KT_TILES)
                        sp.wait_ge(v_done, KT_TILES * b)
                    sp.dma_start(kvT[:, :, 0:S_LEN],
                                 t["ctxT"].rearrange("(c p) s -> p c s", p=P)[:, :, bass.ds(b * S_LEN, S_LEN)]
                                 ).then_inc(ctx_in, 16)

            @block.gpsimd
            def _(pool):
                def copy_ln(b):
                    wait_for(pool, proj_done, ROPES * b)
                    wait_for(pool, v_done, KT_TILES * b)
                    pool.tensor_scalar(kvT[:, :, S_LEN:KEYS], lnT[:, :, bass.ds(b * S_LEN, S_LEN)], 1.0, 1.0,
                                       ALU.mult, ALU.mult).then_inc(ln_copied, 1)

                def inverse_norm(b, r):
                    pool.wait_ge(summed, ROPES * b + r + 1)
                    pool.tensor_scalar(ve[:, r, :], ss[:, r, :], 1.0 / HD, EPS, ALU.mult, ALU.add).then_inc(ve_done, 1)
                    pool.wait_ge(ve_done, ROPES * b + r + 1)
                    pool.tensor_tensor(rn[:, r, :], ve[:, r, :], const[:, C_NEGHALF:C_NEGHALF + REP],
                                       ALU.pow).then_inc(rn_done, 1)
                    pool.wait_ge(rn_done, ROPES * b + r + 1)
                    if r < KT_TILES:
                        pool.wait_ge(roped, ROPES * b + r + 1)
                        for k in range(KV_HEADS):
                            last = pool.tensor_scalar(y[:, r % 2, k * HD:(k + 1) * HD],
                                                      y[:, r % 2, k * HD:(k + 1) * HD],
                                                      rn[:, r, k:k + 1], 1.0, ALU.mult, ALU.mult)
                        last.then_inc(scaled, 1)
                    else:
                        i = (r - KT_TILES) * REP
                        pool.tensor_scalar(scale[:, i:i + REP], rn[:, r, :], float(HD) ** -0.5, 1.0,
                                           ALU.mult, ALU.mult).then_inc(scale_done, 1)

                copy_ln(0)
                for ready in rope_loads:
                    pool.wait_ge(*ready)
                rope_cos(pool, qcos, qw, sc, TILES, TILES, 0, q_tables_done)
                rope_cos(pool, qcos, qw, sc, TILES, TILES, 1, q_tables_done)
                rope_sin(pool, qsin, qw, sc, TILES, TILES, 1, q_tables_done)
                for r in range(FIRST):
                    inverse_norm(0, r)
                for b in range(B):
                    for i in range(UNITS):
                        pool.wait_ge(inv_done, UNITS * b + i + 1)
                        pool.tensor_scalar(probs[:, i % 3, :], probs[:, i % 3, :], inv[:, i:i + 1], 1.0, ALU.mult,
                                           ALU.mult).then_inc(normed, 1)
                        j = slots(COSINES, i, b < B - 1)
                        if j is not None:
                            inverse_norm(*rope_unit(b, j))
                        if j == OWN - 1 and b < B - 1:
                            copy_ln(b + 1)

            @block.scalar
            def _(act):
                def raw_copy(b, r, early=False):
                    act.wait_ge(proj_done, ROPES * b + r + 1)
                    wait_for(act, roped, ROPES * b + r - 1 if not early else max(r - 1, 0))
                    act.activation(raw[:, r % 2, :], proj_bank(r, early), ACT.Copy).then_inc(raw_done, 1)
                    act.wait_ge(raw_done, ROPES * b + r + 1)
                    if not early:
                        act.wait_ge(roped, ROPES * b + r)
                    act.activation(squares(r, early), raw[:, r % 2, :], ACT.Square).then_inc(squared, 1)

                def v_copy(b, k, early=False):
                    act.wait_ge(v_done, KT_TILES * b + k + 1)
                    wait_for(act, pv_done, PAIRS * b)
                    act.activation(Vh[:, k, :], v_bank(k, early), ACT.Copy).then_inc(v_stored, 1)

                def turned_copy(b, r, early=False):
                    act.wait_ge(turned, ROPES * b + r + 1)
                    src = turn_bank(r, early).rearrange("p (k s) -> p k s", k=REP)
                    if r < KT_TILES:
                        act.activation(next_KT[:, :, r * P:(r + 1) * P], src, ACT.Copy).then_inc(stored, 1)
                    else:
                        act.activation(qTh[:, (r - KT_TILES) % Q_RING, :, :], src, ACT.Copy).then_inc(stored, 1)

                def k_high_part(b, k):
                    act.wait_ge(stored, ROPES * b + KT_TILES)
                    if not (isinstance(b, int) and b == 0):
                        act.wait_ge(s_done, UNITS * b - (KV_HEADS - 1 - k) * REP)
                    act.activation(KTh[:, k, :], next_KT[:, k, :], ACT.Copy).then_inc(k_high, 1)

                def exponential(b, i):
                    act.wait_ge(bias_done, UNITS * b + i + 1)
                    wait_for(act, pt_turned, UNITS * b + max(i - 2, 0))
                    act.activation(probs[:, i % 3, :], sps[:, i % 2, :], ACT.Exp, bias=bias[:, i:i + 1],
                                   scale=scale[:, i:i + 1], accum_out=total[:, i:i + 1]).then_inc(exp_done, 1)

                def pt_copy(b, i):
                    act.wait_ge(pt_turned, UNITS * b + i + 1)
                    act.activation(PTh[:, i // 2 % 2, :, i % 2, :],
                                   tps[:, i % 2, :].rearrange("p (k s) -> p k s", k=KT_TILES),
                                   ACT.Copy).then_inc(pt_high, 1)

                def attn_copy(b, pair):
                    act.wait_ge(pv_done, PAIRS * b + pair + 1)
                    h = 2 * pair % 4
                    act.activation(attnT[:, h:h + 2, :].rearrange("p h s -> p (h s)"),
                                   ops[:, 0, 0:2 * P], ACT.Copy).then_inc(at_stored, 1)

                for r in range(FIRST + 2):
                    if r < FIRST:
                        raw_copy(0, r, True)
                    if LAG <= r < KT_TILES + LAG:
                        v_copy(0, r - LAG, True)
                    if r == 2:
                        act.wait_ge(k_tables_done, 4)
                        act.wait_ge(q_tables_done, 4)
                    if r >= 2:
                        turned_copy(0, r - 2, True)

                for k in range(KV_HEADS):
                    k_high_part(0, k)

                def batch(b, more):
                    for i in range(UNITS + 5):
                        if i < UNITS:
                            exponential(b, i)
                        j = slots(START, i, more)
                        if j is not None:
                            raw_copy(*rope_unit(b, j))
                        if i >= 6 and i % 2 == 0:
                            attn_copy(b, (i - 6) // 2)
                        if 2 <= i < UNITS + 2:
                            pt_copy(b, i - 2)
                        j = slots(TURN, i, more)
                        if j is not None:
                            turned_copy(*rope_unit(b, j))
                        if more and i in KEYS_AT:
                            k_high_part(b + 1, KEYS_AT[i])
                        if i == 1 and not (isinstance(b, int) and b == 0):
                            v_copy(b, KT_TILES - 1)
                    if more:
                        for k in range(KT_TILES - 1):
                            v_copy(b + 1, k)

                batches(act, batch)

            @block.vector
            def _(dve):
                def rope_tables_of(b, r):
                    if r < KT_TILES:
                        tile = (b * TPB + r) if r < TPB else (TILES + b * TPB + r - TPB)
                        return kcos[:, tile, :], ksin[:, tile, :]
                    tile = b * TPB + (r - KT_TILES) // KV_HEADS
                    return qcos[:, tile, :], qsin[:, tile, :]

                def rope_first(b, r, early=False):
                    cosw, sinw = rope_tables_of(b, r)
                    dve.wait_ge(squared, ROPES * b + r + 1)
                    dve.tensor_reduce(ss[:, r, :], squares(r, early).rearrange("p (k d) -> p k d", k=REP), AX.X,
                                      ALU.add).then_inc(summed, 1)
                    dve.wait_ge(raw_done, ROPES * b + r + 1)
                    if not (isinstance(b, int) and b == 0 and r < 2):
                        dve.wait_ge(turned, ROPES * b + r - 1)
                    dve.tensor_tensor(y[:, r % 2, :].rearrange("p (k d) -> p k d", k=REP),
                                      raw[:, r % 2, :].rearrange("p (k d) -> p k d", k=REP),
                                      cosw.unsqueeze(1).to_broadcast([P, REP, HD]),
                                      ALU.mult).then_inc(products, 1)

                def rope_second(b, r):
                    cosw, sinw = rope_tables_of(b, r)
                    src = raw[:, r % 2, :].rearrange("p (k d) -> p k d", k=REP)
                    dve.wait_ge(summed, ROPES * b + r + 1)
                    for half in range(2):
                        here = slice(half * ROT, (half + 1) * ROT)
                        other = slice((1 - half) * ROT, (2 - half) * ROT)
                        dve.tensor_tensor(sq[:, :].rearrange("p (k d) -> p k d", k=REP)[:, :, here],
                                          src[:, :, other],
                                          sinw[:, here].unsqueeze(1).to_broadcast([P, REP, ROT]),
                                          ALU.mult).then_inc(products, 1)
                    dve.wait_ge(products, 3 * (ROPES * b + r + 1))
                    dve.tensor_tensor(y[:, r % 2, :], y[:, r % 2, :], sq[:, :], ALU.add).then_inc(roped, 1)

                def maximum(b, i):
                    dve.wait_ge(s_done, UNITS * b + i + 1)
                    dve.tensor_reduce(nmax[:, i:i + 1], sps[:, i % 2, :], AX.X, ALU.max,
                                      negate=True).then_inc(max_done, 1)

                def shift(b, i):
                    if i % REP == 0:
                        dve.wait_ge(scale_done, TPB * KV_HEADS * b + i // REP + 1)
                    dve.wait_ge(max_done, UNITS * b + i + 1)
                    dve.tensor_tensor(bias[:, i:i + 1], nmax[:, i:i + 1], scale[:, i:i + 1],
                                      ALU.mult).then_inc(bias_done, 1)

                def inverse(b, i):
                    dve.wait_ge(exp_done, UNITS * b + i + 1)
                    dve.reciprocal(inv[:, i:i + 1], total[:, i:i + 1]).then_inc(inv_done, 1)

                def pt_low_part(b, i):
                    dve.wait_ge(pt_high, UNITS * b + i + 1)
                    high = PTh[:, i // 2 % 2, :, i % 2, :].bitcast(F32)
                    dve.tensor_tensor(PTl[:, i // 2 % 2, :, i % 2, :],
                                      tps[:, i % 2, :].rearrange("p (k s) -> p k s", k=KT_TILES), high,
                                      ALU.subtract).then_inc(pt_low, 1)

                def q_low_part(b, r, early=False):
                    dve.wait_ge(stored, ROPES * b + r + 1)
                    n = (r - KT_TILES) % Q_RING
                    dve.tensor_tensor(qTl[:, n, :, :], turn_bank(r, early).rearrange("p (k s) -> p k s", k=REP),
                                      qTh[:, n, :, :].bitcast(F32), ALU.subtract).then_inc(q_low, 1)

                def k_low_part(b, k):
                    dve.wait_ge(k_high, KV_HEADS * b + k + 1)
                    dve.tensor_tensor(KTl[:, k, :], next_KT[:, k, :], KTh[:, k, :].bitcast(F32),
                                      ALU.subtract).then_inc(k_low, 1)

                def v_low_part(b, k, early=False):
                    dve.wait_ge(v_stored, KT_TILES * b + k + 1)
                    dve.tensor_tensor(Vl[:, k, :], v_bank(k, early), Vh[:, k, :].bitcast(F32),
                                      ALU.subtract).then_inc(v_low, 1)

                def add_x(b, qt):
                    dve.wait_ge(wo_done, TPB * b + qt + 1)
                    dve.scalar_tensor_tensor(out=X[:, b * TPB + qt, :], in0=wps[:, 0, 0:D],
                                             scalar=gains[:, 1:2], in1=X[:, b * TPB + qt, :],
                                             op0=ALU.mult, op1=ALU.add).then_inc(x_done, 1)

                for ready in rope_loads:
                    dve.wait_ge(*ready)
                for half in range(2):
                    rope_cos(dve, kcos, kw, sc, 0, 2 * TILES, half, k_tables_done)
                    rope_sin(dve, ksin, kw, sc, 0, 2 * TILES, half, k_tables_done)
                dve.wait_ge(k_tables_done, 4)
                for r in range(FIRST):
                    if r == 1:
                        rope_sin(dve, qsin, qw, sc, TILES, TILES, 0, q_tables_done)
                    if r == KT_TILES:
                        dve.wait_ge(q_tables_done, 4)
                    rope_first(0, r, True)
                    rope_second(0, r)
                    if r >= LAG:
                        v_low_part(0, r - LAG, True)
                q_low_part(0, KT_TILES, True)
                for k in range(FIRST - LAG, KT_TILES):
                    v_low_part(0, k, True)
                for k in range(KV_HEADS):
                    k_low_part(0, k)

                def batch(b, more):
                    for i in range(UNITS + 5):
                        j = slots(COSINES, i, more)
                        if i < UNITS:
                            maximum(b, i)
                        if 1 <= i <= UNITS:
                            inverse(b, i - 1)
                        if i < UNITS:
                            shift(b, i)
                        if j is not None:
                            rope_first(*rope_unit(b, j))
                        if 3 <= i < UNITS + 3:
                            pt_low_part(b, i - 3)
                        j = slots(LOW, i, more)
                        if j is not None:
                            q_low_part(*rope_unit(b, j))
                        j = slots(SINES, i, more)
                        if j is not None:
                            rope_second(*rope_unit(b, j))
                        if i == HEADS + 7:
                            add_x(b, 0)
                        if more and i - 1 in KEYS_AT:
                            k_low_part(b + 1, KEYS_AT[i - 1])
                        if i == 1 and not (isinstance(b, int) and b == 0):
                            v_low_part(b, KT_TILES - 1)
                    if more:
                        for k in range(KT_TILES - 1):
                            v_low_part(b + 1, k)
                    add_x(b, 1)

                batches(dve, batch)

            @block.tensor
            def _(pe):
                def project(b, r, early=False):
                    if early:
                        wait_for(pe, raw_done, max(r - 2, 0))
                    else:
                        pe.wait_ge(raw_done, ROPES * b + r)
                        if r == FIRST:
                            pe.wait_ge(v_low, KT_TILES * b + (KT_TILES if isinstance(b, int) and b == 0 else 1))
                    if r == 0 and not early:
                        pe.wait_ge(ctx_in, 16 * b + 16)
                    if r == TPB:
                        pe.wait_ge(ln_copied, b + 1)
                    for c in range(DC):
                        if r < KT_TILES:
                            tok, w = r, wk[:, c, :]
                        else:
                            qt, n = divmod(r - KT_TILES, KV_HEADS)
                            tok, w = TPB + qt, wq[:, c, n * 512:(n + 1) * 512]
                        last = pe.matmul(proj_bank(r, early), kvT[:, c, tok * P:(tok + 1) * P], w,
                                         start=(c == 0), stop=(c == DC - 1))
                    last.then_inc(proj_done, 1)

                def project_v(b, k, early=False):
                    if early:
                        wait_for(pe, v_low, max(k - 1, 0))
                        if k == 2:
                            pe.wait_ge(ln_copied, 1)
                    elif k < 2:
                        if k == 0:
                            pe.wait_ge(raw_done, ROPES * b + FIRST)
                        else:
                            pe.wait_ge(q_low, QUERIES * b + 1)
                    elif k == 2:
                        pe.wait_ge(at_stored, PAIRS * b)
                    else:
                        pe.wait_ge(x_done, TPB * b)
                    for c in range(DC):
                        last = pe.matmul(v_bank(k, early), kvT[:, c, k * P:(k + 1) * P], wv[:, c, :],
                                         start=(c == 0), stop=(c == DC - 1))
                    last.then_inc(v_done, 1)

                def turn(b, r, early=False):
                    if r < KT_TILES:
                        pe.wait_ge(scaled, KT_TILES * b + r + 1)
                    else:
                        pe.wait_ge(roped, ROPES * b + r + 1)
                    if early:
                        wait_for(pe, stored, max(r - 1, 0))
                    else:
                        if 0 < r <= KT_TILES:
                            pe.wait_ge(stored, ROPES * b + r)
                        else:
                            pe.wait_ge(q_low, QUERIES * b + max(r - KT_TILES, 0))
                        if r == FIRST:
                            pe.wait_ge(v_low, KT_TILES * b + (KT_TILES if isinstance(b, int) and b == 0 else 2))
                    for k in range(REP):
                        last = pe.transpose(turn_bank(r, early)[:, k * P:(k + 1) * P],
                                            y[:, r % 2, k * HD:(k + 1) * HD], ident)
                    last.then_inc(turned, 1)

                def scores(b, i):
                    kv = i % HEADS // REP
                    if i % REP == 0:
                        pe.wait_ge(q_low, QUERIES * b + i // REP + 1)
                        if i < HEADS:
                            pe.wait_ge(k_low, KV_HEADS * b + kv + 1)
                    wait_for(pe, exp_done, UNITS * b + max(i - 1, 0))
                    n = i // REP % Q_RING
                    for j, (q, k) in enumerate(((qTh, KTh), (qTh, KTl), (qTl, KTh))):
                        last = pe.matmul(sps[:, i % 2, :], q[:, n, i % REP, :], k[:, kv, :], start=(j == 0),
                                         stop=(j == 2))
                    last.then_inc(s_done, 1)

                def turn_probs(b, i):
                    pe.wait_ge(normed, UNITS * b + i + 1)
                    wait_for(pe, pt_low, UNITS * b + max(i - 1, 0))
                    for k in range(KT_TILES):
                        last = pe.transpose(tps[:, i % 2, k * P:(k + 1) * P],
                                            probs[:, i % 3, k * P:(k + 1) * P], ident)
                    last.then_inc(pt_turned, 1)

                def values(b, pair, half):
                    if half == 0:
                        pe.wait_ge(pt_low, UNITS * b + 2 * pair + 2)
                        if pair == 0:
                            pe.wait_ge(v_low, KT_TILES * b + KT_TILES)
                        wait_for(pe, at_stored, PAIRS * b + pair)
                    kv = 2 * pair % HEADS // REP
                    for k in range(2 * half, 2 * half + 2):
                        for n, (v, pt) in enumerate(((Vh, PTh), (Vh, PTl), (Vl, PTh))):
                            last = pe.matmul(ops[:, 0, 0:2 * P], v[:, k, kv * HD:(kv + 1) * HD],
                                             pt[:, pair % 2, k, :, :].rearrange("p h s -> p (h s)"),
                                             start=(k == 0 and n == 0), stop=(k == KT_TILES - 1 and n == 2))
                    if half == 1:
                        last.then_inc(pv_done, 1)

                def output(b, n):
                    qt, h = divmod(n, HEADS)
                    if h % 2 == 0:
                        pe.wait_ge(at_stored, PAIRS * b + n // 2 + 1)
                    if h == 0:
                        wait_for(pe, x_done, TPB * b + qt)
                    last = pe.matmul(wps[:, 0, 0:D], attnT[:, h % 4, :], wo[:, h, :], start=(h == 0),
                                     stop=(h == HEADS - 1))
                    if h == HEADS - 1:
                        last.then_inc(wo_done, 1)

                for ready in loads:
                    pe.wait_ge(*ready)
                pe.wait_ge(ctx_in, 16)
                for r in range(FIRST + 2):
                    if r < FIRST:
                        project(0, r, True)
                    if LAG <= r < KT_TILES + LAG:
                        project_v(0, r - LAG, True)
                    if r >= 2:
                        turn(0, r - 2, True)

                scores(0, 0)
                scores(0, 1)

                def batch(b, more):
                    for i in range(UNITS + 8):
                        if 2 <= i < UNITS:
                            scores(b, i)
                        if more and UNITS + 5 <= i < UNITS + 7:
                            scores(b + 1, i - UNITS - 5)
                        j = slots(START, i, more)
                        if j is not None:
                            project(*rope_unit(b, j))
                        if 5 <= i < UNITS + 5:
                            values(b, (i - 5) // 2, (i - 5) % 2)
                        if 2 <= i < UNITS + 2:
                            turn_probs(b, i - 2)
                        if i >= 8:
                            output(b, i - 8)
                        j = slots(TURN, i, more)
                        if j is not None:
                            turn(*rope_unit(b, j))
                        if more and i in V_START:
                            project_v(b + 1, V_START[i])
                        if i == 1 and not (isinstance(b, int) and b == 0):
                            project_v(b, KT_TILES - 1)

                batches(pe, batch)


def route(nc, lps, logits_done, ln, slot, expert, sorted_x, const, zeroed):
    with ExitStack() as st:
        m = Memory(nc, st)
        logits = m.sb("e_logits", [P, TILES, EXPERTS])
        best = m.sb("e_best", [P, TILES])
        first = m.sb("e_first", [P, TILES])
        cand = m.sb("e_cand", [P, TILES, EXPERTS])
        hot = m.sb("e_hot", [P, TILES, EXPERTS])
        count = m.sb("e_count", [P, TILES, EXPERTS])
        before = m.sb("e_before", [P, TILES + 1, EXPERTS])
        tiles = m.sb("e_tiles", [P, EXPERTS])
        ends = m.sb("e_ends", [P, EXPERTS])
        base = m.sb("e_base", [P, EXPERTS])
        where = m.sb("e_where", [P, TILES, EXPERTS])
        slotf = m.sb("e_slotf", [P, TILES])
        over = m.sb("e_over", [1, SLOT_TILES, EXPERTS])
        expf = m.sb("e_expf", [1, SLOT_TILES])
        rps = m.ps("e_rps", 1)
        cps = m.ps("e_cps", 1)
        step = m.sem("e_step")
        hot_done = m.sem("e_hot_done")
        ranked = m.sem("e_ranked")
        slots_done = m.sem("e_slots_done")
        scattered = m.sem("e_scattered")
        ids = const[:, C_EXP:C_EXP + EXPERTS]
        all_tiles = [P, TILES, EXPERTS]
        with nc.Block() as block:
            @block.tensor
            def _(pe):
                pe.wait_ge(hot_done, 1)
                hot2 = hot[:, :, :].rearrange("p t e -> p (t e)")
                pe.matmul(rps[:, 0, 0:TILES * EXPERTS], const[:, C_TRI:C_TRI + P], hot2, start=True, stop=True)
                pe.matmul(cps[:, 0, 0:TILES * EXPERTS], const[:, C_ONES:C_ONES + P], hot2, start=True,
                          stop=True).then_inc(ranked, 1)

            @block.vector
            def _(dve):
                n = 0

                def after(ins):
                    nonlocal n
                    ins.then_inc(step, 1)
                    n += 1
                    dve.wait_ge(step, n)

                dve.wait_ge(logits_done, 1)
                after(dve.tensor_copy(logits[:, :, :].rearrange("p t e -> p (t e)"),
                                      lps[:, 0, 0:TILES * EXPERTS]))
                after(dve.tensor_reduce(best[:, :], logits[:, :, :], AX.X, ALU.max))
                after(dve.tensor_tensor(cand[:, :, :], logits[:, :, :], best[:, :].unsqueeze(2).to_broadcast(all_tiles),
                                        ALU.is_equal))
                after(dve.tensor_scalar(base[:, :], ids, float(-EXPERTS), None, ALU.add))
                after(dve.tensor_tensor(cand[:, :, :], cand[:, :, :], base[:, :].unsqueeze(1).to_broadcast(all_tiles),
                                        ALU.mult))
                after(dve.tensor_reduce(first[:, :], cand[:, :, :], AX.X, ALU.min))
                dve.tensor_tensor(hot[:, :, :], first[:, :].unsqueeze(2).to_broadcast(all_tiles),
                                  base[:, :].unsqueeze(1).to_broadcast(all_tiles),
                                  ALU.is_equal).then_inc(hot_done, 1)
                dve.wait_ge(ranked, 1)
                after(dve.tensor_copy(count[:, :, :].rearrange("p t e -> p (t e)"),
                                      cps[:, 0, 0:TILES * EXPERTS]))
                after(dve.memset(before[:, 0, :], 0.0))
                for t in range(TILES):
                    after(dve.tensor_tensor(before[:, t + 1, :], before[:, t, :], count[:, t, :], ALU.add))
                after(dve.tensor_scalar(tiles[:, :], before[:, TILES, :], 1.0 / P, 0.5 - 1.0 / (2 * P), ALU.mult,
                                        ALU.add))
                after(dve.tensor_scalar(tiles[:, :], tiles[:, :], ROUND, None, ALU.add))
                after(dve.tensor_scalar(tiles[:, :], tiles[:, :], ROUND, None, ALU.subtract))
                after(dve.tensor_tensor_scan(ends[:, :], const[:, C_ONES:C_ONES + EXPERTS], tiles[:, :], 0.0,
                                             ALU.mult, ALU.add))
                after(dve.tensor_tensor(base[:, :], ends[:, :], tiles[:, :], ALU.subtract))
                after(dve.tensor_scalar(base[:, :], base[:, :], float(P), None, ALU.mult))
                after(dve.tensor_tensor(where[:, :, :].rearrange("p t e -> p (t e)"), rps[:, 0, 0:TILES * EXPERTS],
                                        before[:, 0:TILES, :].rearrange("p t e -> p (t e)"), ALU.add))
                after(dve.tensor_tensor(where[:, :, :], where[:, :, :], base[:, :].unsqueeze(1).to_broadcast(all_tiles),
                                        ALU.add))
                after(dve.tensor_tensor(where[:, :, :], where[:, :, :], hot[:, :, :], ALU.mult))
                after(dve.tensor_reduce(slotf[:, :], where[:, :, :], AX.X, ALU.add))
                dve.tensor_copy(slot[:, :], slotf[:, :]).then_inc(slots_done, 1)
                shape = [1, SLOT_TILES, EXPERTS]
                after(dve.tensor_tensor(over[:, :, :], ends[0:1, :].unsqueeze(1).to_broadcast(shape),
                                        const[0:1, C_TILE:C_TILE + SLOT_TILES].unsqueeze(2).to_broadcast(shape),
                                        ALU.is_le))
                after(dve.tensor_reduce(expf[:, :], over[:, :, :], AX.X, ALU.add))
                after(dve.tensor_scalar(expert[:, :], expf[:, :], float(EXPERTS - 1), None, ALU.min))

            @block.gpsimd
            def _(pool):
                pool.wait_ge(slots_done, 1)
                pool.wait_ge(*zeroed)
                for t in range(TILES):
                    pool.indirect_dma_start(sorted_x, bass.IndirectOffsetOnAxis(slot[:, t:t + 1], 0),
                                            ln[:, t, :], None).then_inc(scattered, 16)
                pool.wait_ge(scattered, 16 * TILES)


def experts(nc, X, gate, up, down, expert, slot, sorted_x, sorted_y, gains, ident, out, loads,
            down_ready):
    LAST = SLOT_TILES - 1
    assert LAST % 2 == 0
    with ExitStack() as st:
        m = Memory(nc, st)
        xs = m.sb("g_xs", [P, 2, D])
        xT = m.sb("g_xT", [P, 2, DC, P])
        act_g = m.sb("g_act", [P, 2, INNER])
        h = m.sb("g_h", [P, 2, INNER])
        hT = m.sb("g_hT", [P, 2, IC, P])
        ys = m.sb("g_ys", [P, 2, D])
        yg = m.sb("g_yg", [P, TILES, D])
        xps = m.ps("g_xps", 1)
        gps = m.ps("g_gps", 2)
        ups = m.ps("g_ups", 2)
        hps = m.ps("g_hps", 1)
        yps = m.ps("g_yps", 2)
        xs_in = [m.sem(f"g_xs_in{k}") for k in range(2)]
        x_turned = m.sem("g_x_turned")
        x_stored = m.sem("g_x_stored")
        g_done = m.sem("g_g_done")
        u_done = m.sem("g_u_done")
        silu_done = m.sem("g_silu_done")
        h_done = m.sem("g_h_done")
        h_turned = m.sem("g_h_turned")
        h_stored = m.sem("g_h_stored")
        y_done = m.sem("g_y_done")
        y_copied = m.sem("g_y_copied")
        y_out = [m.sem(f"g_y_out{k}") for k in range(2)]
        gathered = [m.sem(f"g_gathered{k}") for k in range(TILES)]
        x_done = m.sem("g_x_done")
        stored = m.sem("g_stored")
        with nc.Block() as block:
            @block.sync
            def _(sp):
                def load(i, par, rnd):
                    if rnd is not None:
                        wait_for(sp, x_turned, i - 1)
                    sp.dma_start(xs[:, par, :], sorted_x[bass.ds(i * P, P), :]).then_inc(xs_in[par], 16)

                def store(i, par):
                    sp.wait_ge(y_copied, i + 1)
                    sp.dma_start(sorted_y[bass.ds(i * P, P), :], ys[:, par, :]).then_inc(y_out[par], 16)

                load(0, 0, None)
                load(1, 1, None)
                for j in range(LAST // 2 - 1):
                    for par in range(2):
                        load(2 * j + par + 2, par, j)
                        store(2 * j + par, par)
                load(LAST, 0, 0)
                store(LAST - 2, 0)
                store(LAST - 1, 1)
                store(LAST, 0)
                for par in range(2):
                    sp.wait_ge(y_out[par], 16 * ((SLOT_TILES + 1 - par) // 2))
                sp.sem_inc(y_copied, 1)
                for t in range(TILES):
                    sp.wait_ge(x_done, t + 1)
                    sp.dma_start(out[t * P:(t + 1) * P, :], X[:, t, :]).then_inc(stored, 16)
                sp.wait_ge(stored, 16 * TILES)

            @block.tensor
            def _(pe):
                for ready in loads:
                    pe.wait_ge(*ready)

                def turn_x(i, par, rnd):
                    pe.wait_ge(xs_in[par], 16 * rnd + 16)
                    wait_for(pe, x_stored, i)
                    for c in range(DC):
                        last = pe.transpose(xps[:, 0, c * P:(c + 1) * P], xs[:, par, c * P:(c + 1) * P], ident)
                    last.then_inc(x_turned, 1)

                def expert_of(i):
                    return pe.value_load(expert[0:1, bass.ds(i, 1)], min_val=0, max_val=EXPERTS - 1)

                def project(e, par, w, banks, done):
                    for c in range(DC):
                        last = pe.matmul(banks[:, par, :], xT[:, par, c, :], w[:, c, bass.ds(e * INNER, INNER)],
                                         start=(c == 0), stop=(c == DC - 1))
                    last.then_inc(done, 1)

                def turn_h(i, par):
                    pe.wait_ge(h_done, i + 1)
                    wait_for(pe, h_stored, i)
                    for c in range(IC):
                        last = pe.transpose(hps[:, 0, c * P:(c + 1) * P], h[:, par, c * P:(c + 1) * P], ident)
                    last.then_inc(h_turned, 1)

                def down_proj(e, i, par):
                    pe.wait_ge(h_stored, i + 1)
                    wait_for(pe, y_copied, i)
                    for c in range(IC):
                        last = pe.matmul(yps[:, par, 0:D], hT[:, par, c, :], down[:, c, bass.ds(e * D, D)],
                                         start=(c == 0), stop=(c == IC - 1))
                    last.then_inc(y_done, 1)

                def ahead(i, par, rnd, turn_next):
                    e, e_next = expert_of(i), expert_of(i + 1)
                    pe.wait_ge(x_stored, i + 2)
                    project(e_next, 1 - par, gate, gps, g_done)
                    turn_h(i, par)
                    project(e_next, 1 - par, up, ups, u_done)
                    if turn_next:
                        turn_x(i + 2, par, rnd + 1)
                    down_proj(e, i, par)

                turn_x(0, 0, 0)
                turn_x(1, 1, 0)
                pe.wait_ge(x_stored, 1)
                e = expert_of(0)
                project(e, 0, gate, gps, g_done)
                project(e, 0, up, ups, u_done)
                pe.wait_ge(*down_ready)

                def pair(j):
                    for par in range(2):
                        ahead(2 * j + par, par, j, True)

                first_then_loop(pe, LAST // 2 - 1, pair)
                ahead(LAST - 2, 0, LAST // 2 - 1, True)
                ahead(LAST - 1, 1, LAST // 2 - 1, False)
                turn_h(LAST, 0)
                down_proj(expert_of(LAST), LAST, 0)

            @block.scalar
            def _(act):
                def copy_x(i, par):
                    act.wait_ge(x_turned, i + 1)
                    act.activation(xT[:, par, :, :], xps[:, 0, 0:D].rearrange("p (c s) -> p c s", c=DC),
                                   ACT.Copy).then_inc(x_stored, 1)

                def silu(i, par):
                    if not (isinstance(i, int) and i < 2):
                        act.wait_ge(h_done, i - 1)
                    act.wait_ge(g_done, i + 1)
                    act.activation(act_g[:, par, :], gps[:, par, :], ACT.Silu).then_inc(silu_done, 1)

                copy_x(0, 0)
                copy_x(1, 1)
                silu(0, 0)
                silu(1, 1)

                def pair(j):
                    for par in range(2):
                        copy_x(2 * j + par + 2, par)
                        silu(2 * j + par + 2, par)

                first_then_loop(act, LAST // 2 - 1, pair)
                copy_x(LAST, 0)
                silu(LAST, 0)

            @block.vector
            def _(dve):
                def copy_h(i, par):
                    dve.wait_ge(h_turned, i + 1)
                    dve.tensor_copy(hT[:, par, :, :].rearrange("p c s -> p (c s)"), hps[:, 0, :]).then_inc(h_stored, 1)

                def copy_y(i, par):
                    dve.wait_ge(y_done, i + 1)
                    dve.tensor_copy(ys[:, par, :], yps[:, par, 0:D]).then_inc(y_copied, 1)

                def product(i, par):
                    dve.wait_ge(silu_done, i + 1)
                    dve.wait_ge(u_done, i + 1)
                    dve.tensor_tensor(h[:, par, :], act_g[:, par, :], ups[:, par, :], ALU.mult).then_inc(h_done, 1)

                product(0, 0)
                for i in range(2):
                    copy_h(i, i)
                    product(i + 1, 1 - i)
                    copy_y(i, i)
                with dve.Fori(1, LAST // 2) as j:
                    for par in range(2):
                        copy_h(2 * j + par, par)
                        product(2 * j + par + 1, 1 - par)
                        dve.wait_ge(y_out[par], 16 * j)
                        copy_y(2 * j + par, par)
                copy_h(LAST, 0)
                dve.wait_ge(y_out[0], 16 * (LAST // 2))
                copy_y(LAST, 0)
                for t in range(TILES):
                    dve.wait_ge(gathered[t], 16)
                    dve.scalar_tensor_tensor(out=X[:, t, :], in0=yg[:, t, :], scalar=gains[:, 3:4], in1=X[:, t, :],
                                             op0=ALU.mult, op1=ALU.add).then_inc(x_done, 1)

            @block.gpsimd
            def _(pool):
                pool.wait_ge(y_copied, SLOT_TILES + 1)
                for t in range(TILES):
                    pool.indirect_dma_start(yg[:, t, :], None, sorted_y,
                                            bass.IndirectOffsetOnAxis(slot[:, t:t + 1], 0)).then_inc(gathered[t], 16)


def flamingo(nc, t, out):
    with ExitStack() as stack:
        mem = Memory(nc, stack)
        X = mem.sb("X", [P, TILES, D])
        const = mem.sb("const", [P, C_WIDE])
        gains = mem.sb("gains", [P, 4])
        ident = const[:, C_IDENT:C_IDENT + P]
        x_in = mem.sem("x_in")
        const_in = mem.sem("const_in")
        gains_in = mem.sem("gains_in")
        sorted_x = nc.dram_tensor("sorted_x", (SLOTS, D), F32, kind="Internal").ap()
        sorted_y = nc.dram_tensor("sorted_y", (SLOTS, D), F32, kind="Internal").ap()

        shared = mem.sb("shared", [P, DC * EXPERTS * INNER])
        lnT = shared[:, 0:DC * TOK].rearrange("p (c s) -> p c s", c=DC)
        ctxT = shared[:, DC * TOK:2 * DC * TOK].rearrange("p (c s) -> p c s", c=DC)
        ctx = shared[:, 2 * DC * TOK:3 * DC * TOK].rearrange("p (t d) -> p t d", t=TILES)
        w1 = shared[:, 3 * DC * TOK:3 * DC * TOK + DC * FF].rearrange("p (c f) -> p c f", c=DC)
        gate = shared[:, :].rearrange("p (c n) -> p c n", c=DC)
        gate_in = mem.sem("expert_gate_in")
        zeroed = mem.sem("zeroed")

        aw = stack.enter_context(ExitStack())
        wq = Memory(nc, aw).sb("wq", [P, DC, HEADS * HD])
        wk = Memory(nc, aw).sb("wk", [P, DC, KV_HEADS * HD])
        wv = Memory(nc, aw).sb("wv", [P, DC, KV_HEADS * HD])
        wo = Memory(nc, aw).sb("wo", [P, HEADS, D])
        attn_w_in = mem.sem("attn_w_in")
        pos = Memory(nc, aw).sb("pos", [P, 2 * TILES], I32)
        kw = Memory(nc, aw).sb("kw", [P, HD])
        qw = Memory(nc, aw).sb("qw", [P, HD])
        sc = Memory(nc, aw).sb("sc", [P, 2, 2 * TILES, ROT])
        pos_in = mem.sem("pos_in")
        norm_w_in = mem.sem("norm_w_in")
        lnT2 = Memory(nc, aw).sb("lnT2", [P, DC, TOK])
        fw = stack.enter_context(ExitStack())
        w2 = Memory(nc, fw).sb("w2", [P, FC, D])
        w1_in = mem.sem("w1_in")
        w2_in = mem.sem("w2_in")

        with ExitStack() as lstm:
            m = Memory(nc, lstm)
            gate_w = m.sb("gate_w", [P, 3 * DC, 32])
            gate_b = m.sb("gate_b", [P, 1])
            selr = m.sb("selr", [32, M_HEADS * P], F32R)
            scale_row = m.sb("scale_row", [P, D])
            cols = m.sb("cols", [P, B, 4, 32])
            Gr = m.sb("Gr", [32, TOK], F32R)
            Mr = m.sb("Mr", [32, TOK], F32R)
            rows = lstm.enter_context(ExitStack())
            sel = Memory(nc, rows).sb("sel", [32, M_HEADS * P])
            ctx_in = m.sem("ctx_in")
            ctxT_in = m.sem("ctxT_in")
            gate_in = m.sem("gate_in")
            bias_in = m.sem("bias_in")
            sel_in = m.sem("sel_in")
            scale_in = m.sem("scale_in")
            tanh_done = m.sem("tanh_done")
            with nc.Block() as block:
                @block.sync
                def _(sp):
                    sp.dma_start(X[:, :, :], t["x"].rearrange("(t p) d -> p t d", p=P)).then_inc(x_in, 16)
                    sp.dma_start(const[:, :], t["const"]).then_inc(const_in, 16)
                    sp.dma_start(ctxT[:, :, :], t["ctxT"].rearrange("(c p) s -> p c s", p=P)).then_inc(ctxT_in, 16)
                    sp.dma_start(gate_w[:, :, :], t["gate_w"].rearrange("(c p) n -> p c n", p=P)).then_inc(gate_in, 16)
                    sp.dma_start(gate_b[:, :], t["gate_b"]).then_inc(bias_in, 16)
                    sp.dma_start(sel[:, :], t["sel"]).then_inc(sel_in, 16)
                    sp.dma_start(ctx[:, :, :], t["ctx"].rearrange("(t p) d -> p t d", p=P)).then_inc(ctx_in, 16)
                    sp.dma_start(w1[:, :, :], t["w1T"].rearrange("(c p) f -> p c f", p=P)).then_inc(w1_in, 16)
                    sp.dma_start(w2[:, :, :], t["w2T"].rearrange("(c p) d -> p c d", p=P)).then_inc(w2_in, 16)
                    sp.dma_start(wk[:, :, :], t["wkT"].rearrange("(c p) n -> p c n", p=P)).then_inc(attn_w_in, 16)
                    sp.dma_start(wv[:, :, :], t["wvT"].rearrange("(c p) n -> p c n", p=P)).then_inc(attn_w_in, 16)
                    sp.dma_start(wq[:, :, :], t["wqT"].rearrange("(c p) n -> p c n", p=P)).then_inc(attn_w_in, 16)
                    sp.dma_start(wo[:, :, :], t["woT"].rearrange("(h p) n -> p h n", p=P)).then_inc(attn_w_in, 16)

                @block.scalar
                def _(act):
                    act.dma_start(gains[:, :], t["gains"].partition_broadcast(P)).then_inc(gains_in, 16)
                    act.dma_start(scale_row[:, :], t["ln_scale"].partition_broadcast(P)).then_inc(scale_in, 16)
                    act.dma_start(pos[:, :], t["pos"]).then_inc(pos_in, 16)
                    act.dma_start(kw[:, :], t["k_norm"].partition_broadcast(P)).then_inc(norm_w_in, 16)
                    act.dma_start(qw[:, :], t["q_norm"].partition_broadcast(P)).then_inc(norm_w_in, 16)
                    act.wait_ge(gains_in, 16)
                    act.activation(gains[:, :], gains[:, :], ACT.Tanh).then_inc(tanh_done, 1)

                @block.vector
                def _(dve):
                    dve.wait_ge(scale_in, 16)
                    dve.wait_ge(tanh_done, 1)
                    dve.tensor_scalar(scale_row[:, :], scale_row[:, :], gains[:, 0:1], None, ALU.mult)
            gates_done = m.sem("gates_done")
            zps = Memory(nc, rows).ps("a_zps", 1)

            def gates(pe, b, c):
                src = lnT if c < DC else ctxT
                return pe.matmul(zps[32 * b:32 * b + 32, 0, 0:S_LEN], gate_w[:, c, :],
                                 src[:, c % DC, b * S_LEN:(b + 1) * S_LEN], start=(c == DC), stop=(c == DC - 1))

            def gates_of_ctx(pe):
                pe.wait_ge(ctxT_in, 16)
                pe.wait_ge(gate_in, 16)
                for b in range(B):
                    for c in range(DC, 3 * DC):
                        gates(pe, b, c)

            def gates_of_x(pe, n):
                if n % TPB == TPB - 1:
                    for c in range(DC):
                        last = gates(pe, n // TPB, c)
                    if n == TILES - 1:
                        last.then_inc(gates_done, 1)

            layernorm_transposed(nc, "l0", X, lnT, ident, const, (const_in, 16), (x_in, 16), follow=gates_of_x,
                                 first=gates_of_ctx)
            mlstm_rows(nc, zps, gates_done, gate_b, sel, const, cols, Gr, Mr, selr, ident,
                       [(bias_in, 16), (sel_in, 16), (ctx_in, 16), (const_in, 16)])
            rows.close()
            mlstm_and_ffn(nc, X, lnT, ctx, ctxT, cols, Gr, Mr, selr, scale_row, const, ident, w1, w2, gains,
                          lnT2, [(w1_in, 16), (w2_in, 16)], pos, (pos_in, 16), sc)
        fw.close()

        with ExitStack() as attn:
            m = Memory(nc, attn)
            kcos = m.sb("kcos", [P, 2 * TILES, HD])
            ksin = m.sb("ksin", [P, 2 * TILES, HD])
            qcos = m.sb("qcos", [P, TILES, HD])
            qsin = m.sb("qsin", [P, TILES, HD])

            def load_gate(sp):
                for e in range(EXPERTS):
                    sp.dma_start(gate[:, :, e * INNER:(e + 1) * INNER],
                                 t["gate"][e].rearrange("(c p) i -> p c i", p=P)).then_inc(gate_in, 16)
                sp.dma_start(sorted_x.rearrange("(t p) d -> t p d", p=P),
                             t["zero"].unsqueeze(0).to_broadcast([SLOT_TILES, P, D])).then_inc(zeroed, 16)

            gqa_attention(nc, t, X, lnT2, wq, wk, wv, wo, kcos, ksin, qcos, qsin, gains, const, ident,
                          [(attn_w_in, 64)], sc, kw, qw,
                          [(norm_w_in, 32)], load_gate)

        aw.close()
        with ExitStack() as moe:
            m = Memory(nc, moe)
            up = m.sb("up", [P, DC, EXPERTS * INNER])
            down = m.sb("down", [P, IC, EXPERTS * D])
            router = m.sb("router", [P, DC, EXPERTS])
            lnT = m.sb("lnT3", [P, DC, TOK])
            ln = m.sb("ln3", [P, TILES, D])
            slot = m.sb("slot", [P, TILES], U32)
            expert = m.sb("expert", [1, SLOT_TILES], I32)
            router_in = m.sem("router_in")
            up_in = m.sem("up_in")
            down_in = m.sem("down_in")
            logits_done = m.sem("logits_done")
            logits_bank = moe.enter_context(ExitStack())
            lps = Memory(nc, logits_bank).ps("e_lps", 1)

            def load_experts(sp):
                sp.dma_start(router[:, :, :], t["router"].rearrange("(c p) e -> p c e", p=P)
                             ).then_inc(router_in, 16)
                for e in range(EXPERTS):
                    sp.dma_start(up[:, :, e * INNER:(e + 1) * INNER], t["up"][e].rearrange("(c p) i -> p c i", p=P)
                                 ).then_inc(up_in, 16)
                for e in range(EXPERTS):
                    sp.dma_start(down[:, :, e * D:(e + 1) * D], t["down"][e].rearrange("(c p) d -> p c d", p=P)
                                 ).then_inc(down_in, 16)

            def route_logits(pe, n):
                if n == 0:
                    pe.wait_ge(router_in, 16)
                for c in range(DC):
                    last = pe.matmul(lps[:, 0, n * EXPERTS:(n + 1) * EXPERTS], lnT[:, c, n * P:(n + 1) * P],
                                     router[:, c, :], start=(c == 0), stop=(c == DC - 1))
                if n == TILES - 1:
                    last.then_inc(logits_done, 1)

            layernorm_transposed(nc, "l3", X, lnT, ident, const, kept=ln, meanwhile=load_experts,
                                 follow=route_logits)
            route(nc, lps, logits_done, ln, slot, expert, sorted_x, const, (zeroed, 16))
            logits_bank.close()
            experts(nc, X, gate, up, down, expert, slot, sorted_x, sorted_y, gains, ident, out,
                    [(gate_in, 16 * EXPERTS), (up_in, 16 * EXPERTS)], (down_in, 16 * EXPERTS))


def kernel(**inputs):
    import numpy as _np
    import concourse.bacc as _bacc
    from concourse import mybir as _mybir
    from concourse.bass_utils import run_bass_kernel_spmd as _run

    i = {k: _np.asarray(v) for k, v in inputs.items()}
    const, sel = host_constants()
    laid = {
        "x": i["x"].reshape(TOK, D),
        "ctx": i["ctx_2048"].reshape(TOK, D),
        "ctxT": i["ctx_2048"].reshape(TOK, D).T,
        "const": const,
        "zero": _np.zeros((P, D), _np.float32),
        "sel": sel,
        "gains": _np.concatenate([i["g_xattn"], i["g_ffn"]]),
        "gate_w": _np.concatenate([i["L0_xattn_Wi"], i["L0_xattn_Wf"]], axis=1),
        "gate_b": _np.tile(_np.concatenate([i["L0_xattn_bi"], i["L0_xattn_bf"]]), B)[:, None],
        "pos": _np.concatenate([i["pos_BxS2"].reshape(TILES, P), i["itok_BxS_4096_4607"].reshape(TILES, P)]).T,
        "k_norm": i["L1_xattn_k_norm_w"],
        "q_norm": i["L1_xattn_q_norm_w"],
        "wqT": i["L1_xattn_Wq"].T,
        "wkT": i["L1_xattn_Wk"].T,
        "wvT": i["L1_xattn_Wv"].T,
        "woT": i["L1_xattn_Wo"].T,
        "router": i["L1_ffn_router_w"],
        "gate": i["L1_ffn_gate_w"],
        "up": i["L1_ffn_up_w"],
        "down": i["L1_ffn_down_w"],
        "w1T": i["L0_ffn_W1"].T,
        "w2T": i["L0_ffn_W2"].T,
        "ln_scale": i["L0_xattn_ln_scale"],
    }
    nc = _bacc.Bacc("TRN2", target_bir_lowering=False, num_devices=1)
    arrays, args = {}, {}
    for name, a in laid.items():
        a = _np.ascontiguousarray(a)
        arrays[f"in_{name}"] = a
        args[name] = nc.dram_tensor(f"in_{name}", a.shape, _mybir.dt.from_np(a.dtype), kind="ExternalInput").ap()
    out = nc.dram_tensor("out", (TOK, D), F32, kind="ExternalOutput").ap()
    flamingo(nc, args, out)
    r = _run(nc, [arrays], core_ids=[0])
    return r.results[0]["out"].reshape(B, S_LEN, D)
```
